# Optimizing a Trainium2 kernel written in Bass

```python
import numpy as np
import jax
import jax.numpy as jnp

def _softmax(x, axis=-1):
    return jax.nn.softmax(x, axis=axis)

def _gelu(x):
    return jax.nn.gelu(x, approximate=True)

def _silu(x):
    return jax.nn.silu(x)

def _sigmoid(x):
    return jax.nn.sigmoid(x)

def _layernorm(x, axis=-1, eps=1e-05):
    m = jnp.mean(x, axis=axis, keepdims=True)
    v = jnp.var(x, axis=axis, keepdims=True)
    return (x - m) / jnp.sqrt(v + eps)

def _scatter_add(tgt, idx, src, axis=0):
    return tgt.at[idx].add(src)

def _segment_sum(src, seg, n):
    return jax.ops.segment_sum(src, seg, n)
kernel_name = 'mk_gnn_preln_d2_gnn_r8_ba5161'

def setup_inputs(seed: int=0):
    np.random.seed(seed)
    _w = jnp.asarray

    def _rec_inputs():
        import jax
        import jax.numpy as jnp
        _gk = jax.random.key(seed)
        x = -0.000202 + 1 * jax.random.normal(jax.random.fold_in(_gk, 1), (6250, 128), jnp.float32)
        _s = jax.random.randint(jax.random.fold_in(_gk, 2), (100000,), 0, 6250, jnp.int32)
        _d = jax.random.randint(jax.random.fold_in(_gk, 3), (100000,), 0, 6250, jnp.int32)
        _loop = jnp.arange(6250, dtype=jnp.int32)
        src = jnp.concatenate([_s, _d, _loop])
        dst = jnp.concatenate([_d, _s, _loop])
        _o = jnp.argsort(dst, stable=True)
        src = src[_o]
        dst = dst[_o]
        edge_type_9 = jax.random.randint(jax.random.fold_in(_gk, 13), (206250,), 0, 9, jnp.int32)
        edge_weight = jax.random.uniform(jax.random.fold_in(_gk, 14), (206250,), jnp.float32, 0.0, 0.999999)
        return (x, src, dst, edge_type_9, edge_weight)
    x, src, dst, edge_type_9, edge_weight = _rec_inputs()

    def _L0_gnn_setup():
        import jax, jax.numpy as jnp
        import numpy as np
        NUM_EDGE_TYPES = 8
        HIDDEN = 128
        N_NODES = 6250
        N_EDGES = 75000

        def _gru_cell(x, h, W_ih, W_hh, b_ih, b_hh):
            H = h.shape[-1]
            gi = x @ W_ih.T + b_ih
            gh = h @ W_hh.T + b_hh
            i_r, i_z, i_n = (gi[:, :H], gi[:, H:2 * H], gi[:, 2 * H:])
            h_r, h_z, h_n = (gh[:, :H], gh[:, H:2 * H], gh[:, 2 * H:])
            r = jax.nn.sigmoid(i_r + h_r)
            z = jax.nn.sigmoid(i_z + h_z)
            n = jnp.tanh(i_n + r * h_n)
            return (1.0 - z) * n + z * h
        key = jax.random.key(seed)
        ks = jax.random.split(key, 10)
        H = HIDDEN
        h = jax.random.normal(ks[0], (N_NODES, H), dtype=jnp.float32)
        edge_index = jax.random.randint(ks[1], (2, N_EDGES), 0, N_NODES, dtype=jnp.int32)
        edge_type = jax.random.randint(ks[2], (N_EDGES,), 0, NUM_EDGE_TYPES + 1, dtype=jnp.int32)
        s = 1.0 / np.sqrt(H)
        W_msg = jax.random.uniform(ks[3], (H, H), jnp.float32, -s, s)
        b_msg = jax.random.uniform(ks[4], (H,), jnp.float32, -s, s)
        edge_embed = jax.random.normal(ks[5], (NUM_EDGE_TYPES + 1, H), dtype=jnp.float32)
        W_ih = jax.random.uniform(ks[6], (3 * H, H), jnp.float32, -s, s)
        W_hh = jax.random.uniform(ks[7], (3 * H, H), jnp.float32, -s, s)
        b_ih = jax.random.uniform(ks[8], (3 * H,), jnp.float32, -s, s)
        b_hh = jax.random.uniform(ks[9], (3 * H,), jnp.float32, -s, s)
        return {'h': h, 'edge_index': edge_index, 'edge_type': edge_type, 'num_nodes': N_NODES, 'W_msg': W_msg, 'b_msg': b_msg, 'edge_embed': edge_embed, 'W_ih': W_ih, 'W_hh': W_hh, 'b_ih': b_ih, 'b_hh': b_hh}
    _L0_gnn_all = _L0_gnn_setup()
    _L0_gnn_in = {k: v for k, v in _L0_gnn_all.items() if k in ('W_msg', 'b_msg', 'edge_embed', 'W_ih', 'W_hh', 'b_ih', 'b_hh')}
    del _L0_gnn_all

    def _L1_gnn_setup():
        import jax, jax.numpy as jnp
        import numpy as np
        BIG = 1000000000.0
        EPS_BETA = 1e-06
        EPS_BN = 1e-05
        N_NODES = 6250
        N_EDGES = 100000
        IN_DIM = 128
        OUT_DIM = 128
        key = jax.random.key(seed)
        ks = jax.random.split(key, 8)
        h = jax.random.normal(ks[0], (N_NODES, IN_DIM), dtype=jnp.float32)
        src = jax.random.randint(ks[1], (N_EDGES,), 0, N_NODES, dtype=jnp.int32)
        dst = jax.random.randint(ks[2], (N_EDGES,), 0, N_NODES, dtype=jnp.int32)
        sigma_GD = jax.random.uniform(ks[3], (N_EDGES,), dtype=jnp.float32)
        fc_w = jax.random.normal(ks[4], (IN_DIM, OUT_DIM), dtype=jnp.float32) / np.sqrt(IN_DIM)
        fc_b = jax.random.normal(ks[5], (OUT_DIM,), dtype=jnp.float32) * 0.01
        attn_w = jax.random.normal(ks[6], (2 * OUT_DIM, 1), dtype=jnp.float32) / np.sqrt(2 * OUT_DIM)
        attn_b = jax.random.normal(ks[7], (1,), dtype=jnp.float32) * 0.01
        bn_gamma = jnp.ones((OUT_DIM,), dtype=jnp.float32)
        bn_beta = jnp.zeros((OUT_DIM,), dtype=jnp.float32)
        return {'h': h, 'src': src, 'dst': dst, 'sigma_GD': sigma_GD, 'fc_w': fc_w, 'fc_b': fc_b, 'attn_w': attn_w, 'attn_b': attn_b, 'bn_gamma': bn_gamma, 'bn_beta': bn_beta}
    _L1_gnn_all = _L1_gnn_setup()
    _L1_gnn_in = {k: v for k, v in _L1_gnn_all.items() if k in ('fc_w', 'fc_b', 'attn_w', 'attn_b', 'bn_gamma', 'bn_beta')}
    del _L1_gnn_all
    return {'x': x, 'src': src, 'dst': dst, 'edge_type_9': edge_type_9, 'edge_weight': edge_weight, 'L0_gnn_W_msg': _L0_gnn_in['W_msg'], 'L0_gnn_b_msg': _L0_gnn_in['b_msg'], 'L0_gnn_edge_embed': _L0_gnn_in['edge_embed'], 'L0_gnn_W_ih': _L0_gnn_in['W_ih'], 'L0_gnn_W_hh': _L0_gnn_in['W_hh'], 'L0_gnn_b_ih': _L0_gnn_in['b_ih'], 'L0_gnn_b_hh': _L0_gnn_in['b_hh'], 'L1_gnn_fc_w': _L1_gnn_in['fc_w'], 'L1_gnn_fc_b': _L1_gnn_in['fc_b'], 'L1_gnn_attn_w': _L1_gnn_in['attn_w'], 'L1_gnn_attn_b': _L1_gnn_in['attn_b'], 'L1_gnn_bn_gamma': _L1_gnn_in['bn_gamma'], 'L1_gnn_bn_beta': _L1_gnn_in['bn_beta']}

def reference(x, src, dst, edge_type_9, edge_weight, L0_gnn_W_msg, L0_gnn_b_msg, L0_gnn_edge_embed, L0_gnn_W_ih, L0_gnn_W_hh, L0_gnn_b_ih, L0_gnn_b_hh, L1_gnn_fc_w, L1_gnn_fc_b, L1_gnn_attn_w, L1_gnn_attn_b, L1_gnn_bn_gamma, L1_gnn_bn_beta):
    import jax
    import jax.numpy as jnp

    def _L0_gnn_ref(h, edge_index, edge_type, num_nodes, W_msg, b_msg, edge_embed, W_ih, W_hh, b_ih, b_hh):
        import jax, jax.numpy as jnp
        import numpy as np
        NUM_EDGE_TYPES = 8
        HIDDEN = 128
        N_NODES = 6250
        N_EDGES = 75000

        def _gru_cell(x, h, W_ih, W_hh, b_ih, b_hh):
            H = h.shape[-1]
            gi = x @ W_ih.T + b_ih
            gh = h @ W_hh.T + b_hh
            i_r, i_z, i_n = (gi[:, :H], gi[:, H:2 * H], gi[:, 2 * H:])
            h_r, h_z, h_n = (gh[:, :H], gh[:, H:2 * H], gh[:, 2 * H:])
            r = jax.nn.sigmoid(i_r + h_r)
            z = jax.nn.sigmoid(i_z + h_z)
            n = jnp.tanh(i_n + r * h_n)
            return (1.0 - z) * n + z * h
        src = edge_index[0]
        dst = edge_index[1]
        src_h = h[src] @ W_msg.T + b_msg
        emb = edge_embed[jnp.clip(edge_type, 0, NUM_EDGE_TYPES)]
        msg = src_h + emb
        messages = jax.ops.segment_sum(msg, dst, num_segments=num_nodes)
        h_new = _gru_cell(messages, h[:num_nodes], W_ih, W_hh, b_ih, b_hh)
        result = jnp.zeros_like(h).at[:num_nodes].set(h_new)
        return result

    def _L1_gnn_ref(h, src, dst, sigma_GD, fc_w, fc_b, attn_w, attn_b, bn_gamma, bn_beta):
        import jax, jax.numpy as jnp
        import numpy as np
        BIG = 1000000000.0
        EPS_BETA = 1e-06
        EPS_BN = 1e-05
        N_NODES = 6250
        N_EDGES = 100000
        IN_DIM = 128
        OUT_DIM = 128
        n = h.shape[0]
        z = h @ fc_w + fc_b
        z = jnp.where(jnp.isinf(z), BIG, z)
        d = z.shape[1]
        w_src, w_dst = (attn_w[:d], attn_w[d:])
        z_src = z[src]
        a = z_src @ w_src + z[dst] @ w_dst + attn_b
        a = jnp.where(jnp.isinf(a), BIG, a)
        e = jax.nn.leaky_relu(a, negative_slope=0.01)[:, 0]
        m = jax.ops.segment_max(e, dst, num_segments=n)
        ex = jnp.exp(e - m[dst])
        denom = jax.ops.segment_sum(ex, dst, num_segments=n)
        alpha = ex / denom[dst]
        bsum = jax.ops.segment_sum(sigma_GD, dst, num_segments=n)
        beta = sigma_GD / (bsum[dst] + EPS_BETA)
        h_new = jax.ops.segment_sum((alpha * beta)[:, None] * z_src, dst, num_segments=n)
        h_new = jnp.where(jnp.isinf(h_new), BIG, h_new)
        mu = h_new.mean(axis=0)
        var = ((h_new - mu) ** 2).mean(axis=0)
        h_bn = (h_new - mu) * jax.lax.rsqrt(var + EPS_BN) * bn_gamma + bn_beta
        return jax.nn.elu(h_bn)
    edge_index = jnp.stack([src, dst])
    h = jnp.maximum(_layernorm(x, axis=-1), 0.0)
    x = x + _L0_gnn_ref(h, edge_index, edge_type_9, 6250, L0_gnn_W_msg, L0_gnn_b_msg, L0_gnn_edge_embed, L0_gnn_W_ih, L0_gnn_W_hh, L0_gnn_b_ih, L0_gnn_b_hh)
    h = jnp.maximum(_layernorm(x, axis=-1), 0.0)
    x = x + _L1_gnn_ref(h, src, dst, edge_weight, L1_gnn_fc_w, L1_gnn_fc_b, L1_gnn_attn_w, L1_gnn_attn_b, L1_gnn_bn_gamma, L1_gnn_bn_beta)
    return x

_drawn_inputs = setup_inputs


def setup_inputs(seed=0):
    import zlib

    import numpy as np

    out = dict(_drawn_inputs(seed))
    spreads = {'L1_gnn_bn_gamma': (1.0, 0.2), 'L1_gnn_bn_beta': (0.0, 0.1)}
    factors = {'L0_gnn_b_ih': 8.0, 'L0_gnn_b_hh': 8.0, 'L1_gnn_fc_b': 8.0}
    for name, (base, spread) in spreads.items():
        noise = np.random.default_rng([zlib.crc32(name.encode()), seed]).standard_normal(out[name].shape)
        drawn = base * np.exp(spread * noise) if base else spread * noise
        out[name] = jnp.asarray(drawn.astype(out[name].dtype))
    for name, factor in factors.items():
        out[name] = (out[name] * factor).astype(out[name].dtype)
    return out
```

```python
from contextlib import ExitStack

import numpy as np

import concourse.bass as bass
from concourse import mybir

F32 = mybir.dt.float32
BF16 = mybir.dt.bfloat16
I32 = mybir.dt.int32
U32 = mybir.dt.uint32
ALU = mybir.AluOpType
ACT = mybir.ActivationFunctionType
AX = mybir.AxisListType

P = 128
TILES = 8
GROUP = TILES * P
WINDOW = 64
PAD_DST = -20000.0
LN_EPS = 1e-5
BETA_EPS = 1e-6
BIG = 1e9
F32_MAX = float(np.finfo(np.float32).max)
TYPES = 9


def gnn(nc, x, src, dst, edge_type, edge_weight, W_msg, b_msg, edge_embed, W_ih, W_hh, b_ih, b_hh,
        fc_w, fc_b, attn_w, attn_b, bn_gamma, bn_beta, out):
    N, D = x.shape
    (E,) = src.shape
    NT = -(-N // P)
    NTAIL = N - (NT - 1) * P
    ROWS = NT * P
    BLOCKS = -(-E // (P * P))
    CHUNK = BLOCKS * P
    FULL, REST = E // CHUNK, E % CHUNK
    GROUPS = -(-E // GROUP)
    PAIRS = GROUPS // 2
    ECOLS = BLOCKS * P
    assert D == P and GROUPS == 2 * PAIRS and ECOLS >= (GROUPS + 2) * TILES and NT % 4 == 1
    TURNS = (GROUPS - 2) // 5
    EARLY = 2 * TURNS + 2
    assert GROUPS == EARLY + 3 * TURNS
    WINS = -(-N // WINDOW)
    ACCN = -(-(N + WINDOW) // P) * P
    CH = 4 * P
    NCH = N // CH
    CTAIL = N - NCH * CH

    h_tab = nc.dram_tensor("h_tab", [ROWS, D], F32, kind="Internal").ap()
    z_tab = nc.dram_tensor("z_tab", [ROWS, D], F32, kind="Internal").ap()
    early = nc.dram_tensor("early", [EARLY * P, TILES * D], F32, kind="Internal").ap()
    lo_row = nc.dram_tensor("lo_row", [1, P * CHUNK], BF16, kind="Internal").ap()
    ad_row = nc.dram_tensor("ad_row", [1, ROWS], F32, kind="Internal").ap()

    with ExitStack() as ctx:
        def sb(name, cols, dt=F32, rows=P):
            return ctx.enter_context(nc.sbuf_tensor(name, [rows, cols], dt))

        phase = ExitStack()
        held = []

        def sem(name):
            held.append(phase.enter_context(nc.semaphore(name)))
            return held[-1]

        landed = [ctx.enter_context(nc.semaphore(f"landed{s}")) for s in range(3)]
        far_landed1 = ctx.enter_context(nc.semaphore("far_landed1"))
        far_landed7 = ctx.enter_context(nc.semaphore("far_landed7"))

        def end_phase():
            with nc.Block() as block:
                @block.sync
                def _(sp):
                    for s in held:
                        sp.sem_clear(s)
            phase.close()
            held.clear()

        bank = [ctx.enter_context(nc.psum_tensor(f"bank{i}", [P, 512], F32)) for i in range(8)]

        nodes = sb("nodes", NT * D)
        sums = sb("sums", ACCN)
        side = sb("side", ACCN)
        dst_terms = sb("dst_terms", ACCN)
        srcT = sb("srcT", ECOLS, U32)
        hiT = sb("hiT", ECOLS)
        relT = sb("relT", ECOLS)
        typeT = sb("typeT", ECOLS)
        sigT = sb("sigT", ECOLS)
        logits = sb("logits", 2 * ECOLS)
        logits3 = logits[:, :].rearrange("p (a t) -> p a t", a=2)
        dstC = sb("dstC", CHUNK)
        edgeC = [dst_terms[:, k * CHUNK:(k + 1) * CHUNK] for k in range(3)]
        scanC = [side[:, k * CHUNK:(k + 1) * CHUNK] for k in range(3)]

        rows = [sb(f"rows{s}", TILES * D) for s in range(3)] + [t[:, 0:TILES * D] for t in (typeT, hiT)]
        hot = [sb(f"hot{s}", TILES * WINDOW) for s in range(5)]
        whot = [sb(f"whot{s}", TILES * WINDOW) for s in range(5)]
        thot = [sb(f"thot{s}", TILES * TYPES) for s in range(2)]
        idx = [sb(f"idx{s}", TILES, U32) for s in range(3)]
        base_i = sb("base_i", GROUPS + 4, I32, 1)
        base_turn = sb("base_turn", 5 * (TURNS + 1), I32, 1)
        base_f = sb("base_f", GROUPS, F32, 1)
        base_b = sb("base_b", GROUPS)

        ident = sb("ident", P)
        ones = sb("ones", P)
        iota_i = sb("iota_i", P, I32)
        iota = sb("iota", P)
        pidx_i = sb("pidx_i", 1, I32)
        pidx = sb("pidx", 1)
        eps = sb("eps", 1)
        big = sb("big", P)
        end_i = sb("end_i", GROUPS, I32, 1)
        end_f = sb("end_f", GROUPS, F32, 1)
        far_group = sb("far_group", GROUPS, I32, 1)
        far_rank = sb("far_rank", GROUPS, I32, 1)
        far_count = sb("far_count", GROUPS, F32, 1)
        ones_row = end_f[:, :]
        far_any = sb("far_any", 1, I32, 1)
        far_ids = [sb(f"far_ids{k}", TILES) for k in range(2)]
        win_ids = sb("win_ids", WINDOW)
        win_base = sb("win_base", WINS)

        wraw = [rows[2][:, i * D:(i + 1) * D] for i in range(7)]
        WmT = sb("WmT", D)
        WihT = sb("WihT", 3 * D)
        WhhT = sb("WhhT", 3 * D)
        emb = sb("emb", D, F32, TYPES)
        bmsg = sb("bmsg", D, F32, TYPES)
        bias_ih, bias_hh = hot[2][0:1, 0:3 * D], hot[3][0:1, 0:3 * D]
        bias = sb("bias", 4 * D, F32, 1)
        fcw = sb("fcw", D)
        fcb = sb("fcb", D, F32, 1)
        wsd = sb("wsd", 2 * D)
        battn = sb("battn", 1)
        gamma = sb("gamma", 1)
        beta = sb("beta", 1)

        stats = sb("stats", NT * 6)
        st = sb("st", 8 * NT)
        rstd = sb("rstd", NT)
        shift = sb("shift", NT)
        terms = sb("terms", 2 * NT)
        as_tab, ad_tab = terms[:, 0:NT], terms[:, NT:2 * NT]
        dots = [sb(f"dots{s}", 2) for s in range(4)]
        adT = sb("adT", P, F32, NT)

        def dram_tile(tab, t):
            return tab[bass.ds(t * P, P), :]

        consts, ld_x, ld_e, ld_w, zeroed, padded, blank = (sem(n) for n in (
            "consts", "ld_x", "ld_e", "ld_w", "zeroed", "padded", "blank"))
        v1, a1, p1 = sem("v1"), sem("a1"), sem("p1")
        h_made, lo_stored = sem("h_made"), sem("lo_stored")
        h_stored = [sem(f"h_stored{i}") for i in range(2)]
        src_i = edgeC[0].bitcast(I32)
        raw_i = [edgeC[1].bitcast(I32), edgeC[2].bitcast(I32)]
        srcC, typeC, sigC = scanC
        lo_i = logits[:, 0:CHUNK].bitcast(I32)
        lo_b = logits[:, CHUNK:2 * CHUNK].bitcast(BF16)[:, 0:CHUNK]
        hbuf = [rows[0], rows[1]]
        var1, std1, scale1 = sem("var1"), sem("std1"), sem("scale1")
        chunk_loads = [(src, src_i), (dst, raw_i[0]), (edge_type, raw_i[1]), (edge_weight, sigC)]

        def norm_scalars(eng, chain, n, var_ready, std_ready, scale_ready):
            s = stats[:, :].rearrange("p (t k) -> p k t", k=6)
            mean2, diff, m2, diff2, part, var, std = (st[:, k * NT:(k + 1) * NT] for k in range(7))
            nc.vector.tensor_tensor(mean2, s[:, 1, :], s[:, 4, :], ALU.add).then_inc(chain, 1)
            nc.vector.tensor_tensor(diff, s[:, 1, :], s[:, 4, :], ALU.subtract).then_inc(chain, 1)
            nc.vector.tensor_tensor(m2, s[:, 2, :], s[:, 5, :], ALU.add).then_inc(chain, 1)
            eng.wait_ge(chain, n + 3)
            nc.vector.tensor_tensor(diff2, diff, diff, ALU.mult).then_inc(chain, 1)
            nc.vector.tensor_scalar(part, m2, 1.0 / D, LN_EPS, ALU.mult, ALU.add).then_inc(chain, 1)
            eng.wait_ge(chain, n + 5)
            nc.vector.scalar_tensor_tensor(var, diff2, 0.25, part, ALU.mult, ALU.add).then_inc(var_ready, 1)
            eng.wait_ge(std_ready, 1)
            nc.vector.reciprocal(rstd[:, :], std).then_inc(chain, 1)
            eng.wait_ge(chain, n + 6)
            nc.vector.scalar_tensor_tensor(shift[:, :], mean2, -0.5, rstd[:, :], ALU.mult,
                                           ALU.mult).then_inc(scale_ready, 1)

        with nc.Block() as block:
            @block.sync
            def _(sp):
                sp.wait_ge(padded, 5)
                for a, to in chunk_loads:
                    a2 = a[0:FULL * CHUNK].rearrange("(p k) -> p k", k=CHUNK)
                    sp.dma_start(to[0:FULL, :], a2).then_inc(ld_e, 16)
                    sp.dma_start(to[FULL:FULL + 1, 0:REST],
                                 a[FULL * CHUNK:E].rearrange("(p k) -> p k", p=1)).then_inc(ld_e, 16)
                sp.dma_start(base_i[0:1, 0:GROUPS],
                             dst[0:E].rearrange("(p k) -> p k", p=1)[:, 0:(GROUPS - 1) * GROUP + 1:GROUP],
                             allow_slow_non_contiguous=True).then_inc(ld_e, 16)
                sp.dma_start(end_i[0:1, 0:GROUPS - 1],
                             dst[0:E].rearrange("(p k) -> p k", p=1)[:, GROUP - 1:(GROUPS - 1) * GROUP:GROUP],
                             allow_slow_non_contiguous=True).then_inc(ld_e, 16)
                sp.dma_start(end_i[0:1, GROUPS - 1:GROUPS], dst[E - 1:E].rearrange("(p k) -> p k", p=1)).then_inc(ld_e, 16)
                sp.dma_start(wraw[0], W_msg).then_inc(ld_w, 16)
                for k in range(3):
                    sp.dma_start(wraw[1 + k], W_ih[k * D:(k + 1) * D, :]).then_inc(ld_w, 16)
                    sp.dma_start(wraw[4 + k], W_hh[k * D:(k + 1) * D, :]).then_inc(ld_w, 16)
                sp.dma_start(emb[:, :], edge_embed).then_inc(ld_w, 16)
                sp.dma_start(bmsg[:, :], b_msg.rearrange("(a d) -> a d", a=1).broadcast_to([TYPES, D])).then_inc(ld_w, 16)
                sp.dma_start(bias_ih, b_ih.rearrange("(a d) -> a d", a=1)).then_inc(ld_w, 16)
                sp.dma_start(bias_hh, b_hh.rearrange("(a d) -> a d", a=1)).then_inc(ld_w, 16)
                sp.dma_start(fcw[:, :], fc_w).then_inc(ld_w, 16)
                sp.dma_start(fcb[:, :], fc_b.rearrange("(a d) -> a d", a=1)).then_inc(ld_w, 16)
                sp.dma_start(wsd[:, :], attn_w.rearrange("k a -> a k").broadcast_to([P, 2 * D])).then_inc(ld_w, 16)
                sp.dma_start(battn[:, :], attn_b.rearrange("(a d) -> a d", a=1).broadcast_to([P, 1])).then_inc(ld_w, 16)
                sp.dma_start(gamma[:, :], bn_gamma.rearrange("(d a) -> d a", a=1)).then_inc(ld_w, 16)
                sp.dma_start(beta[:, :], bn_beta.rearrange("(d a) -> d a", a=1)).then_inc(ld_w, 16)
                sp.wait_ge(v1, 2)
                sp.dma_start(lo_row.rearrange("a (p k) -> (a p) k", p=P), lo_b).then_inc(lo_stored, 16)
                for b in range(NT // 8):
                    sp.wait_ge(h_made, 8 * (b + 1))
                    sp.dma_start(h_tab[b * 8 * P:(b + 1) * 8 * P, :].rearrange("(t p) d -> p t d", p=P),
                                 hbuf[b % 2][:, :].rearrange("p (t d) -> p t d", d=D)).then_inc(h_stored[b % 2], 16)
                sp.wait_ge(h_made, NT)
                sp.dma_start(h_tab[(NT - 1) * P:NT * P, :], hbuf[0][:, 0:D]).then_inc(h_stored[0], 16)
                sp.wait_ge(h_stored[0], 16 * (NT // 16 + 1))
                sp.wait_ge(h_stored[1], 16 * (NT // 16))
                sp.wait_ge(lo_stored, 16)
                sp.wait_ge(ld_w, 16 * 17)
                sp.wait_ge(ld_e, 16 * 11)

            @block.gpsimd
            def _(pool):
                nc.gpsimd.memset(src_i, 0).then_inc(padded, 1)
                nc.gpsimd.memset(raw_i[0], int(PAD_DST)).then_inc(padded, 1)
                nc.gpsimd.memset(raw_i[1], 0).then_inc(padded, 1)
                nc.gpsimd.memset(sigC, 0.0).then_inc(padded, 1)
                nc.gpsimd.memset(ident[:, :], 0.0).then_inc(blank, 1)
                nc.gpsimd.memset(ones[:, :], 1.0).then_inc(consts, 1)
                nc.gpsimd.memset(eps[:, :], LN_EPS).then_inc(consts, 1)
                nc.gpsimd.memset(big[:, :], BIG).then_inc(consts, 1)
                nc.gpsimd.iota(iota_i[:, :], [[1, P]], base=0, channel_multiplier=0).then_inc(consts, 1)
                nc.gpsimd.iota(pidx_i[:, :], [[0, 1]], base=0, channel_multiplier=1).then_inc(consts, 1)
                pool.wait_ge(blank, 1)
                nc.gpsimd.affine_select(out=ident[:, :], in_=ident[:, :], compare_op=ALU.not_equal, fill=1.0,
                                        base=0, pattern=[[-1, P]], channel_multiplier=1).then_inc(consts, 1)
                pool.wait_ge(consts, 6)
                nc.gpsimd.tensor_copy(iota[:, :], iota_i[:, :]).then_inc(consts, 1)
                nc.gpsimd.tensor_scalar(win_base[:, :], iota_i[:, 0:WINS], float(WINDOW), 1.0, ALU.mult, ALU.add).then_inc(consts, 1)
                nc.gpsimd.tensor_copy(pidx[:, :], pidx_i[:, :]).then_inc(consts, 1)

            @block.scalar
            def _(act):
                act.wait_ge(zeroed, 1)
                act.dma_start(nodes[:, 0:(NT - 1) * D].rearrange("p (t d) -> p t d", d=D),
                              x[0:(NT - 1) * P, :].rearrange("(t p) d -> p t d", p=P)).then_inc(ld_x, 16)
                act.dma_start(nodes[0:NTAIL, (NT - 1) * D:NT * D], x[(NT - 1) * P:N, :]).then_inc(ld_x, 16)
                act.wait_ge(ld_e, 16 * 11)
                nc.scalar.activation(typeC, raw_i[1], ACT.Copy).then_inc(a1, 1)
                act.wait_ge(var1, 1)
                nc.scalar.activation(st[:, 6 * NT:7 * NT], st[:, 5 * NT:6 * NT], ACT.Sqrt).then_inc(std1, 1)
                act.wait_ge(scale1, 1)
                for b in range(NT // 8 + 1):
                    if b >= 2:
                        act.wait_ge(h_stored[b % 2], 16 * (b // 2))
                    for k in range(8 if b < NT // 8 else 1):
                        t = 8 * b + k
                        nc.scalar.activation(hbuf[b % 2][:, k * D:(k + 1) * D], nodes[:, t * D:(t + 1) * D],
                                             ACT.Relu, bias=shift[:, t:t + 1],
                                             scale=rstd[:, t:t + 1]).then_inc(h_made, 1)

            @block.tensor
            def _(pe):
                pe.wait_ge(consts, 9)
                k = 0
                for n, c in enumerate((srcC, dstC[:, :], typeC, sigC)):
                    if n == 0:
                        pe.wait_ge(v1, 4)
                    if n == 2:
                        pe.wait_ge(a1, 1)
                    for b in range(0, BLOCKS, 4):
                        if k >= 8:
                            pe.wait_ge(v1, 4 + k - 7)
                        for q in range(b, min(b + 4, BLOCKS)):
                            mm = nc.tensor.transpose(bank[k % 8][:, (q - b) * P:(q - b + 1) * P],
                                                     c[:, q * P:(q + 1) * P], ident[:, :])
                        mm.then_inc(p1, 1)
                        k += 1
                pe.wait_ge(v1, 5 + k)
                nc.tensor.matmul(bank[0][:, 0:GROUPS], ones[0:1, :], base_f[:, :], start=True, stop=True).then_inc(p1, 1)
                pe.wait_ge(ld_w, 16 * 17)
                for i in range(7):
                    mm = nc.tensor.transpose(bank[1 + i // 4][:, (i % 4) * P:(i % 4 + 1) * P], wraw[i], ident[:, :])
                mm.then_inc(p1, 1)

            @block.vector
            def _(dve):
                nc.vector.memset(nodes[:, (NT - 1) * D:NT * D], 0.0).then_inc(zeroed, 1)
                nc.vector.memset(base_i[:, :], 0).then_inc(padded, 1)
                dve.wait_ge(ld_e, 16 * 11)
                nc.vector.tensor_scalar(lo_i, src_i, P - 1, None, ALU.bitwise_and).then_inc(v1, 1)
                dve.wait_ge(v1, 1)
                nc.vector.tensor_copy(lo_b, lo_i).then_inc(v1, 1)
                nc.vector.tensor_copy(srcC, src_i).then_inc(v1, 1)
                nc.vector.tensor_copy(dstC[:, :], raw_i[0]).then_inc(v1, 1)
                per = -(-BLOCKS // 4)
                for k in range(4 * per):
                    to = (srcT, relT, typeT, sigT)[k // per]
                    b = 4 * (k % per)
                    m = min(4, BLOCKS - b)
                    dve.wait_ge(p1, k + 1)
                    view = to[:, :].rearrange("j (p b) -> j b p", b=BLOCKS)[:, b:b + m, :]
                    nc.vector.tensor_copy(view, bank[k % 8][:, 0:m * P].rearrange("j (b p) -> j b p", b=m)).then_inc(v1, 1)
                n = 4 + 4 * per
                nc.vector.tensor_copy(base_f[:, :], base_i[:, 0:GROUPS]).then_inc(v1, 1)
                n += 1
                dve.wait_ge(p1, 4 * per + 1)
                nc.vector.tensor_copy(base_b[:, :], bank[0][:, 0:GROUPS]).then_inc(v1, 1)
                dve.wait_ge(v1, n + 1)
                rel3 = relT[:, 0:GROUPS * TILES].rearrange("p (g j) -> p g j", j=TILES)
                nc.vector.tensor_tensor(rel3, rel3, base_b[:, :].unsqueeze(2).broadcast_to([P, GROUPS, TILES]),
                                        ALU.subtract).then_inc(v1, 1)
                nc.vector.tensor_scalar(typeT[:, :], typeT[:, :], 0.0, float(TYPES - 1), ALU.max, ALU.min).then_inc(v1, 1)
                dve.wait_ge(v1, n + 3)
                nc.vector.tensor_tensor(end_f[:, :], end_i[:, :], base_i[:, 0:GROUPS], ALU.subtract).then_inc(v1, 1)
                nc.vector.tensor_scalar(lo_i, srcT[:, :].bitcast(I32), 7, None, ALU.logical_shift_right).then_inc(v1, 1)
                dve.wait_ge(lo_stored, 16)
                dve.wait_ge(v1, n + 5)
                nc.vector.tensor_copy(hiT[:, :], lo_i).then_inc(v1, 1)
                n += 6
                dve.wait_ge(p1, 4 * per + 2)
                nc.vector.tensor_copy(WmT[:, :], bank[1][:, 0:D]).then_inc(v1, 1)
                nc.vector.tensor_copy(WihT[:, :], bank[1][:, D:4 * D]).then_inc(v1, 1)
                nc.vector.tensor_copy(WhhT[:, :], bank[2][:, 0:3 * D]).then_inc(v1, 1)
                nc.vector.tensor_tensor(emb[:, :], emb[:, :], bmsg[:, :], ALU.add).then_inc(v1, 1)
                nc.vector.tensor_tensor(bias[:, 0:2 * D], bias_ih[:, 0:2 * D], bias_hh[:, 0:2 * D], ALU.add).then_inc(v1, 1)
                nc.vector.tensor_copy(bias[:, 2 * D:3 * D], bias_ih[:, 2 * D:3 * D]).then_inc(v1, 1)
                nc.vector.tensor_copy(bias[:, 3 * D:4 * D], bias_hh[:, 2 * D:3 * D]).then_inc(v1, 1)
                n += 7
                nc.vector.tensor_scalar(far_group[:, :], end_f[:, :], float(WINDOW), None, ALU.is_ge).then_inc(v1, 1)
                dve.wait_ge(v1, n + 1)
                nc.vector.memset(ones_row, 1.0).then_inc(v1, 1)
                n += 1
                dve.wait_ge(v1, n + 1)
                nc.vector.tensor_reduce(far_any[:, :], far_group[:, :], AX.X, ALU.max).then_inc(v1, 1)
                nc.vector.tensor_tensor_scan(far_count[:, :], ones_row, far_group[:, :], 0.0, ALU.mult, ALU.add).then_inc(v1, 1)
                dve.wait_ge(v1, n + 3)
                nc.vector.tensor_tensor(far_rank[:, :], far_count[:, :], far_group[:, :], ALU.subtract).then_inc(v1, 1)
                n += 2
                n += 2
                dve.wait_ge(ld_x, 32)
                with dve.Fori(0, NT) as t:
                    nc.vector.bn_stats(stats[:, bass.ds(t * 6, 6)], nodes[:, bass.ds(t * D, D)]).then_inc(v1, 1)
                n += NT
                dve.wait_ge(v1, n)
                norm_scalars(dve, v1, n, var1, std1, scale1)


        end_phase()

        def slot_sems(name):
            return [sem(f"{name}{s}") for s in range(2)]

        def onehot(to, rel, ids=iota):
            k = to.shape[1] // TILES
            return nc.vector.tensor_tensor(to.rearrange("p (j w) -> p j w", j=TILES),
                                           rel.unsqueeze(2).broadcast_to([P, TILES, k]),
                                           ids[:, 0:k].unsqueeze(1).broadcast_to([P, TILES, k]), ALU.is_equal)

        def columns(t, g):
            return t[:, bass.ds(g * TILES, TILES)]

        def gather(table, s):
            for j in range(TILES):
                yield nc.gpsimd.indirect_dma_start(rows[s][:, j * D:(j + 1) * D], None, table,
                                                   bass.IndirectOffsetOnAxis(ap=idx[s][:, j:j + 1], axis=0))

        def sum_tiles(s, weighted, extra, m):
            for lhs, k, by, c in ((rows[s], D, weighted, 0), (extra, m, hot[s], WINDOW)):
                for j in range(TILES):
                    mm = nc.tensor.matmul(bank[s][0:k, c:c + WINDOW], lhs[:, j * k:(j + 1) * k],
                                          by[:, j * WINDOW:(j + 1) * WINDOW], start=j == 0, stop=j == TILES - 1)
            return mm

        def add_window(s, m, at):
            to, to2 = sums[:, bass.ds(at, WINDOW)], side[0:m, bass.ds(at, WINDOW)]
            yield nc.vector.tensor_tensor(to, to, bank[s][:, 0:WINDOW], ALU.add)
            yield nc.vector.tensor_tensor(to2, to2, bank[s][0:m, WINDOW:2 * WINDOW], ALU.add)

        def far_steps(eng, step):
            with eng.If(eng.value_load(far_any[0:1, 0:1], min_val=0, max_val=1) > 0):
                with eng.Fori(0, GROUPS) as g:
                    with eng.If(eng.value_load(far_group[0:1, bass.ds(g, 1)], min_val=0, max_val=1) > 0):
                        rank = eng.value_load(far_rank[0:1, bass.ds(g, 1)], min_val=0, max_val=GROUPS)
                        with eng.Fori(0, WINS) as w:
                            step(g, w, rank * WINS + w)
                    eng.nop()
                eng.nop()
            eng.nop()

        def far_destinations(dve, g, w, q, done):
            n = 4 * q
            rel = columns(relT, g)
            nc.vector.tensor_scalar(far_ids[0][:, :], rel, float(WINDOW), None, ALU.is_ge).then_inc(done, 1)
            nc.vector.tensor_scalar(far_ids[1][:, :], rel, base_b[:, bass.ds(g, 1)], 1.0, ALU.add, ALU.add).then_inc(done, 1)
            dve.wait_ge(done, n + 2)
            nc.vector.tensor_tensor(far_ids[1][:, :], far_ids[1][:, :], far_ids[0][:, :], ALU.mult).then_inc(done, 1)
            nc.vector.tensor_scalar(win_ids[:, :], iota[:, 0:WINDOW], win_base[:, bass.ds(w, 1)], None, ALU.add).then_inc(done, 1)
            dve.wait_ge(done, n + 4)
            return far_ids[1][:, :]

        staged1, hot1, summed1 = (slot_sems(n) for n in ("staged1", "hot1", "summed1"))
        issued1 = sem("issued1")
        added1 = sem("added1")

        with nc.Block() as block:
            @block.gpsimd
            def _(pool):
                with pool.Fori(0, PAIRS) as i:
                    for s in range(2):
                        pool.wait_ge(staged1[s], i + 1)
                        pool.sem_inc(issued1)
                        for d in gather(h_tab, s):
                            d.then_inc(landed[s], 16)

            @block.tensor
            def _(pe):
                with pe.Fori(0, PAIRS) as i:
                    for s in range(2):
                        pe.wait_ge(hot1[s], 2 * i + 2)
                        pe.wait_ge(added1, 4 * i + 2 * s + 2)
                        pe.wait_ge(landed[s], (i + 1) * (16 * TILES))
                        sum_tiles(s, hot[s], thot[s], TYPES).then_inc(summed1[s], 1)

            @block.vector
            def _(dve):
                def stage(g, s):
                    nc.vector.tensor_copy(idx[s][:, :], columns(srcT, g)).then_inc(staged1[s], 1)

                def build(g, s):
                    onehot(hot[s][:, :], columns(relT, g)).then_inc(hot1[s], 1)
                    onehot(thot[s][:, :], columns(typeT, g)).then_inc(hot1[s], 1)

                for s in range(2):
                    stage(s, s)
                for s in range(2):
                    build(s, s)
                nc.vector.memset(sums[:, :], 0.0).then_inc(added1, 2)
                nc.vector.memset(side[:, :], 0.0).then_inc(added1, 2)
                with dve.Fori(0, PAIRS) as i:
                    at = [dve.value_load(base_i[0:1, bass.ds(2 * i + s, 1)], min_val=0, max_val=N - 1)
                          for s in range(2)]
                    for s in range(2):
                        dve.wait_ge(summed1[s], i + 1)
                        stage(2 * i + (2 + s), s)
                        dve.wait_ge(added1, 4 * i + 2 * s + 4)
                        for a in add_window(s, TYPES, at[s]):
                            a.then_inc(added1, 1)
                        build(2 * i + (2 + s), s)

        far1 = sem("far1")
        LAST_ADD = 4 + 2 * GROUPS
        with nc.Block() as block:
            @block.gpsimd
            def _(pool):
                def step(g, w, q):
                    pool.wait_ge(staged1[0], q + (PAIRS + 2))
                    pool.sem_inc(issued1)
                    for d in gather(h_tab, 0):
                        d.then_inc(far_landed1, 16)

                far_steps(pool, step)

            @block.tensor
            def _(pe):
                def step(g, w, q):
                    pe.wait_ge(hot1[0], 2 * q + (2 * PAIRS + 4))
                    pe.wait_ge(far_landed1, (q + 1) * (16 * TILES))
                    sum_tiles(0, hot[0], thot[0], TYPES).then_inc(summed1[0], 1)

                far_steps(pe, step)

            @block.vector
            def _(dve):
                def step(g, w, q):
                    nc.vector.tensor_copy(idx[0][:, :], columns(srcT, g)).then_inc(staged1[0], 1)
                    ids = far_destinations(dve, g, w, q, far1)
                    onehot(hot[0][:, :], ids, win_ids).then_inc(hot1[0], 1)
                    onehot(thot[0][:, :], columns(typeT, g)).then_inc(hot1[0], 1)
                    dve.wait_ge(summed1[0], q + (PAIRS + 1))
                    dve.wait_ge(added1, 2 * q + LAST_ADD)
                    for a in add_window(0, TYPES, w * WINDOW):
                        a.then_inc(added1, 1)

                far_steps(dve, step)

        end_phase()

        SLOTS = 4
        hcur = [rows[s // 2][:, (s % 2) * D:(s % 2 + 1) * D] for s in range(SLOTS)]
        turned = [rows[s // 2][:, (2 + 2 * (s % 2)) * D:(4 + 2 * (s % 2)) * D] for s in range(SLOTS)]
        hT, msgT = [b[:, 0:D] for b in turned], [b[:, D:2 * D] for b in turned]
        new = [rows[s // 2][:, (6 + s % 2) * D:(7 + s % 2) * D] for s in range(SLOTS)]
        gates = [(hot + whot)[s][:, 0:2 * D] for s in range(SLOTS)]
        cand = [(hot + whot)[s][:, 2 * D:3 * D] for s in range(SLOTS)]

        def ring(name):
            return [sem(f"{name}{s}") for s in range(SLOTS)]

        def tiles_in_ring(eng, pipeline):
            pipeline((0, 0, 0), None)
            with eng.Fori(0, (NT - 1) // SLOTS) as i:
                for k in range(1, SLOTS + 1):
                    pipeline((i * SLOTS + k, k % SLOTS, i + k // SLOTS), (i * SLOTS + (k - 1), k - 1, i))
            pipeline(None, (NT - 1, (NT - 1) % SLOTS, (NT - 1) // SLOTS))

        (h_in, msg_raw, msg_ready, gate_raw, gate_ready, pre_ready, cand_ready,
         tile_free) = (ring(n) for n in ("h_in", "msg_raw", "msg_ready", "gate_raw",
                                         "gate_ready", "pre_ready", "cand_ready", "tile_free"))
        v3, var3, std3, scale3 = sem("v3"), sem("var3"), sem("std3"), sem("scale3")

        with nc.Block() as block:
            @block.sync
            def _(sp):
                for s in range(SLOTS):
                    sp.dma_start(hcur[s], dram_tile(h_tab, s)).then_inc(h_in[s], 16)
                with sp.Fori(0, (NT - 1) // SLOTS - 1) as i:
                    for s in range(SLOTS):
                        sp.wait_ge(tile_free[s], i + 1)
                        sp.dma_start(hcur[s], dram_tile(h_tab, i * SLOTS + (SLOTS + s))).then_inc(h_in[s], 16)
                sp.wait_ge(tile_free[0], (NT - 1) // SLOTS)
                sp.dma_start(hcur[0], dram_tile(h_tab, NT - 1)).then_inc(h_in[0], 16)

            @block.tensor
            def _(pe):
                def pipeline(a, b):
                    if a:
                        t, s, n = a
                        pe.wait_ge(h_in[s], (n + 1) * 16)
                        nc.tensor.transpose(bank[s][:, 0:D], hcur[s], ident[:, :])
                        nodes_t = bass.ds(t * P, P)
                        nc.tensor.matmul(bank[s][:, D:2 * D], WmT[:, :], sums[:, nodes_t], start=True, stop=False)
                        nc.tensor.matmul(bank[s][:, D:2 * D], emb[:, :], side[0:TYPES, nodes_t], start=False,
                                         stop=True).then_inc(msg_raw[s], 1)
                    if b:
                        t, s, n = b
                        g = bank[4 + s]
                        nc.tensor.matmul(g[:, 0:4 * D], ones[0:1, :], bias[:, :], start=True, stop=False)
                        pe.wait_ge(msg_ready[s], n + 1)
                        nc.tensor.matmul(g[:, 0:2 * D], hT[s], WhhT[:, 0:2 * D], start=False, stop=False)
                        nc.tensor.matmul(g[:, 3 * D:4 * D], hT[s], WhhT[:, 2 * D:3 * D], start=False, stop=False)
                        nc.tensor.matmul(g[:, 0:3 * D], msgT[s], WihT[:, :], start=False, stop=True).then_inc(gate_raw[s], 1)

                tiles_in_ring(pe, pipeline)

            @block.scalar
            def _(act):
                def pipeline(a, b):
                    if a:
                        t, s, n = a
                        act.wait_ge(msg_raw[s], n + 1)
                        nc.scalar.activation(turned[s], bank[s][:, 0:2 * D], ACT.Copy).then_inc(msg_ready[s], 1)
                    if b:
                        t, s, n = b
                        act.wait_ge(gate_raw[s], n + 1)
                        nc.scalar.activation(gates[s], bank[4 + s][:, 0:2 * D], ACT.Sigmoid).then_inc(gate_ready[s], 1)
                        act.wait_ge(pre_ready[s], 2 * n + 2)
                        nc.scalar.activation(new[s], cand[s], ACT.Tanh).then_inc(cand_ready[s], 1)

                tiles_in_ring(act, pipeline)
                act.wait_ge(var3, 1)
                nc.scalar.activation(st[:, 6 * NT:7 * NT], st[:, 5 * NT:6 * NT], ACT.Sqrt).then_inc(std3, 1)

            @block.vector
            def _(dve):
                def pipeline(a, b):
                    if b:
                        t, s, n = b
                        r, z = gates[s][:, 0:D], gates[s][:, D:2 * D]
                        dve.wait_ge(gate_ready[s], n + 1)
                        nc.vector.tensor_tensor(cand[s], r, bank[4 + s][:, 3 * D:4 * D], ALU.mult).then_inc(pre_ready[s], 1)
                        dve.wait_ge(pre_ready[s], 2 * n + 1)
                        nc.vector.tensor_tensor(cand[s], cand[s], bank[4 + s][:, 2 * D:3 * D], ALU.add).then_inc(pre_ready[s], 1)
                        dve.wait_ge(cand_ready[s], n + 1)
                        x_t = nodes[:, bass.ds(t * D, D)]
                        nc.vector.tensor_tensor(cand[s], hcur[s], new[s], ALU.subtract).then_inc(v3, 1)
                        nc.vector.tensor_tensor(x_t, x_t, new[s], ALU.add).then_inc(v3, 1)
                        dve.wait_ge(v3, 4 * t + 1)
                        nc.vector.tensor_tensor(cand[s], cand[s], z, ALU.mult).then_inc(v3, 1)
                        dve.wait_ge(v3, 4 * t + 3)
                        nc.vector.tensor_tensor(x_t, x_t, cand[s], ALU.add).then_inc(v3, 1)
                        dve.wait_ge(v3, 4 * t + 4)
                        nc.vector.bn_stats(stats[:, bass.ds(t * 6, 6)], x_t).then_inc(tile_free[s], 1)

                tiles_in_ring(dve, pipeline)
                for s in range(SLOTS):
                    dve.wait_ge(tile_free[s], (NT - 1) // SLOTS + (s == 0))
                norm_scalars(dve, v3, 4 * NT, var3, std3, scale3)

        end_phase()

        h2 = hcur
        h2T = hT
        zrow = msgT
        zmask = [m.bitcast(I32) for m in new]
        prod = [(g[:, 0:D], g[:, D:2 * D]) for g in gates]
        (h2_ready, h2T_raw, h2T_ready, z_raw, z_ready, z_stored, guard, dotted) = (
            ring(n) for n in ("h2_ready", "h2T_raw", "h2T_ready", "z_raw", "z_ready", "z_stored", "guard", "dotted"))
        b4, ad_raw, ad_made, ad_stored = (sem(n) for n in ("b4", "ad_raw", "ad_made", "ad_stored"))

        paused4 = sem("paused4")

        def guard_inf(eng, value, mask, filler, done, n, carrier):
            nc.vector.tensor_scalar(mask, value, -F32_MAX, None, ALU.is_lt).then_inc(done, 1)
            eng.wait_ge(done, n + 1)
            nc.vector.scalar_tensor_tensor(mask, value, F32_MAX, mask, ALU.is_gt, ALU.max).then_inc(done, 1)
            eng.wait_ge(done, n + 2)
            eng.sem_inc(carrier)
            return nc.vector.copy_predicated(value, mask, filler)

        with nc.Block() as block:
            @block.scalar
            def _(act):
                def pipeline(a, b):
                    if a:
                        t, s, n = a
                        act.wait_ge(dotted[s], 3 * n + 3)
                        nc.scalar.activation(h2[s], nodes[:, bass.ds(t * D, D)], ACT.Relu, bias=shift[:, bass.ds(t, 1)],
                                             scale=rstd[:, bass.ds(t, 1)]).then_inc(h2_ready[s], 1)
                    if b:
                        t, s, n = b
                        act.wait_ge(h2T_raw[s], n + 1)
                        nc.scalar.activation(h2T[s], bank[s][:, 0:D], ACT.Copy).then_inc(h2T_ready[s], 1)

                tiles_in_ring(act, pipeline)

            @block.tensor
            def _(pe):
                def pipeline(a, b):
                    if a:
                        t, s, n = a
                        pe.wait_ge(h2_ready[s], n + 1)
                        nc.tensor.transpose(bank[s][:, 0:D], h2[s], ident[:, :]).then_inc(h2T_raw[s], 1)
                    if b:
                        t, s, n = b
                        pe.wait_ge(h2T_ready[s], n + 1)
                        nc.tensor.matmul(bank[4 + s][:, 0:D], ones[0:1, :], fcb[:, :], start=True, stop=False)
                        nc.tensor.matmul(bank[4 + s][:, 0:D], h2T[s], fcw[:, :], start=False, stop=True).then_inc(z_raw[s], 1)

                tiles_in_ring(pe, pipeline)
                pe.wait_ge(b4, 1)
                nc.tensor.transpose(bank[0][0:NT, 0:P], ad_tab, ident[:, :]).then_inc(ad_raw, 1)

            @block.vector
            def _(dve):
                for s in range(SLOTS):
                    nc.vector.memset(dots[s][:, :], 0.0).then_inc(dotted[s], 3)

                def pipeline(a, b):
                    if b:
                        t, s, n = b
                        dve.wait_ge(z_raw[s], n + 1)
                        dve.wait_ge(z_stored[s], (n + 1) * 16)
                        nc.vector.tensor_copy(zrow[s], bank[4 + s][:, 0:D]).then_inc(guard[s], 1)
                        dve.wait_ge(guard[s], 4 * n + 1)
                        guard_inf(dve, zrow[s], zmask[s], big[:, :], guard[s], 4 * n + 1, paused4).then_inc(guard[s], 1)
                        dve.wait_ge(guard[s], 4 * n + 4)
                        dve.wait_ge(dotted[s], 3 * n + 3)
                        for k in range(2):
                            nc.vector.tensor_tensor_reduce(prod[s][k], zrow[s], wsd[:, k * D:(k + 1) * D], 1.0, 0.0, ALU.mult,
                                                           ALU.add, dots[s][:, k:k + 1]).then_inc(dotted[s], 1)
                        dve.wait_ge(dotted[s], 3 * n + 5)
                        nc.vector.tensor_copy(terms[:, :].rearrange("p (k t) -> p k t", k=2)[:, :, bass.ds(t, 1)],
                                              dots[s][:, :].unsqueeze(2)).then_inc(dotted[s], 1)

                tiles_in_ring(dve, pipeline)
                for s in range(SLOTS):
                    dve.wait_ge(dotted[s], 3 * ((NT - 1) // SLOTS + (s == 0)) + 3)
                nc.vector.tensor_scalar(ad_tab, ad_tab, battn[:, 0:1], None, ALU.add).then_inc(b4, 1)
                dve.wait_ge(ad_raw, 1)
                nc.vector.tensor_copy(adT[:, :], bank[0][0:NT, 0:P]).then_inc(ad_made, 1)

            @block.sync
            def _(sp):
                def pipeline(a, b):
                    if b:
                        t, s, n = b
                        sp.wait_ge(guard[s], 4 * n + 4)
                        sp.dma_start(dram_tile(z_tab, t), zrow[s]).then_inc(z_stored[s], 16)

                for s in range(SLOTS):
                    sp.sem_inc(z_stored[s], 16)
                tiles_in_ring(sp, pipeline)
                sp.wait_ge(ad_made, 1)
                sp.dma_start(ad_row.rearrange("a (t p) -> (a t) p", p=P), adT[:, :]).then_inc(ad_stored, 16)
                sp.wait_ge(ad_stored, 16)
                for s in range(SLOTS):
                    sp.wait_ge(z_stored[s], 16 * ((NT - 1) // SLOTS + (s == 0) + 1))

        end_phase()

        lo_all = [sums[:, s * GROUP // 2:(s + 1) * GROUP // 2].bitcast(BF16) for s in range(2)]
        lo_hot = [side[:, s * GROUP:(s + 1) * GROUP] for s in range(2)]
        hi_hot = [whot[s][:, 0:TILES * NT] for s in range(2)]
        hi_pick = [hot[s][:, 0:TILES * NT] for s in range(2)]
        lo_in, lo_made, hi_made, picked, chosen, scored = (slot_sems(n) for n in (
            "lo_in", "lo_made", "hi_made", "picked", "chosen", "scored"))
        filled, issued5 = sem("filled"), sem("issued5")
        staged5, put_by = slot_sems("staged5"), slot_sems("put_by")

        score, gate, back = scanC
        fwd = edgeC[0]
        both = edgeC[1]
        edge_cols = st[:, 0:8]
        line = sums[0:1, 2 * GROUP:2 * GROUP + 12 * P]
        to_chunk, v6, a6, to_line, to_col, to_tile = (sem(n) for n in (
            "to_chunk", "v6", "a6", "to_line", "to_col", "to_tile"))
        PER = -(-BLOCKS // 4)

        with nc.Block() as block:
            @block.sync
            def _(sp):
                def load(g, s):
                    sp.dma_start(lo_all[s], lo_row[:, bass.ds(g * GROUP, GROUP)].broadcast_to([P, GROUP])
                                 ).then_inc(lo_in[s], 16)

                for s in range(2):
                    load(s, s)
                with sp.Fori(0, PAIRS) as i:
                    for s in range(2):
                        sp.wait_ge(lo_made[s], i + 1)
                        load(2 * i + (2 + s), s)
                for s in range(2):
                    sp.wait_ge(lo_in[s], 16 * (PAIRS + 1))

            @block.gpsimd
            def _(pool):
                with pool.Fori(0, EARLY // 2) as i:
                    for s in range(2):
                        pool.wait_ge(staged5[s], i + 1)
                        pool.sem_inc(issued5)
                        for d in gather(z_tab, s):
                            d.then_inc(landed[s], 16)

            @block.scalar
            def _(act):
                def stage(g, s):
                    nc.scalar.copy(idx[s][:, :], columns(srcT, g)).then_inc(staged5[s], 1)

                for s in range(2):
                    stage(s, s)
                with act.Fori(0, EARLY // 2) as i:
                    for s in range(2):
                        act.wait_ge(landed[s], (i + (PAIRS + 1)) * (16 * TILES))
                        act.dma_start(early[bass.ds((2 * i + s) * P, P), :], rows[s][:, :]).then_inc(put_by[s], 16)
                        act.wait_ge(put_by[s], (i + 1) * 16)
                        stage(2 * i + (2 + s), s)

            @block.tensor
            def _(pe):
                with pe.Fori(0, PAIRS) as i:
                    for s in range(2):
                        pe.wait_ge(lo_made[s], i + 1)
                        pe.wait_ge(chosen[s], i + 1)
                        for j in range(TILES):
                            mm = nc.tensor.matmul(bank[s][:, j * NT:(j + 1) * NT], lo_hot[s][:, j * P:(j + 1) * P],
                                                  as_tab, start=True, stop=True)
                        mm.then_inc(picked[s], 1)
                for s in range(2):
                    pe.wait_ge(scored[s], PAIRS)
                scores = logits[:, 0:ECOLS].rearrange("j (p b) -> j b p", b=BLOCKS)
                for b in range(BLOCKS):
                    mm = nc.tensor.transpose(bank[b // 4][:, (b % 4) * P:(b % 4 + 1) * P], scores[:, b, :], ident[:, :])
                    if b % 4 == 3 or b == BLOCKS - 1:
                        mm.then_inc(to_chunk, 1)
                pe.wait_ge(a6, 1)
                for k in range(4):
                    mm = nc.tensor.transpose(bank[5][0:1, k * P:(k + 1) * P], edge_cols[:, k:k + 1], ident[:, :])
                mm.then_inc(to_line, 1)
                pe.wait_ge(a6, 2)
                for k in range(2):
                    mm = nc.tensor.transpose(bank[6][:, k:k + 1], line[0:1, (8 + k) * P:(9 + k) * P], ident[0:1, 0:1])
                mm.then_inc(to_col, 1)
                pe.wait_ge(a6, 3)
                for b in range(BLOCKS):
                    mm = nc.tensor.transpose(bank[b // 4][:, (b % 4) * P:(b % 4 + 1) * P], both[:, b * P:(b + 1) * P], ident[:, :])
                    if b % 4 == 3 or b == BLOCKS - 1:
                        mm.then_inc(to_tile, 1)

            @block.vector
            def _(dve):
                def make(g, s, n):
                    dve.wait_ge(lo_in[s], (n + 1) * 16)
                    nc.vector.tensor_scalar(lo_hot[s], lo_all[s], pidx[:, 0:1], None, ALU.is_equal).then_inc(lo_made[s], 1)
                    onehot(hi_hot[s], columns(hiT, g)).then_inc(hi_made[s], 1)

                nc.vector.memset(logits[:, :], 0.0).then_inc(filled, 1)
                for s in range(2):
                    nc.vector.memset(hi_hot[s], 0.0).then_inc(chosen[s], 1)
                    dve.wait_ge(chosen[s], 1)
                dve.wait_ge(filled, 1)
                for s in range(2):
                    make(s, s, 0)
                with dve.Fori(0, PAIRS) as i:
                    for s in range(2):
                        dve.wait_ge(picked[s], i + 1)
                        dve.wait_ge(hi_made[s], i + 1)
                        nc.vector.tensor_tensor(hi_pick[s], bank[s][:, 0:TILES * NT], hi_hot[s], ALU.mult).then_inc(chosen[s], 1)
                        dve.wait_ge(chosen[s], i + 2)
                        make(2 * i + (2 + s), s, i + 1)
                        nc.vector.tensor_reduce(columns(logits, 2 * i + s), hi_pick[s].rearrange("p (j k) -> p j k", j=TILES),
                                                AX.X, ALU.add).then_inc(scored[s], 1)
                for s in range(2):
                    dve.wait_ge(lo_made[s], PAIRS + 1)
                    dve.wait_ge(scored[s], PAIRS)
                n = [0]

                def step(ins):
                    n[0] += 1
                    ins.then_inc(v6, 1)
                    dve.wait_ge(v6, n[0])

                def gates_from(same):
                    step(nc.vector.tensor_scalar(same, same, 2.0, -1.0, ALU.mult, ALU.add))
                    step(nc.vector.tensor_scalar(same, same, F32_MAX, None, ALU.mult))

                def scan(to, by, data, start, backward):
                    r = slice(None, None, -1) if backward else slice(None)
                    step(nc.vector.tensor_tensor_scan(to[:, r], by[:, r], data[:, r], start, ALU.min, ALU.max))

                for k in range(PER):
                    m = min(4, BLOCKS - 4 * k) * P
                    dve.wait_ge(to_chunk, k + 1)
                    step(nc.vector.tensor_copy(score[:, 4 * k * P:4 * k * P + m], bank[k][:, 0:m]))
                step(nc.vector.memset(gate, 1.0))
                step(nc.vector.tensor_tensor(gate[:, 1:CHUNK], dstC[:, 1:CHUNK], dstC[:, 0:CHUNK - 1], ALU.is_equal))
                gates_from(gate)
                step(nc.vector.memset(back, F32_MAX))
                step(nc.vector.tensor_copy(back[:, 0:CHUNK - 1], gate[:, 1:CHUNK]))
                scan(fwd, gate, score, -F32_MAX, False)
                scan(both, back, score, -F32_MAX, True)
                step(nc.vector.tensor_copy(edge_cols[:, 0:1], dstC[:, 0:1]))
                step(nc.vector.tensor_copy(edge_cols[:, 1:2], dstC[:, CHUNK - 1:CHUNK]))
                step(nc.vector.tensor_copy(edge_cols[:, 2:3], fwd[:, CHUNK - 1:CHUNK]))
                step(nc.vector.tensor_copy(edge_cols[:, 3:4], both[:, 0:1]))
                nc.vector.memset(line, 0.0).then_inc(a6, 1)
                dve.wait_ge(a6, 1)
                dve.wait_ge(to_line, 1)
                first, last, f_state, b_state, conn, through, through_b, fs, f_carry, b_carry, tmp, _ = (
                    line[:, k * P:(k + 1) * P] for k in range(12))
                step(nc.vector.tensor_copy(line[:, 0:4 * P], bank[5][0:1, 0:4 * P]))
                step(nc.vector.tensor_tensor(conn[:, 1:P], first[:, 1:P], last[:, 0:P - 1], ALU.is_equal))
                step(nc.vector.tensor_tensor(tmp, first, last, ALU.is_equal))
                step(nc.vector.tensor_tensor(through, tmp, conn, ALU.mult))
                step(nc.vector.tensor_tensor(through_b[:, 0:P - 1], tmp[:, 0:P - 1], conn[:, 1:P], ALU.mult))
                gates_from(through)
                gates_from(through_b)
                gates_from(conn)
                scan(fs, through, f_state, -F32_MAX, False)
                step(nc.vector.memset(f_carry, -F32_MAX))
                step(nc.vector.tensor_tensor(f_carry[:, 1:P], fs[:, 0:P - 1], conn[:, 1:P], ALU.min))
                scan(tmp, through_b, b_state, -F32_MAX, True)
                step(nc.vector.memset(b_carry, -F32_MAX))
                step(nc.vector.tensor_tensor(b_carry[:, 0:P - 1], tmp[:, 1:P], conn[:, 1:P], ALU.min))
                nc.vector.memset(line[:, 11 * P:12 * P], 0.0).then_inc(a6, 1)
                dve.wait_ge(to_col, 1)
                step(nc.vector.tensor_copy(edge_cols[:, 4:6], bank[6][:, 0:2]))
                scan(fwd, gate, score, edge_cols[:, 4:5], False)
                scan(both, back, score, edge_cols[:, 5:6], True)
                nc.vector.tensor_tensor(both, both, fwd, ALU.max).then_inc(a6, 1)
                for k in range(PER):
                    m = min(4, BLOCKS - 4 * k)
                    dve.wait_ge(to_tile, k + 1)
                    view = logits[:, ECOLS:2 * ECOLS].rearrange("j (p b) -> j b p", b=BLOCKS)[:, 4 * k:4 * k + m, :]
                    step(nc.vector.tensor_copy(view, bank[k][:, 0:m * P].rearrange("j (b p) -> j b p", b=m)))

        end_phase()

        ORDER = (0, 3, 1, 4, 2)
        ADDED0 = 2 * len(ORDER)

        def group_of(s, i):
            return EARLY + 3 * i + s if s < 3 else 2 * i + (s - 3)

        staged7, summed7, logit7, prob7, weigh7, small7, loaded7 = ([sem(f"{n}{s}") for s in range(5)] for n in (
            "staged7", "summed7", "logit7", "prob7", "weigh7", "small7", "loaded7"))
        turn_made = sem("turn_made")
        added7, terms_in, zero7, paused7, issued7 = (sem(n) for n in ("added7", "terms_in", "zero7", "paused7", "issued7"))
        small = [WihT[:, s * 9 * TILES:(s + 1) * 9 * TILES] for s in range(5)]
        pair = [t[:, 0:2 * TILES] for t in small]
        lg = [t[:, 2 * TILES:4 * TILES] for t in small]
        lgmask = [t[:, 4 * TILES:6 * TILES].bitcast(I32) for t in small]
        dterm, diff7, ew = ([t[:, k * TILES:(k + 1) * TILES] for t in small] for k in (6, 7, 8))
        SMALL = 9

        def probabilities(g, s):
            pw = pair[s].rearrange("p (j k) -> p k j", k=2)
            nc.scalar.activation(pw[:, 0, :], diff7[s], ACT.Exp).then_inc(prob7[s], 1)
            nc.scalar.activation(pw[:, 1, :], columns(sigT, g), ACT.Copy).then_inc(prob7[s], 1)

        def tile_view(t):
            return t.rearrange("p (j w) -> p j w", j=TILES)

        def stage(g, s):
            nc.vector.tensor_copy(idx[s][:, :], columns(srcT, g)).then_inc(staged7[s], 1)

        def build(g, s, n, at, rel=None, ids=iota):
            k = n * SMALL
            onehot(hot[s][:, :], columns(relT, g) if rel is None else rel, ids).then_inc(small7[s], 1)
            nc.vector.wait_ge(small7[s], k + 1)
            h, w = tile_view(hot[s][:, :]), tile_view(whot[s][:, :])
            nc.vector.tensor_tensor(w, h, dst_terms[:, bass.ds(at, WINDOW)].unsqueeze(1).broadcast_to(
                [P, TILES, WINDOW]), ALU.mult).then_inc(small7[s], 1)
            nc.vector.wait_ge(small7[s], k + 2)
            nc.vector.tensor_reduce(dterm[s], w, AX.X, ALU.add).then_inc(small7[s], 1)
            nc.vector.wait_ge(small7[s], k + 3)
            l3 = lg[s].rearrange("p (a j) -> p a j", a=2)
            nc.vector.tensor_tensor(l3, logits3[:, :, bass.ds(g * TILES, TILES)],
                                    dterm[s].unsqueeze(1).broadcast_to([P, 2, TILES]),
                                    ALU.add).then_inc(small7[s], 1)
            nc.vector.wait_ge(small7[s], k + 4)
            guard_inf(nc.vector, lg[s], lgmask[s], big[:, 0:2 * TILES], small7[s], k + 4, paused7).then_inc(small7[s], 1)
            nc.vector.wait_ge(small7[s], k + 7)
            nc.vector.scalar_tensor_tensor(lg[s], lg[s], 0.01, lg[s], ALU.mult,
                                           ALU.max).then_inc(small7[s], 1)
            nc.vector.wait_ge(small7[s], k + 8)
            nc.vector.tensor_tensor(diff7[s], lg[s][:, 0:TILES], lg[s][:, TILES:2 * TILES],
                                    ALU.subtract).then_inc(logit7[s], 1)
            nc.vector.wait_ge(prob7[s], 2 * n + 2)
            pw = pair[s].rearrange("p (j k) -> p k j", k=2)
            nc.vector.tensor_tensor(ew[s], pw[:, 0, :], pw[:, 1, :], ALU.mult).then_inc(small7[s], 1)
            nc.vector.wait_ge(small7[s], k + 9)
            nc.vector.tensor_tensor(w, h, ew[s].unsqueeze(2).broadcast_to([P, TILES, WINDOW]),
                                    ALU.mult).then_inc(weigh7[s], 1)

        def bases(dve, regs, i):
            dve.reg_load(regs, base_turn[0:1, bass.ds(i * 5, len(regs))])
            return [dve.snap(r, min_val=0, max_val=N - 1) for r in regs]

        with nc.Block() as block:
            @block.sync
            def _(sp):
                def load(s, i):
                    sp.dma_start(rows[s], early[bass.ds(group_of(s, i) * P, P), :]).then_inc(loaded7[s], 16)

                sp.dma_start(dst_terms[:, 0:ROWS], ad_row.broadcast_to([P, ROWS])).then_inc(terms_in, 16)
                for s in (3, 4):
                    load(s, 0)
                with sp.Fori(0, TURNS) as i:
                    for s in (3, 4):
                        sp.wait_ge(summed7[s], i + 1)
                        load(s, i + 1)

            @block.gpsimd
            def _(pool):
                with pool.Fori(0, TURNS) as i:
                    for s in range(3):
                        pool.wait_ge(staged7[s], i + 1)
                        pool.sem_inc(issued7)
                        for d in gather(z_tab, s):
                            d.then_inc(landed[s], 16)

            @block.tensor
            def _(pe):
                def unit(k, s, i):
                    pe.wait_ge(weigh7[s], i + 1)
                    pe.wait_ge(added7, 2 * (5 * i + k) + (ADDED0 - 8))
                    if s < 3:
                        before = PAIRS + EARLY // 2 if s < 2 else 0
                        pe.wait_ge(landed[s], (i + (before + 1)) * (16 * TILES))
                    else:
                        pe.wait_ge(loaded7[s], (i + 1) * 16)
                    sum_tiles(s, whot[s], pair[s], 2).then_inc(summed7[s], 1)

                with pe.Fori(0, TURNS) as i:
                    for k, s in enumerate(ORDER):
                        unit(k, s, i)
                for k, s in enumerate((3, 4)):
                    unit(k, s, TURNS)

            @block.scalar
            def _(act):
                with act.Fori(0, TURNS + 1) as i:
                    for s in ORDER:
                        act.wait_ge(logit7[s], i + 1)
                        probabilities(group_of(s, i), s)

            @block.vector
            def _(dve):
                turns3 = base_turn[:, :].rearrange("p (i u) -> p u i", u=5)
                for k, s in enumerate(ORDER):
                    g0, step = (EARLY + s, 3) if s < 3 else (s - 3, 2)
                    nc.vector.tensor_copy(turns3[:, k, :], base_i[:, g0:g0 + step * TURNS + 1:step]).then_inc(turn_made, 1)
                for s in range(3):
                    stage(group_of(s, 0), s)
                nc.vector.memset(sums[:, :], 0.0).then_inc(added7, ADDED0 // 2)
                nc.vector.memset(side[:, :], 0.0).then_inc(added7, ADDED0 // 2)
                nc.vector.memset(dst_terms[:, ROWS:ACCN], 0.0).then_inc(zero7, 1)
                dve.wait_ge(zero7, 1)
                dve.wait_ge(terms_in, 16)
                dve.wait_ge(turn_made, 5)
                regs = [dve.alloc_register(f"base{k}") for k in range(10)]
                at = bases(dve, regs[0:5], 0)
                for k, s in enumerate(ORDER):
                    build(group_of(s, 0), s, 0, at[k])

                def finish(k, s, i, at):
                    dve.wait_ge(added7, 2 * (5 * i + k) + ADDED0)
                    for a in add_window(s, 2, at):
                        a.then_inc(added7, 1)

                with dve.Fori(0, TURNS) as i:
                    at = bases(dve, regs, i)
                    for k, s in enumerate(ORDER):
                        dve.wait_ge(summed7[s], i + 1)
                        if s < 3:
                            stage(group_of(s, i + 1), s)
                        finish(k, s, i, at[k])
                        build(group_of(s, i + 1), s, i + 1, at[k + 5])
                at = bases(dve, regs[0:5], TURNS)
                for k, s in enumerate((3, 4)):
                    dve.wait_ge(summed7[s], TURNS + 1)
                    finish(k, s, TURNS, at[ORDER.index(s)])

        far7 = sem("far7")
        with nc.Block() as block:
            @block.gpsimd
            def _(pool):
                def step(g, w, q):
                    pool.wait_ge(staged7[0], q + (TURNS + 2))
                    pool.sem_inc(issued7)
                    for d in gather(z_tab, 0):
                        d.then_inc(far_landed7, 16)

                far_steps(pool, step)

            @block.tensor
            def _(pe):
                def step(g, w, q):
                    pe.wait_ge(weigh7[0], q + (TURNS + 2))
                    pe.wait_ge(far_landed7, (q + 1) * (16 * TILES))
                    sum_tiles(0, whot[0], pair[0], 2).then_inc(summed7[0], 1)

                far_steps(pe, step)

            @block.scalar
            def _(act):
                def step(g, w, q):
                    act.wait_ge(logit7[0], q + (TURNS + 2))
                    probabilities(g, 0)

                far_steps(act, step)

            @block.vector
            def _(dve):
                def step(g, w, q):
                    stage(g, 0)
                    ids = far_destinations(dve, g, w, q, far7)
                    build(g, 0, q + (TURNS + 1), w * WINDOW, ids, win_ids)
                    dve.wait_ge(summed7[0], q + (TURNS + 1))
                    dve.wait_ge(added7, 2 * q + ADDED0 + 2 * GROUPS)
                    for a in add_window(0, 2, w * WINDOW):
                        a.then_inc(added7, 1)

                far_steps(dve, step)

        end_phase()

        den, bsm, scaled, paused8 = (sem(n) for n in ("den", "bsm", "scaled", "paused8"))
        v8, var8, std8 = sem("v8"), sem("var8"), sem("std8")
        quot = [rows[0][:, s * CH:(s + 1) * CH] for s in range(2)]
        bns = WhhT[:, 0:6 * (NCH + 1)]
        mv = sb("mv", 2)
        col = sb("col", 4)
        maskc = rows[1][:, 0:CH].bitcast(I32)
        bigc = whot[0]
        inv = dst_terms
        pos = [hot[s][:, 0:CH] for s in range(2)]
        ex = [whot[s][:, 0:CH] for s in range(2)]
        el = [rows[0][:, s * CH:(s + 1) * CH] for s in range(2)]
        res = [rows[1][:, s * CH:(s + 1) * CH] for s in range(2)]
        neg_ready, exp_ready, elu_ready, turned, res_ready, out_done = (slot_sems(n) for n in (
            "neg_ready", "exp_ready", "elu_ready", "turned", "res_ready", "out_done"))

        with nc.Block() as block:
            @block.tensor
            def _(pe):
                for c in range(NCH + 1):
                    m = CH if c < NCH else CTAIL
                    if c >= 2:
                        pe.wait_ge(v8, 5 * (c - 2) + 3)
                    for k in range(2):
                        nc.tensor.matmul(bank[2 * (c % 2) + k][:, 0:m], ident[0:2, k:k + 1].broadcast_to([2, P]),
                                         side[0:2, c * CH:c * CH + m], start=True, stop=True).then_inc(den, 1)

            @block.vector
            def _(dve):
                nc.vector.memset(bigc[:, :], BIG).then_inc(bsm, 1)
                dve.wait_ge(bsm, 1)
                for c in range(NCH + 1):
                    m = CH if c < NCH else CTAIL
                    part = sums[:, c * CH:c * CH + m]
                    q = quot[c % 2][:, 0:m]
                    r = inv[:, c * CH:c * CH + m]
                    n = 5 * c
                    dve.wait_ge(den, 2 * c + 2)
                    nc.vector.tensor_scalar(q, bank[2 * (c % 2)][:, 0:m], 0.5, None, ALU.max).then_inc(v8, 1)
                    dve.wait_ge(v8, n + 1)
                    nc.vector.scalar_tensor_tensor(r, bank[2 * (c % 2) + 1][:, 0:m], BETA_EPS, q, ALU.add,
                                                   ALU.mult).then_inc(v8, 1)
                    dve.wait_ge(v8, n + 2)
                    nc.vector.reciprocal(r, r).then_inc(v8, 1)
                    dve.wait_ge(v8, n + 3)
                    nc.vector.tensor_tensor(part, part, r, ALU.mult).then_inc(v8, 1)
                    dve.wait_ge(v8, n + 4)
                    guard_inf(dve, part, maskc[:, 0:m], bigc[:, 0:m], scaled, 3 * c, paused8).then_inc(scaled, 1)
                    dve.wait_ge(scaled, 3 * c + 3)
                    nc.vector.bn_stats(bns[:, 6 * c:6 * c + 6], part).then_inc(v8, 1)
                n = 5 * (NCH + 1)
                dve.wait_ge(v8, n)
                nc.vector.bn_aggr(mv[:, :], bns).then_inc(var8, 1)
                dve.wait_ge(std8, 1)
                nc.vector.reciprocal(col[:, 1:2], col[:, 0:1]).then_inc(v8, 1)
                dve.wait_ge(v8, n + 1)
                nc.vector.tensor_tensor(col[:, 2:3], col[:, 1:2], gamma[:, :], ALU.mult).then_inc(v8, 1)
                dve.wait_ge(v8, n + 2)

            @block.scalar
            def _(act):
                act.wait_ge(var8, 1)
                nc.scalar.activation(col[:, 0:1], mv[:, 1:2], ACT.Sqrt, bias=eps[:, 0:1]).then_inc(std8, 1)

        with nc.Block() as block:
            def chunk(c):
                return sums[:, bass.ds(c * CH, CH)]

            @block.vector
            def _(dve):
                def first(c, s, m, n):
                    part = sums[:, bass.ds(c * CH, m)]
                    y = el[s][:, 0:m]
                    nc.vector.tensor_scalar(part, part, mv[:, 0:1], col[:, 2:3], ALU.subtract, ALU.mult).then_inc(neg_ready[s], 1)
                    dve.wait_ge(neg_ready[s], 4 * n + 1)
                    nc.vector.tensor_scalar(part, part, beta[:, 0:1], None, ALU.add).then_inc(neg_ready[s], 1)
                    dve.wait_ge(neg_ready[s], 4 * n + 2)
                    nc.vector.tensor_scalar(ex[s][:, 0:m], part, 0.0, None, ALU.min).then_inc(neg_ready[s], 1)
                    nc.vector.tensor_scalar(pos[s][:, 0:m], part, 0.0, None, ALU.max).then_inc(neg_ready[s], 1)
                    dve.wait_ge(exp_ready[s], n + 1)
                    dve.wait_ge(neg_ready[s], 4 * n + 4)
                    nc.vector.scalar_tensor_tensor(y, ex[s][:, 0:m], -1.0, pos[s][:, 0:m], ALU.add, ALU.add).then_inc(elu_ready[s], 1)

                def second(c, s, m, n):
                    dve.wait_ge(turned[s], n + 1)
                    for k in range(-(-m // P)):
                        w = min(P, m - k * P)
                        ins = nc.vector.tensor_tensor(res[s][0:w, k * D:(k + 1) * D], bank[s][0:w, k * D:(k + 1) * D],
                                                      nodes[0:w, bass.ds(c * CH + k * P, D)], ALU.add)
                    ins.then_inc(res_ready[s], 1)

                with dve.Fori(0, NCH // 2) as i:
                    for s in range(2):
                        first(2 * i + s, s, CH, i)
                        dve.wait_ge(out_done[s], (i + 1) * 16)
                        second(2 * i + s, s, CH, i)
                first(NCH, 0, CTAIL, NCH // 2)
                dve.wait_ge(out_done[0], (NCH // 2 + 1) * 16)
                second(NCH, 0, CTAIL, NCH // 2)

            @block.scalar
            def _(act):
                def one(s, m, n):
                    act.wait_ge(neg_ready[s], 4 * n + 3)
                    nc.scalar.activation(ex[s][:, 0:m], ex[s][:, 0:m], ACT.Exp).then_inc(exp_ready[s], 1)

                with act.Fori(0, NCH // 2) as i:
                    for s in range(2):
                        one(s, CH, i)
                one(0, CTAIL, NCH // 2)

            @block.tensor
            def _(pe):
                def one(s, m, n):
                    pe.wait_ge(elu_ready[s], n + 1)
                    for k in range(-(-m // P)):
                        w = min(P, m - k * P)
                        mm = nc.tensor.transpose(bank[s][0:w, k * P:(k + 1) * P], el[s][:, k * P:k * P + w], ident[:, :])
                    mm.then_inc(turned[s], 1)

                with pe.Fori(0, NCH // 2) as i:
                    for s in range(2):
                        one(s, CH, i)
                one(0, CTAIL, NCH // 2)

            @block.sync
            def _(sp):
                for s in range(2):
                    sp.sem_inc(out_done[s], 16)
                with sp.Fori(0, NCH // 2) as i:
                    for s in range(2):
                        sp.wait_ge(res_ready[s], i + 1)
                        sp.dma_start(out[bass.ds((2 * i + s) * CH, CH), :].rearrange("(k p) d -> p k d", p=P),
                                     res[s].rearrange("p (k d) -> p k d", d=D)).then_inc(out_done[s], 16)
                sp.wait_ge(res_ready[0], NCH // 2 + 1)
                for k in range(-(-CTAIL // P)):
                    w = min(P, CTAIL - k * P)
                    sp.dma_start(out[NCH * CH + k * P:NCH * CH + k * P + w, :], res[0][0:w, k * D:(k + 1) * D]
                                 ).then_inc(out_done[0], 16)
                sp.wait_ge(out_done[0], 16 * (NCH // 2 + 1 + -(-CTAIL // P)))
                sp.wait_ge(out_done[1], 16 * (NCH // 2 + 1))

        phase.close()


_INS = ["x", "src", "dst", "edge_type_9", "edge_weight", "L0_gnn_W_msg", "L0_gnn_b_msg", "L0_gnn_edge_embed",
        "L0_gnn_W_ih", "L0_gnn_W_hh", "L0_gnn_b_ih", "L0_gnn_b_hh", "L1_gnn_fc_w", "L1_gnn_fc_b",
        "L1_gnn_attn_w", "L1_gnn_attn_b", "L1_gnn_bn_gamma", "L1_gnn_bn_beta"]


def kernel(**inputs):
    import numpy as _np
    import concourse.bacc as _bacc
    from concourse import mybir as _mybir
    from concourse.bass_utils import run_bass_kernel_spmd as _run

    nc = _bacc.Bacc("TRN2", target_bir_lowering=False, num_devices=1)
    arrays, args = {}, []
    for name in _INS:
        a = _np.ascontiguousarray(inputs[name])
        arrays[f"in_{name}"] = a
        args.append(nc.dram_tensor(f"in_{name}", a.shape, _mybir.dt.from_np(a.dtype), kind="ExternalInput").ap())
    shape = inputs["x"].shape
    args.append(nc.dram_tensor("out_dram", shape, _mybir.dt.float32, kind="ExternalOutput").ap())
    gnn(nc, *args)
    r = _run(nc, [arrays], core_ids=[0])
    return r.results[0]["out_dram"]
```

```python
from contextlib import ExitStack

import numpy as np

import concourse.bass as bass
from concourse import mybir

F32 = mybir.dt.float32
BF16 = mybir.dt.bfloat16
I32 = mybir.dt.int32
U32 = mybir.dt.uint32
ALU = mybir.AluOpType
ACT = mybir.ActivationFunctionType
AX = mybir.AxisListType

P = 128
TILES = 8
GROUP = TILES * P
WINDOW = 64
SPAN = 8
PAD_DST = -20000.0
LN_EPS = 1e-5
BETA_EPS = 1e-6
BIG = 1e9
F32_MAX = float(np.finfo(np.float32).max)
TYPES = 9


def gnn(nc, x, src, dst, edge_type, edge_weight, W_msg, b_msg, edge_embed, W_ih, W_hh, b_ih, b_hh,
        fc_w, fc_b, attn_w, attn_b, bn_gamma, bn_beta, out):
    N, D = x.shape
    (E,) = src.shape
    NT = -(-N // P)
    NTAIL = N - (NT - 1) * P
    ROWS = NT * P
    BLOCKS = -(-E // (P * P))
    CHUNK = BLOCKS * P
    FULL, REST = E // CHUNK, E % CHUNK
    GROUPS = -(-E // GROUP)
    PAIRS = GROUPS // 2
    ECOLS = BLOCKS * P
    assert D == P and GROUPS == 2 * PAIRS and ECOLS >= (GROUPS + 2) * TILES and NT % 4 == 1
    TURNS = (GROUPS - 2) // 5
    EARLY = 2 * TURNS + 2
    assert GROUPS == EARLY + 3 * TURNS
    DENSE = 2 * TURNS
    KEYS = NT * SPAN
    UTILES = 2 * TILES
    assert DENSE * GROUP <= E and KEYS <= 512 and UTILES * SPAN == P
    WINS = -(-N // WINDOW)
    ACCN = -(-(N + WINDOW) // P) * P
    CH = 4 * P
    NCH = N // CH
    CTAIL = N - NCH * CH

    h_tab = nc.dram_tensor("h_tab", [ROWS, D], F32, kind="Internal").ap()
    z_tab = nc.dram_tensor("z_tab", [ROWS, D], F32, kind="Internal").ap()
    early = nc.dram_tensor("early", [EARLY * P, TILES * D], F32, kind="Internal").ap()
    lo_row = nc.dram_tensor("lo_row", [1, P * CHUNK], BF16, kind="Internal").ap()
    dst_tab = nc.dram_tensor("dst_tab", [P, CHUNK], F32, kind="Internal").ap()
    sig_tab = nc.dram_tensor("sig_tab", [P, ECOLS], F32, kind="Internal").ap()
    ad_row = nc.dram_tensor("ad_row", [1, ROWS], F32, kind="Internal").ap()

    with ExitStack() as ctx:
        def sb(name, cols, dt=F32, rows=P):
            return ctx.enter_context(nc.sbuf_tensor(name, [rows, cols], dt))

        phase = ExitStack()
        held = []

        def sem(name):
            held.append(phase.enter_context(nc.semaphore(name)))
            return held[-1]

        landed = [ctx.enter_context(nc.semaphore(f"landed{s}")) for s in range(3)]
        far_landed1 = ctx.enter_context(nc.semaphore("far_landed1"))
        far_landed7 = ctx.enter_context(nc.semaphore("far_landed7"))

        def end_phase():
            with nc.Block() as block:
                @block.sync
                def _(sp):
                    for s in held:
                        sp.sem_clear(s)
            phase.close()
            held.clear()

        bank = [ctx.enter_context(nc.psum_tensor(f"bank{i}", [P, 512], F32)) for i in range(8)]

        nodes = sb("nodes", NT * D)
        sums = sb("sums", ACCN)
        side = sb("side", ACCN)
        dst_terms = sb("dst_terms", ACCN)
        srcT = sb("srcT", ECOLS, U32)
        hiT = sb("hiT", ECOLS)
        relT = sb("relT", ECOLS)
        typeT = sb("typeT", ECOLS)
        sigT = sb("sigT", ECOLS)
        logits = sb("logits", 2 * ECOLS)
        logits3 = logits[:, :].rearrange("p (a t) -> p a t", a=2)
        dstC = sb("dstC", CHUNK)
        edgeC = [dst_terms[:, k * CHUNK:(k + 1) * CHUNK] for k in range(3)]
        scanC = [side[:, k * CHUNK:(k + 1) * CHUNK] for k in range(3)]

        rows = [sb(f"rows{s}", TILES * D) for s in range(3)] + [t[:, 0:TILES * D] for t in (typeT, hiT)]
        HW = TILES * WINDOW
        hots = sb("hots", 10 * HW)
        hot = [hots[:, s * HW:(s + 1) * HW] for s in range(5)]
        whot = [hots[:, (5 + s) * HW:(6 + s) * HW] for s in range(5)]
        idx = [sb(f"idx{s}", TILES, U32) for s in range(3)]
        base_i = sb("base_i", GROUPS + 4, I32, 1)
        base_turn = sb("base_turn", 5 * (TURNS + 1), I32, 1)
        base_b = sb("base_b", GROUPS)

        ident = sb("ident", P)
        ones = sb("ones", P)
        iota = sb("iota", P)
        pidx_i = sb("pidx_i", 1, I32)
        pidx = sb("pidx", 1)
        eps = sb("eps", 1)
        big = sb("big", P)
        iota_key = sb("iota_key", KEYS)
        expand = sb("expand", P, F32, UTILES)
        unit_col = sb("unit_col", TURNS)
        col_base = sb("col_base", 2)
        far_group = sb("far_group", GROUPS, I32, 1)
        far_rank = sb("far_rank", GROUPS, I32, 1)
        far_any = sb("far_any", 1, I32, 1)
        far_ids = [sb(f"far_ids{k}", TILES) for k in range(2)]
        win_ids = sb("win_ids", WINDOW)
        win_base = sb("win_base", WINS)

        wraw = [rows[2][:, i * D:(i + 1) * D] for i in range(7)]
        WmT = sb("WmT", D)
        WihT = sb("WihT", 3 * D)
        WhhT = sb("WhhT", 3 * D)
        emb = sb("emb", D, F32, TYPES)
        bmsg = sb("bmsg", D, F32, TYPES)
        bias_ih, bias_hh = hot[2][0:1, 0:3 * D], hot[3][0:1, 0:3 * D]
        bias = sb("bias", 4 * D, F32, 1)
        fcw = sb("fcw", D)
        fcb = sb("fcb", D, F32, 1)
        wsd = sb("wsd", 2 * D)
        battn = sb("battn", 1)
        gamma = sb("gamma", 1)
        beta = sb("beta", 1)

        stats = sb("stats", NT * 6)
        st = sb("st", 8 * NT)
        rstd = sb("rstd", NT)
        shift = sb("shift", NT)
        terms = sb("terms", 2 * NT)
        as_tab, ad_tab = terms[:, 0:NT], terms[:, NT:2 * NT]
        dots = [sb(f"dots{s}", 2) for s in range(4)]
        adT = sb("adT", P, F32, NT)

        def dram_tile(tab, t):
            return tab[bass.ds(t * P, P), :]

        consts, ld_x, ld_e, ld_w, zeroed, padded, blank = (sem(n) for n in (
            "consts", "ld_x", "ld_e", "ld_w", "zeroed", "padded", "blank"))
        v1, a1, p1, put_by1, units_in = (sem(n) for n in ("v1", "a1", "p1", "put_by1", "units_in"))
        h_head, h_split = sem("h_head"), sem("h_split")
        h_made, lo_stored = sem("h_made"), sem("lo_stored")
        h_stored = [sem(f"h_stored{i}") for i in range(2)]
        src_i = edgeC[0].bitcast(I32)
        raw_i = [edgeC[1].bitcast(I32), edgeC[2].bitcast(I32)]
        srcC, typeC, sigC = scanC
        lo_i = logits[:, 0:CHUNK].bitcast(I32)
        PER = -(-BLOCKS // 4)
        DCOLS = DENSE * TILES
        key = hiT[:, 0:DCOLS]
        key_i = sums[:, 0:KEYS].bitcast(I32)
        in_tile, in_span, near, pair_key = (sums[:, 512 + k * DCOLS:512 + (k + 1) * DCOLS] for k in range(4))
        far_edge = sums[:, 512 + 4 * DCOLS:512 + 4 * DCOLS + GROUPS * TILES]
        far_in = sums[:, ACCN - GROUPS:ACCN]
        ones_row = sums[0:1, ACCN - 2 * GROUPS:ACCN - GROUPS]
        base_f = sums[0:1, ACCN - 3 * GROUPS:ACCN - 2 * GROUPS]
        far_count = sums[0:1, ACCN - 4 * GROUPS:ACCN - 3 * GROUPS]
        iota_i = sums[:, ACCN - 4 * GROUPS - P:ACCN - 4 * GROUPS].bitcast(I32)
        units = sums[0:UTILES, ACCN - 4 * GROUPS - P - 4 * TURNS:ACCN - 4 * GROUPS - P]
        tile_base_i = units[:, 0:2 * TURNS].bitcast(I32)
        tile_base = units[:, 2 * TURNS:4 * TURNS]
        assert 512 + 4 * DCOLS + (TILES + 4) * GROUPS + P + 4 * TURNS <= ACCN
        HEADS = 32
        parts_at = [(dst_terms[:, :].bitcast(BF16), 0), (logits[:, :].bitcast(BF16), HEADS)]

        def parts(t, m):
            mem, first = parts_at[t >= HEADS]
            return mem[:, (t - first) * 3 * D:(t - first + m) * 3 * D]

        def part_view(t, m, k):
            return parts(t, m).rearrange("p (t k d) -> p k t d", k=3, d=D)[:, k]

        rest = [sums[:, k * TILES * D:(k + 1) * TILES * D] for k in range(2)]
        lo_b = logits[:, CHUNK:2 * CHUNK].bitcast(BF16)[:, 0:CHUNK]
        hbuf = [rows[0], rows[1]]
        var1, std1, scale1 = sem("var1"), sem("std1"), sem("scale1")
        chunk_loads = [(src, src_i), (dst, raw_i[0]), (edge_type, raw_i[1]), (edge_weight, sigC)]

        def norm_scalars(eng, chain, n, var_ready, std_ready, scale_ready):
            s = stats[:, :].rearrange("p (t k) -> p k t", k=6)
            mean2, diff, m2, diff2, part, var, std = (st[:, k * NT:(k + 1) * NT] for k in range(7))
            nc.vector.tensor_tensor(mean2, s[:, 1, :], s[:, 4, :], ALU.add).then_inc(chain, 1)
            nc.vector.tensor_tensor(diff, s[:, 1, :], s[:, 4, :], ALU.subtract).then_inc(chain, 1)
            nc.vector.tensor_tensor(m2, s[:, 2, :], s[:, 5, :], ALU.add).then_inc(chain, 1)
            eng.wait_ge(chain, n + 3)
            nc.vector.tensor_tensor(diff2, diff, diff, ALU.mult).then_inc(chain, 1)
            nc.vector.tensor_scalar(part, m2, 1.0 / D, LN_EPS, ALU.mult, ALU.add).then_inc(chain, 1)
            eng.wait_ge(chain, n + 5)
            nc.vector.scalar_tensor_tensor(var, diff2, 0.25, part, ALU.mult, ALU.add).then_inc(var_ready, 1)
            eng.wait_ge(std_ready, 1)
            nc.vector.reciprocal(rstd[:, :], std).then_inc(chain, 1)
            eng.wait_ge(chain, n + 6)
            nc.vector.scalar_tensor_tensor(shift[:, :], mean2, -0.5, rstd[:, :], ALU.mult,
                                           ALU.mult).then_inc(scale_ready, 1)

        with nc.Block() as block:
            @block.sync
            def _(sp):
                sp.wait_ge(padded, 5)
                for a, to in chunk_loads:
                    a2 = a[0:FULL * CHUNK].rearrange("(p k) -> p k", k=CHUNK)
                    sp.dma_start(to[0:FULL, :], a2).then_inc(ld_e, 16)
                    sp.dma_start(to[FULL:FULL + 1, 0:REST],
                                 a[FULL * CHUNK:E].rearrange("(p k) -> p k", p=1)).then_inc(ld_e, 16)
                sp.dma_start(base_i[0:1, 0:GROUPS],
                             dst[0:E].rearrange("(p k) -> p k", p=1)[:, 0:(GROUPS - 1) * GROUP + 1:GROUP],
                             allow_slow_non_contiguous=True).then_inc(ld_e, 16)
                in_units = dst[0:DENSE * GROUP]
                sp.dma_start(tile_base_i[:, 0:TURNS], in_units.rearrange("(u k e) -> k u e", k=UTILES, e=P)[:, :, 0],
                             allow_slow_non_contiguous=True).then_inc(units_in, 16)
                for k in range(2):
                    sp.dma_start(tile_base_i[k * TILES:(k + 1) * TILES, TURNS:2 * TURNS],
                                 in_units.rearrange("(u k e) -> k u e", k=2, e=GROUP)[k:k + 1, :, 0].broadcast_to([TILES, TURNS]),
                                 allow_slow_non_contiguous=True).then_inc(units_in, 16)
                sp.dma_start(wraw[0], W_msg).then_inc(ld_w, 16)
                for k in range(3):
                    sp.dma_start(wraw[1 + k], W_ih[k * D:(k + 1) * D, :]).then_inc(ld_w, 16)
                    sp.dma_start(wraw[4 + k], W_hh[k * D:(k + 1) * D, :]).then_inc(ld_w, 16)
                sp.dma_start(emb[:, :], edge_embed).then_inc(ld_w, 16)
                sp.dma_start(bmsg[:, :], b_msg.rearrange("(a d) -> a d", a=1).broadcast_to([TYPES, D])).then_inc(ld_w, 16)
                sp.dma_start(bias_ih, b_ih.rearrange("(a d) -> a d", a=1)).then_inc(ld_w, 16)
                sp.dma_start(bias_hh, b_hh.rearrange("(a d) -> a d", a=1)).then_inc(ld_w, 16)
                sp.dma_start(fcw[:, :], fc_w).then_inc(ld_w, 16)
                sp.dma_start(fcb[:, :], fc_b.rearrange("(a d) -> a d", a=1)).then_inc(ld_w, 16)
                sp.dma_start(wsd[:, :], attn_w.rearrange("k a -> a k").broadcast_to([P, 2 * D])).then_inc(ld_w, 16)
                sp.dma_start(battn[:, :], attn_b.rearrange("(a d) -> a d", a=1).broadcast_to([P, 1])).then_inc(ld_w, 16)
                sp.dma_start(gamma[:, :], bn_gamma.rearrange("(d a) -> d a", a=1)).then_inc(ld_w, 16)
                sp.dma_start(beta[:, :], bn_beta.rearrange("(d a) -> d a", a=1)).then_inc(ld_w, 16)
                sp.wait_ge(v1, 2)
                sp.dma_start(lo_row.rearrange("a (p k) -> (a p) k", p=P), lo_b).then_inc(lo_stored, 16)
                sp.wait_ge(v1, 4 + 4 * PER)
                sp.dma_start(dst_tab, dstC[:, :]).then_inc(put_by1, 16)
                sp.dma_start(sig_tab, sigT[:, :]).then_inc(put_by1, 16)
                for b in range(NT // 8):
                    sp.wait_ge(h_made, 8 * (b + 1))
                    sp.dma_start(h_tab[b * 8 * P:(b + 1) * 8 * P, :].rearrange("(t p) d -> p t d", p=P),
                                 hbuf[b % 2][:, :].rearrange("p (t d) -> p t d", d=D)).then_inc(h_stored[b % 2], 16)
                sp.wait_ge(h_made, NT)
                sp.dma_start(h_tab[(NT - 1) * P:NT * P, :], hbuf[0][:, 0:D]).then_inc(h_stored[0], 16)
                sp.wait_ge(h_stored[0], 16 * (NT // 16 + 1))
                sp.wait_ge(h_stored[1], 16 * (NT // 16))
                sp.wait_ge(lo_stored, 16)
                sp.wait_ge(put_by1, 32)
                sp.wait_ge(ld_w, 16 * 17)
                sp.wait_ge(ld_e, 16 * 9)

            @block.gpsimd
            def _(pool):
                nc.gpsimd.memset(src_i, 0).then_inc(padded, 1)
                nc.gpsimd.memset(raw_i[0], int(PAD_DST)).then_inc(padded, 1)
                nc.gpsimd.memset(raw_i[1], 0).then_inc(padded, 1)
                nc.gpsimd.memset(sigC, 0.0).then_inc(padded, 1)
                nc.gpsimd.memset(ident[:, :], 0.0).then_inc(blank, 1)
                nc.gpsimd.memset(ones[:, :], 1.0).then_inc(consts, 1)
                nc.gpsimd.memset(eps[:, :], LN_EPS).then_inc(consts, 1)
                nc.gpsimd.memset(big[:, :], BIG).then_inc(consts, 1)
                nc.gpsimd.iota(iota_i[:, :], [[1, P]], base=0, channel_multiplier=0).then_inc(consts, 1)
                nc.gpsimd.iota(pidx_i[:, :], [[0, 1]], base=0, channel_multiplier=1).then_inc(consts, 1)
                pool.wait_ge(blank, 1)
                nc.gpsimd.affine_select(out=ident[:, :], in_=ident[:, :], compare_op=ALU.not_equal, fill=1.0,
                                        base=0, pattern=[[-1, P]], channel_multiplier=1).then_inc(consts, 1)
                pool.wait_ge(consts, 6)
                nc.gpsimd.tensor_copy(iota[:, :], iota_i[:, :]).then_inc(consts, 1)
                nc.gpsimd.tensor_scalar(win_base[:, :], iota_i[:, 0:WINS], float(WINDOW), 1.0, ALU.mult, ALU.add).then_inc(consts, 1)
                nc.gpsimd.tensor_copy(pidx[:, :], pidx_i[:, :]).then_inc(consts, 1)
                nc.gpsimd.memset(expand[:, :], 1.0).then_inc(blank, 1)
                pool.wait_ge(blank, 2)
                nc.gpsimd.affine_select(out=expand[:, :], in_=expand[:, :], compare_op=ALU.is_ge, fill=0.0,
                                        base=0, pattern=[[1, P]], channel_multiplier=-SPAN).then_inc(blank, 1)
                pool.wait_ge(blank, 3)
                nc.gpsimd.affine_select(out=expand[:, :], in_=expand[:, :], compare_op=ALU.is_ge, fill=0.0,
                                        base=SPAN - 1, pattern=[[-1, P]], channel_multiplier=SPAN).then_inc(consts, 1)
                nc.gpsimd.iota(key_i, [[1, KEYS]], base=1, channel_multiplier=0).then_inc(blank, 1)
                pool.wait_ge(blank, 4)
                nc.gpsimd.tensor_copy(iota_key[:, :], key_i).then_inc(consts, 1)

            @block.scalar
            def _(act):
                act.wait_ge(zeroed, 1)
                act.dma_start(nodes[:, 0:(NT - 1) * D].rearrange("p (t d) -> p t d", d=D),
                              x[0:(NT - 1) * P, :].rearrange("(t p) d -> p t d", p=P)).then_inc(ld_x, 16)
                act.dma_start(nodes[0:NTAIL, (NT - 1) * D:NT * D], x[(NT - 1) * P:N, :]).then_inc(ld_x, 16)
                act.wait_ge(ld_e, 16 * 9)
                nc.scalar.activation(typeC, raw_i[1], ACT.Copy).then_inc(a1, 1)
                act.wait_ge(var1, 1)
                nc.scalar.activation(st[:, 6 * NT:7 * NT], st[:, 5 * NT:6 * NT], ACT.Sqrt).then_inc(std1, 1)
                act.wait_ge(scale1, 1)
                for b in range(NT // 8 + 1):
                    if b >= 2:
                        act.wait_ge(h_stored[b % 2], 16 * (b // 2))
                        act.wait_ge(h_split, 3 * (b - 1))
                    m = 8 if b < NT // 8 else 1
                    for k in range(m):
                        t = 8 * b + k
                        nc.scalar.activation(hbuf[b % 2][:, k * D:(k + 1) * D], nodes[:, t * D:(t + 1) * D],
                                             ACT.Relu, bias=shift[:, t:t + 1],
                                             scale=rstd[:, t:t + 1]).then_inc(h_made, 1)
                    act.wait_ge(h_made, 8 * b + m)
                    nc.scalar.activation(part_view(8 * b, m, 0), hbuf[b % 2][:, 0:m * D].rearrange("p (t d) -> p t d", d=D),
                                         ACT.Copy).then_inc(h_head, 1)

            @block.tensor
            def _(pe):
                pe.wait_ge(consts, 11)
                k = 0
                for n, c in enumerate((srcC, dstC[:, :], typeC, sigC)):
                    if n == 0:
                        pe.wait_ge(v1, 4)
                    if n == 2:
                        pe.wait_ge(a1, 1)
                    for b in range(0, BLOCKS, 4):
                        if k >= 8:
                            pe.wait_ge(v1, 4 + k - 7)
                        for q in range(b, min(b + 4, BLOCKS)):
                            mm = nc.tensor.transpose(bank[k % 8][:, (q - b) * P:(q - b + 1) * P],
                                                     c[:, q * P:(q + 1) * P], ident[:, :])
                        mm.then_inc(p1, 1)
                        k += 1
                pe.wait_ge(v1, 5 + k)
                nc.tensor.matmul(bank[0][:, 0:GROUPS], ones[0:1, :], base_f[:, :], start=True, stop=True).then_inc(p1, 1)
                pe.wait_ge(v1, 5 + k + 2)
                for b in range(0, DCOLS, 512):
                    m = min(512, DCOLS - b)
                    mm = nc.tensor.matmul(bank[3 + b // 512][:, 0:m], ones[0:1, :], relT[0:1, b:b + m], start=True, stop=True)
                mm.then_inc(p1, 1)
                pe.wait_ge(v1, 5 + k + 6)
                nc.tensor.matmul(bank[5][:, 0:TURNS], expand[:, :], tile_base[:, 0:TURNS], start=True, stop=True).then_inc(p1, 1)
                pe.wait_ge(v1, 5 + k + 17)
                nc.tensor.matmul(bank[6][0:1, 0:GROUPS], ones[:, 0:1], far_in, start=True, stop=True).then_inc(p1, 1)
                pe.wait_ge(ld_w, 16 * 17)
                for i in range(7):
                    mm = nc.tensor.transpose(bank[1 + i // 4][:, (i % 4) * P:(i % 4 + 1) * P], wraw[i], ident[:, :])
                mm.then_inc(p1, 1)

            @block.vector
            def _(dve):
                nc.vector.memset(nodes[:, (NT - 1) * D:NT * D], 0.0).then_inc(zeroed, 1)
                nc.vector.memset(base_i[:, :], 0).then_inc(padded, 1)
                dve.wait_ge(ld_e, 16 * 9)
                nc.vector.tensor_scalar(lo_i, src_i, P - 1, None, ALU.bitwise_and).then_inc(v1, 1)
                dve.wait_ge(v1, 1)
                nc.vector.tensor_copy(lo_b, lo_i).then_inc(v1, 1)
                nc.vector.tensor_copy(srcC, src_i).then_inc(v1, 1)
                nc.vector.tensor_copy(dstC[:, :], raw_i[0]).then_inc(v1, 1)
                for k in range(4 * PER):
                    to = (srcT, relT, typeT, sigT)[k // PER]
                    b = 4 * (k % PER)
                    m = min(4, BLOCKS - b)
                    dve.wait_ge(p1, k + 1)
                    view = to[:, :].rearrange("j (p b) -> j b p", b=BLOCKS)[:, b:b + m, :]
                    nc.vector.tensor_copy(view, bank[k % 8][:, 0:m * P].rearrange("j (b p) -> j b p", b=m)).then_inc(v1, 1)
                n = 4 + 4 * PER
                nc.vector.tensor_copy(base_f[:, :], base_i[:, 0:GROUPS]).then_inc(v1, 1)
                n += 1
                dve.wait_ge(p1, 4 * PER + 1)
                nc.vector.tensor_copy(base_b[:, :], bank[0][:, 0:GROUPS]).then_inc(v1, 1)
                dve.wait_ge(v1, n + 1)
                rel3 = relT[:, 0:GROUPS * TILES].rearrange("p (g j) -> p g j", j=TILES)
                nc.vector.tensor_tensor(rel3, rel3, base_b[:, :].unsqueeze(2).broadcast_to([P, GROUPS, TILES]),
                                        ALU.subtract).then_inc(v1, 1)
                nc.vector.tensor_scalar(typeT[:, :], typeT[:, :], 0.0, float(TYPES - 1), ALU.max, ALU.min).then_inc(v1, 1)
                nc.vector.tensor_scalar(lo_i, srcT[:, :].bitcast(I32), 7, None, ALU.logical_shift_right).then_inc(v1, 1)
                dve.wait_ge(lo_stored, 16)
                dve.wait_ge(v1, n + 4)
                nc.vector.tensor_copy(hiT[:, :], lo_i).then_inc(v1, 1)
                dve.wait_ge(units_in, 48)
                nc.vector.tensor_tensor(tile_base[:, 0:TURNS], tile_base_i[:, 0:TURNS], tile_base_i[:, TURNS:2 * TURNS],
                                        ALU.subtract).then_inc(v1, 1)
                nc.vector.tensor_scalar(col_base[:, 0:1].bitcast(I32), pidx_i[:, :], (SPAN - 1) | WINDOW, None,
                                        ALU.bitwise_and).then_inc(v1, 1)
                dve.wait_ge(v1, n + 7)
                nc.vector.tensor_copy(col_base[:, 1:2], col_base[:, 0:1].bitcast(I32)).then_inc(v1, 1)
                dve.wait_ge(p1, 4 * PER + 2)
                for b in range(0, DCOLS, 512):
                    m = min(512, DCOLS - b)
                    nc.vector.tensor_tensor(in_tile[:, b:b + m], relT[:, b:b + m], bank[3 + b // 512][:, 0:m],
                                            ALU.subtract).then_inc(v1, 1)
                assert DCOLS > 512 and DCOLS <= 1024
                dve.wait_ge(v1, n + 10)
                nc.vector.tensor_scalar(in_span, in_tile, float(SPAN), None, ALU.is_lt).then_inc(v1, 1)
                nc.vector.scalar_tensor_tensor(pair_key, hiT[:, 0:DCOLS], float(SPAN), in_tile, ALU.mult, ALU.add).then_inc(v1, 1)
                dve.wait_ge(v1, n + 12)
                nc.vector.scalar_tensor_tensor(near, relT[:, 0:DCOLS], float(WINDOW), in_span, ALU.is_lt, ALU.mult).then_inc(v1, 1)
                dve.wait_ge(v1, n + 13)
                nc.vector.scalar_tensor_tensor(key, pair_key, 1.0, near, ALU.add, ALU.mult).then_inc(v1, 1)
                nc.vector.tensor_scalar(far_edge[:, DCOLS:], relT[:, DCOLS:GROUPS * TILES], float(WINDOW), None,
                                        ALU.is_ge).then_inc(v1, 1)
                dve.wait_ge(v1, n + 15)
                nc.vector.tensor_scalar(far_edge[:, 0:DCOLS], key, 0.0, None, ALU.is_equal).then_inc(v1, 1)
                dve.wait_ge(v1, n + 16)
                nc.vector.tensor_reduce(far_in, far_edge.rearrange("p (g j) -> p g j", j=TILES), AX.X, ALU.max).then_inc(v1, 1)
                n += 17
                dve.wait_ge(p1, 4 * PER + 3)
                nc.vector.tensor_scalar(unit_col[:, :], bank[5][:, 0:TURNS], col_base[:, 1:2], None, ALU.add).then_inc(v1, 1)
                nc.vector.memset(ones_row, 1.0).then_inc(v1, 1)
                dve.wait_ge(p1, 4 * PER + 4)
                nc.vector.tensor_scalar(far_group[:, :], bank[6][0:1, 0:GROUPS], 1.0, None, ALU.min).then_inc(v1, 1)
                dve.wait_ge(v1, n + 3)
                nc.vector.tensor_reduce(far_any[:, :], far_group[:, :], AX.X, ALU.max).then_inc(v1, 1)
                nc.vector.tensor_tensor_scan(far_count[:, :], ones_row, far_group[:, :], 0.0, ALU.mult, ALU.add).then_inc(v1, 1)
                dve.wait_ge(v1, n + 5)
                nc.vector.tensor_tensor(far_rank[:, :], far_count[:, :], far_group[:, :], ALU.subtract).then_inc(v1, 1)
                n += 6
                dve.wait_ge(p1, 4 * PER + 5)
                nc.vector.tensor_copy(WmT[:, :], bank[1][:, 0:D]).then_inc(v1, 1)
                nc.vector.tensor_copy(WihT[:, :], bank[1][:, D:4 * D]).then_inc(v1, 1)
                nc.vector.tensor_copy(WhhT[:, :], bank[2][:, 0:3 * D]).then_inc(v1, 1)
                nc.vector.tensor_tensor(emb[:, :], emb[:, :], bmsg[:, :], ALU.add).then_inc(v1, 1)
                nc.vector.tensor_tensor(bias[:, 0:2 * D], bias_ih[:, 0:2 * D], bias_hh[:, 0:2 * D], ALU.add).then_inc(v1, 1)
                nc.vector.tensor_copy(bias[:, 2 * D:3 * D], bias_ih[:, 2 * D:3 * D]).then_inc(v1, 1)
                nc.vector.tensor_copy(bias[:, 3 * D:4 * D], bias_hh[:, 2 * D:3 * D]).then_inc(v1, 1)
                n += 7
                dve.wait_ge(ld_x, 32)
                with dve.Fori(0, NT) as t:
                    nc.vector.bn_stats(stats[:, bass.ds(t * 6, 6)], nodes[:, bass.ds(t * D, D)]).then_inc(v1, 1)
                n += NT
                dve.wait_ge(v1, n)
                norm_scalars(dve, v1, n, var1, std1, scale1)
                for b in range(NT // 8 + 1):
                    m = 8 if b < NT // 8 else 1
                    left = rest[b % 2][:, 0:m * D].rearrange("p (t d) -> p t d", d=D)
                    dve.wait_ge(h_head, b + 1)
                    nc.vector.tensor_tensor(left, hbuf[b % 2][:, 0:m * D].rearrange("p (t d) -> p t d", d=D),
                                            part_view(8 * b, m, 0), ALU.subtract).then_inc(h_split, 1)
                    dve.wait_ge(h_split, 3 * b + 1)
                    nc.vector.tensor_copy(part_view(8 * b, m, 1), left).then_inc(h_split, 1)
                    dve.wait_ge(h_split, 3 * b + 2)
                    nc.vector.tensor_tensor(part_view(8 * b, m, 2), left, part_view(8 * b, m, 1), ALU.subtract).then_inc(h_split, 1)

        end_phase()

        def slot_sems(name):
            return [sem(f"{name}{s}") for s in range(2)]

        def onehot(to, rel, ids=iota):
            k = to.shape[1] // TILES
            return nc.vector.tensor_tensor(to.rearrange("p (j w) -> p j w", j=TILES),
                                           rel.unsqueeze(2).broadcast_to([P, TILES, k]),
                                           ids[:, 0:k].unsqueeze(1).broadcast_to([P, TILES, k]), ALU.is_equal)

        def columns(t, g):
            return t[:, bass.ds(g * TILES, TILES)]

        def gather(table, s):
            for j in range(TILES):
                yield nc.gpsimd.indirect_dma_start(rows[s][:, j * D:(j + 1) * D], None, table,
                                                   bass.IndirectOffsetOnAxis(ap=idx[s][:, j:j + 1], axis=0))

        def sum_tiles(s, weighted, extra, m, plain):
            for lhs, k, by, c in ((rows[s], D, weighted, 0), (extra, m, plain, WINDOW)):
                for j in range(TILES):
                    mm = nc.tensor.matmul(bank[s][0:k, c:c + WINDOW], lhs[:, j * k:(j + 1) * k],
                                          by[:, j * WINDOW:(j + 1) * WINDOW], start=j == 0, stop=j == TILES - 1)
            return mm

        def add_window(s, m, at, main=0, other=WINDOW):
            to, to2 = sums[:, bass.ds(at, WINDOW)], side[0:m, bass.ds(at, WINDOW)]
            yield nc.vector.tensor_tensor(to, to, bank[s][:, main:main + WINDOW], ALU.add)
            yield nc.vector.tensor_tensor(to2, to2, bank[s][0:m, other:other + WINDOW], ALU.add)

        def far_steps(eng, step, first=0, end=GROUPS):
            with eng.If(eng.value_load(far_any[0:1, 0:1], min_val=0, max_val=1) > 0):
                with eng.Fori(first, end) as g:
                    with eng.If(eng.value_load(far_group[0:1, bass.ds(g, 1)], min_val=0, max_val=1) > 0):
                        rank = eng.value_load(far_rank[0:1, bass.ds(g, 1)], min_val=0, max_val=GROUPS)
                        with eng.Fori(0, WINS) as w:
                            step(g, w, rank * WINS + w)
                    eng.nop()
                eng.nop()
            eng.nop()

        def far_destinations(dve, g, w, q, done, dense=False):
            n = 4 * q
            rel = columns(relT, g)
            if dense:
                nc.vector.tensor_scalar(far_ids[0][:, :], columns(key, g), 0.0, None, ALU.is_equal).then_inc(done, 1)
            else:
                nc.vector.tensor_scalar(far_ids[0][:, :], rel, float(WINDOW), None, ALU.is_ge).then_inc(done, 1)
            nc.vector.tensor_scalar(far_ids[1][:, :], rel, base_b[:, bass.ds(g, 1)], 1.0, ALU.add, ALU.add).then_inc(done, 1)
            dve.wait_ge(done, n + 2)
            nc.vector.tensor_tensor(far_ids[1][:, :], far_ids[1][:, :], far_ids[0][:, :], ALU.mult).then_inc(done, 1)
            nc.vector.tensor_scalar(win_ids[:, :], iota[:, 0:WINDOW], win_base[:, bass.ds(w, 1)], None, ALU.add).then_inc(done, 1)
            dve.wait_ge(done, n + 4)
            return far_ids[1][:, :]

        CROWD = 3
        KEYBUF = 4
        AHEAD = DCOLS + KEYBUF
        lo_of = dstC[:, 0:AHEAD]
        key_hot = [dstC[:, AHEAD + k * KEYS // 2:AHEAD + (k + 1) * KEYS // 2].bitcast(BF16) for k in range(KEYBUF)]
        to_window = dstC[:, AHEAD + KEYBUF * KEYS // 2:AHEAD + KEYBUF * KEYS // 2 + P]
        narrow = [sigT[:, s * HW // 2:(s + 1) * HW // 2].bitcast(BF16) for s in range(3)]
        unit_hot = sigT[:, 3 * HW // 2:5 * HW // 2].bitcast(BF16)
        unit_sums = sigT[:, 5 * HW // 2:5 * HW // 2 + 3 * D]
        spare = hots[:, 3 * HW:10 * HW]
        counts = spare[:, 0:NT * P // 2].bitcast(BF16)
        lo_hot1 = [spare[:, (NT + k) * P // 2:(NT + k + 1) * P // 2].bitcast(BF16) for k in range(KEYBUF)]
        small_at = (NT + KEYBUF) * P // 2
        thot = [spare[:, small_at + s * TILES * TYPES // 2:small_at + (s + 1) * TILES * TYPES // 2].bitcast(BF16) for s in range(3)]
        unit_types = spare[:, small_at + 3 * TILES * TYPES // 2:small_at + 5 * TILES * TYPES // 2].bitcast(BF16)
        assert small_at + 5 * TILES * TYPES // 2 <= 7 * HW
        low_i = counts.bitcast(I32)[:, 0:AHEAD]
        count_bank, unit_bank, window_bank = bank[3:3 + CROWD], bank[6], bank[7]

        staged1, hot1, narrow1, summed1 = ([sem(f"{n}{s}") for s in range(3)] for n in ("staged1", "hot1", "narrow1", "summed1"))
        issued1 = sem("issued1")
        added1 = sem("added1")
        low1 = sem("low1")
        table1, tile_hot, counted, kept, unit_made, unit_raw, unit_kept, unit_done = (sem(n) for n in (
            "table1", "tile_hot", "counted", "kept", "unit_made", "unit_raw", "unit_kept", "unit_done"))

        def bases(dve, regs, i):
            dve.reg_load(regs, base_turn[0:1, bass.ds(i * 5, len(regs))])
            return [dve.snap(r, min_val=0, max_val=N - 1) for r in regs]

        def gathered(s, i):
            return DENSE + 3 * i + s

        with nc.Block() as block:
            @block.gpsimd
            def _(pool):
                def group(s, i):
                    pool.wait_ge(staged1[s], i + 1)
                    pool.sem_inc(issued1)
                    for d in gather(h_tab, s):
                        d.then_inc(landed[s], 16)

                with pool.Fori(0, TURNS) as i:
                    for s in range(3):
                        group(s, i)
                for s in range(2):
                    group(s, TURNS)

            @block.tensor
            def _(pe):
                def group(s, i):
                    pe.wait_ge(hot1[s], 2 * i + 2)
                    pe.wait_ge(narrow1[s], i + 1)
                    pe.wait_ge(landed[s], (i + 1) * (16 * TILES))
                    sum_tiles(s, hot[s], thot[s], TYPES, narrow[s]).then_inc(summed1[s], 1)

                def count(i, j):
                    pe.wait_ge(tile_hot, (i * UTILES + (j + 1)) * 2)
                    pe.wait_ge(kept, i * UTILES + (j + 1 if j >= CROWD else CROWD))
                    nc.tensor.matmul(count_bank[j % CROWD][:, 0:KEYS], lo_hot1[j % KEYBUF], key_hot[j % KEYBUF],
                                     start=True, stop=True).then_inc(counted, 1)

                def unit(i):
                    pe.wait_ge(kept, i * UTILES + (UTILES + CROWD))
                    for t in range(NT):
                        mm = nc.tensor.matmul(unit_bank[:, 0:3 * D], counts[:, t * P:(t + 1) * P], parts(t, 1),
                                              start=t == 0, stop=t == NT - 1)
                    mm.then_inc(unit_raw, 1)
                    pe.wait_ge(unit_made, (i + 1) * 3)
                    for g in range(2):
                        for j in range(g * TILES, (g + 1) * TILES):
                            nc.tensor.matmul(window_bank[0:TYPES, P + g * WINDOW:P + (g + 1) * WINDOW],
                                             unit_types[:, j * TYPES:(j + 1) * TYPES], unit_hot[:, j * WINDOW:(j + 1) * WINDOW],
                                             start=j == g * TILES, stop=j == (g + 1) * TILES - 1)
                    pe.wait_ge(unit_kept, i + 1)
                    for k in range(3):
                        mm = nc.tensor.matmul(window_bank[:, 0:P], unit_sums[:, k * D:(k + 1) * D], to_window,
                                              start=k == 0, stop=k == 2)
                    mm.then_inc(unit_done, 1)

                pe.sem_inc(counted, KEYBUF)
                with pe.Fori(0, TURNS) as i:
                    for s in range(3):
                        group(s, i)
                        if s < 2:
                            for j in range(s * TILES, (s + 1) * TILES):
                                count(i, j)
                    unit(i)
                for s in range(2):
                    group(s, TURNS)

            @block.scalar
            def _(act):
                def narrow_copy(s, i):
                    act.wait_ge(hot1[s], 2 * i + 1)
                    nc.scalar.activation(narrow[s], hot[s], ACT.Copy).then_inc(narrow1[s], 1)

                by_tile = counts.rearrange("p (t c) -> p t c", c=P)
                for s in range(3):
                    narrow_copy(s, 0)
                act.sem_inc(kept, CROWD)
                act.sem_inc(unit_raw)
                with act.Fori(0, TURNS) as i:
                    for j in range(UTILES):
                        act.wait_ge(counted, i * UTILES + (j + 1 + KEYBUF))
                        if j == 0:
                            act.wait_ge(unit_raw, i + 1)
                        nc.scalar.activation(by_tile[:, :, j * SPAN:(j + 1) * SPAN],
                                             count_bank[j % CROWD][:, 0:KEYS].rearrange("p (t w) -> p t w", w=SPAN),
                                             ACT.Copy).then_inc(kept, 1)
                        if j == TILES - 1:
                            narrow_copy(0, i + 1)
                    narrow_copy(1, i + 1)
                    act.wait_ge(unit_raw, i + 2)
                    nc.scalar.activation(unit_sums, unit_bank[:, 0:3 * D], ACT.Copy).then_inc(unit_kept, 1)
                    narrow_copy(2, i + 1)

            @block.vector
            def _(dve):
                def stage(g, s):
                    nc.vector.tensor_copy(idx[s][:, :], columns(srcT, g)).then_inc(staged1[s], 1)

                def build(g, s):
                    onehot(hot[s], columns(relT, g)).then_inc(hot1[s], 1)
                    onehot(thot[s], columns(typeT, g)).then_inc(hot1[s], 1)

                def tile_onehots(i, j):
                    dve.wait_ge(counted, i * UTILES + (j + 1))
                    col = bass.ds(i * UTILES + j, 1)
                    nc.vector.tensor_scalar(key_hot[j % KEYBUF], iota_key[:, :], hiT[:, col], None, ALU.is_equal).then_inc(tile_hot, 1)
                    nc.vector.tensor_scalar(lo_hot1[j % KEYBUF], iota[:, :], dstC[:, col], None, ALU.is_equal).then_inc(tile_hot, 1)

                def unit_onehots(i):
                    cols = bass.ds(i * UTILES, UTILES)
                    for to, ids, m in ((unit_hot, relT, WINDOW), (unit_types, typeT, TYPES)):
                        nc.vector.tensor_tensor(to.rearrange("p (j w) -> p j w", w=m), ids[:, cols].unsqueeze(2).broadcast_to([P, UTILES, m]),
                                                iota[:, 0:m].unsqueeze(1).broadcast_to([P, UTILES, m]), ALU.is_equal).then_inc(unit_made, 1)
                    nc.vector.tensor_scalar(to_window, iota[:, :], unit_col[:, bass.ds(i, 1)], None, ALU.is_equal).then_inc(unit_made, 1)

                def add_group(s, at, n):
                    dve.wait_ge(added1, n)
                    for a in add_window(s, TYPES, at):
                        a.then_inc(added1, 1)

                def add_unit(at, n):
                    for g in range(2):
                        dve.wait_ge(added1, n + 2 * g)
                        for a in add_window(7, TYPES, at[g], g * WINDOW, P + g * WINDOW):
                            a.then_inc(added1, 1)

                turns3 = base_turn[:, :].rearrange("p (i u) -> p u i", u=5)
                for s in range(3):
                    stage(gathered(s, 0), s)
                    nc.vector.tensor_copy(turns3[:, s, :], base_i[:, DENSE + s:DENSE + s + 3 * TURNS + 1:3]).then_inc(table1, 1)
                for s in range(3):
                    build(gathered(s, 0), s)
                for g in range(2):
                    nc.vector.memset(turns3[:, 3 + g, 0:1], 0).then_inc(table1, 1)
                    nc.vector.tensor_copy(turns3[:, 3 + g, 1:TURNS + 1], base_i[:, g:g + 2 * TURNS - 1:2]).then_inc(table1, 1)
                nc.vector.tensor_scalar(low_i, srcT[:, 0:AHEAD].bitcast(I32), P - 1, None, ALU.bitwise_and).then_inc(low1, 1)
                dve.wait_ge(low1, 1)
                nc.vector.tensor_copy(lo_of, low_i).then_inc(low1, 1)
                dve.wait_ge(low1, 2)
                nc.vector.memset(sums[:, :], 0.0).then_inc(added1, 5)
                nc.vector.memset(side[:, :], 0.0).then_inc(added1, 5)
                nc.vector.memset(window_bank[:, 0:2 * P], 0.0).then_inc(unit_done, 1)
                for j in range(KEYBUF):
                    tile_onehots(0, j)
                dve.wait_ge(table1, 7)
                regs = [dve.alloc_register(f"first{k}") for k in range(5)]
                with dve.Fori(0, TURNS) as i:
                    at = bases(dve, regs, i)
                    for s in range(3):
                        n = i * 10 + 10 + (2 * s if s < 2 else 8)
                        dve.wait_ge(summed1[s], i + 1)
                        stage(gathered(s, i + 1), s)
                        add_group(s, at[s], n)
                        build(gathered(s, i + 1), s)
                        if s == 1:
                            dve.wait_ge(unit_done, i + 1)
                            add_unit(at[3:5], n + 2)
                            unit_onehots(i)
                        if s < 2:
                            for j in range(s * TILES + KEYBUF, (s + 1) * TILES + KEYBUF):
                                tile_onehots(i + j // UTILES, j % UTILES)
                at = bases(dve, regs, TURNS)
                for s in range(2):
                    dve.wait_ge(summed1[s], TURNS + 1)
                    add_group(s, at[s], 10 * (TURNS + 1) + 2 * s)
                dve.wait_ge(unit_done, TURNS + 1)
                add_unit(at[3:5], 10 * (TURNS + 1) + 4)

        far1 = sem("far1")
        LAST_ADD = 10 * (TURNS + 1) + 8
        with nc.Block() as block:
            @block.gpsimd
            def _(pool):
                def step(g, w, q):
                    pool.wait_ge(staged1[0], q + (TURNS + 2))
                    pool.sem_inc(issued1)
                    for d in gather(h_tab, 0):
                        d.then_inc(far_landed1, 16)

                far_steps(pool, step)

            @block.tensor
            def _(pe):
                def step(g, w, q):
                    pe.wait_ge(hot1[0], 2 * q + (2 * TURNS + 4))
                    pe.wait_ge(narrow1[0], q + (TURNS + 2))
                    pe.wait_ge(far_landed1, (q + 1) * (16 * TILES))
                    sum_tiles(0, hot[0], thot[0], TYPES, narrow[0]).then_inc(summed1[0], 1)

                far_steps(pe, step)

            @block.scalar
            def _(act):
                def step(g, w, q):
                    act.wait_ge(hot1[0], 2 * q + (2 * TURNS + 3))
                    nc.scalar.activation(narrow[0], hot[0], ACT.Copy).then_inc(narrow1[0], 1)

                far_steps(act, step)

            @block.vector
            def _(dve):
                def step(g, w, q, dense):
                    nc.vector.tensor_copy(idx[0][:, :], columns(srcT, g)).then_inc(staged1[0], 1)
                    ids = far_destinations(dve, g, w, q, far1, dense)
                    onehot(hot[0], ids, win_ids).then_inc(hot1[0], 1)
                    onehot(thot[0], columns(typeT, g)).then_inc(hot1[0], 1)
                    dve.wait_ge(summed1[0], q + (TURNS + 2))
                    dve.wait_ge(added1, 2 * q + LAST_ADD)
                    for a in add_window(0, TYPES, w * WINDOW):
                        a.then_inc(added1, 1)

                far_steps(dve, lambda g, w, q: step(g, w, q, True), 0, DENSE)
                far_steps(dve, lambda g, w, q: step(g, w, q, False), DENSE, GROUPS)

        end_phase()

        SLOTS = 4
        hcur = [rows[s // 2][:, (s % 2) * D:(s % 2 + 1) * D] for s in range(SLOTS)]
        turned = [rows[s // 2][:, (2 + 2 * (s % 2)) * D:(4 + 2 * (s % 2)) * D] for s in range(SLOTS)]
        hT, msgT = [b[:, 0:D] for b in turned], [b[:, D:2 * D] for b in turned]
        new = [rows[s // 2][:, (6 + s % 2) * D:(7 + s % 2) * D] for s in range(SLOTS)]
        gates = [(hot + whot)[s][:, 0:2 * D] for s in range(SLOTS)]
        cand = [(hot + whot)[s][:, 2 * D:3 * D] for s in range(SLOTS)]

        def ring(name):
            return [sem(f"{name}{s}") for s in range(SLOTS)]

        def tiles_in_ring(eng, pipeline):
            pipeline((0, 0, 0), None)
            with eng.Fori(0, (NT - 1) // SLOTS) as i:
                for k in range(1, SLOTS + 1):
                    pipeline((i * SLOTS + k, k % SLOTS, i + k // SLOTS), (i * SLOTS + (k - 1), k - 1, i))
            pipeline(None, (NT - 1, (NT - 1) % SLOTS, (NT - 1) // SLOTS))

        (h_in, msg_raw, msg_ready, gate_raw, gate_ready, pre_ready, cand_ready,
         tile_free) = (ring(n) for n in ("h_in", "msg_raw", "msg_ready", "gate_raw",
                                         "gate_ready", "pre_ready", "cand_ready", "tile_free"))
        v3, var3, std3, scale3 = sem("v3"), sem("var3"), sem("std3"), sem("scale3")

        with nc.Block() as block:
            @block.sync
            def _(sp):
                for s in range(SLOTS):
                    sp.dma_start(hcur[s], dram_tile(h_tab, s)).then_inc(h_in[s], 16)
                with sp.Fori(0, (NT - 1) // SLOTS - 1) as i:
                    for s in range(SLOTS):
                        sp.wait_ge(tile_free[s], i + 1)
                        sp.dma_start(hcur[s], dram_tile(h_tab, i * SLOTS + (SLOTS + s))).then_inc(h_in[s], 16)
                sp.wait_ge(tile_free[0], (NT - 1) // SLOTS)
                sp.dma_start(hcur[0], dram_tile(h_tab, NT - 1)).then_inc(h_in[0], 16)

            @block.tensor
            def _(pe):
                def pipeline(a, b):
                    if a:
                        t, s, n = a
                        pe.wait_ge(h_in[s], (n + 1) * 16)
                        nc.tensor.transpose(bank[s][:, 0:D], hcur[s], ident[:, :])
                        nodes_t = bass.ds(t * P, P)
                        nc.tensor.matmul(bank[s][:, D:2 * D], WmT[:, :], sums[:, nodes_t], start=True, stop=False)
                        nc.tensor.matmul(bank[s][:, D:2 * D], emb[:, :], side[0:TYPES, nodes_t], start=False,
                                         stop=True).then_inc(msg_raw[s], 1)
                    if b:
                        t, s, n = b
                        g = bank[4 + s]
                        nc.tensor.matmul(g[:, 0:4 * D], ones[0:1, :], bias[:, :], start=True, stop=False)
                        pe.wait_ge(msg_ready[s], n + 1)
                        nc.tensor.matmul(g[:, 0:2 * D], hT[s], WhhT[:, 0:2 * D], start=False, stop=False)
                        nc.tensor.matmul(g[:, 3 * D:4 * D], hT[s], WhhT[:, 2 * D:3 * D], start=False, stop=False)
                        nc.tensor.matmul(g[:, 0:3 * D], msgT[s], WihT[:, :], start=False, stop=True).then_inc(gate_raw[s], 1)

                tiles_in_ring(pe, pipeline)

            @block.scalar
            def _(act):
                def pipeline(a, b):
                    if a:
                        t, s, n = a
                        act.wait_ge(msg_raw[s], n + 1)
                        nc.scalar.activation(turned[s], bank[s][:, 0:2 * D], ACT.Copy).then_inc(msg_ready[s], 1)
                    if b:
                        t, s, n = b
                        act.wait_ge(gate_raw[s], n + 1)
                        nc.scalar.activation(gates[s], bank[4 + s][:, 0:2 * D], ACT.Sigmoid).then_inc(gate_ready[s], 1)
                        act.wait_ge(pre_ready[s], 2 * n + 2)
                        nc.scalar.activation(new[s], cand[s], ACT.Tanh).then_inc(cand_ready[s], 1)

                tiles_in_ring(act, pipeline)
                act.wait_ge(var3, 1)
                nc.scalar.activation(st[:, 6 * NT:7 * NT], st[:, 5 * NT:6 * NT], ACT.Sqrt).then_inc(std3, 1)

            @block.vector
            def _(dve):
                def pipeline(a, b):
                    if b:
                        t, s, n = b
                        r, z = gates[s][:, 0:D], gates[s][:, D:2 * D]
                        dve.wait_ge(gate_ready[s], n + 1)
                        nc.vector.tensor_tensor(cand[s], r, bank[4 + s][:, 3 * D:4 * D], ALU.mult).then_inc(pre_ready[s], 1)
                        dve.wait_ge(pre_ready[s], 2 * n + 1)
                        nc.vector.tensor_tensor(cand[s], cand[s], bank[4 + s][:, 2 * D:3 * D], ALU.add).then_inc(pre_ready[s], 1)
                        dve.wait_ge(cand_ready[s], n + 1)
                        x_t = nodes[:, bass.ds(t * D, D)]
                        nc.vector.tensor_tensor(cand[s], hcur[s], new[s], ALU.subtract).then_inc(v3, 1)
                        nc.vector.tensor_tensor(x_t, x_t, new[s], ALU.add).then_inc(v3, 1)
                        dve.wait_ge(v3, 4 * t + 1)
                        nc.vector.tensor_tensor(cand[s], cand[s], z, ALU.mult).then_inc(v3, 1)
                        dve.wait_ge(v3, 4 * t + 3)
                        nc.vector.tensor_tensor(x_t, x_t, cand[s], ALU.add).then_inc(v3, 1)
                        dve.wait_ge(v3, 4 * t + 4)
                        nc.vector.bn_stats(stats[:, bass.ds(t * 6, 6)], x_t).then_inc(tile_free[s], 1)

                tiles_in_ring(dve, pipeline)
                for s in range(SLOTS):
                    dve.wait_ge(tile_free[s], (NT - 1) // SLOTS + (s == 0))
                norm_scalars(dve, v3, 4 * NT, var3, std3, scale3)

        end_phase()

        h2 = hcur
        h2T = hT
        zrow = msgT
        zmask = [m.bitcast(I32) for m in new]
        prod = [(g[:, 0:D], g[:, D:2 * D]) for g in gates]
        (h2_ready, h2T_raw, h2T_ready, z_raw, z_ready, z_stored, guard, dotted) = (
            ring(n) for n in ("h2_ready", "h2T_raw", "h2T_ready", "z_raw", "z_ready", "z_stored", "guard", "dotted"))
        b4, ad_raw, ad_made, ad_stored = (sem(n) for n in ("b4", "ad_raw", "ad_made", "ad_stored"))

        paused4 = sem("paused4")

        def guard_inf(eng, value, mask, filler, done, n, carrier):
            nc.vector.tensor_scalar(mask, value, -F32_MAX, None, ALU.is_lt).then_inc(done, 1)
            eng.wait_ge(done, n + 1)
            nc.vector.scalar_tensor_tensor(mask, value, F32_MAX, mask, ALU.is_gt, ALU.max).then_inc(done, 1)
            eng.wait_ge(done, n + 2)
            eng.sem_inc(carrier)
            return nc.vector.copy_predicated(value, mask, filler)

        with nc.Block() as block:
            @block.scalar
            def _(act):
                def pipeline(a, b):
                    if a:
                        t, s, n = a
                        act.wait_ge(dotted[s], 3 * n + 3)
                        nc.scalar.activation(h2[s], nodes[:, bass.ds(t * D, D)], ACT.Relu, bias=shift[:, bass.ds(t, 1)],
                                             scale=rstd[:, bass.ds(t, 1)]).then_inc(h2_ready[s], 1)
                    if b:
                        t, s, n = b
                        act.wait_ge(h2T_raw[s], n + 1)
                        nc.scalar.activation(h2T[s], bank[s][:, 0:D], ACT.Copy).then_inc(h2T_ready[s], 1)

                tiles_in_ring(act, pipeline)

            @block.tensor
            def _(pe):
                def pipeline(a, b):
                    if a:
                        t, s, n = a
                        pe.wait_ge(h2_ready[s], n + 1)
                        nc.tensor.transpose(bank[s][:, 0:D], h2[s], ident[:, :]).then_inc(h2T_raw[s], 1)
                    if b:
                        t, s, n = b
                        pe.wait_ge(h2T_ready[s], n + 1)
                        nc.tensor.matmul(bank[4 + s][:, 0:D], ones[0:1, :], fcb[:, :], start=True, stop=False)
                        nc.tensor.matmul(bank[4 + s][:, 0:D], h2T[s], fcw[:, :], start=False, stop=True).then_inc(z_raw[s], 1)

                tiles_in_ring(pe, pipeline)
                pe.wait_ge(b4, 1)
                nc.tensor.transpose(bank[0][0:NT, 0:P], ad_tab, ident[:, :]).then_inc(ad_raw, 1)

            @block.vector
            def _(dve):
                for s in range(SLOTS):
                    nc.vector.memset(dots[s][:, :], 0.0).then_inc(dotted[s], 3)

                def pipeline(a, b):
                    if b:
                        t, s, n = b
                        dve.wait_ge(z_raw[s], n + 1)
                        dve.wait_ge(z_stored[s], (n + 1) * 16)
                        nc.vector.tensor_copy(zrow[s], bank[4 + s][:, 0:D]).then_inc(guard[s], 1)
                        dve.wait_ge(guard[s], 4 * n + 1)
                        guard_inf(dve, zrow[s], zmask[s], big[:, :], guard[s], 4 * n + 1, paused4).then_inc(guard[s], 1)
                        dve.wait_ge(guard[s], 4 * n + 4)
                        dve.wait_ge(dotted[s], 3 * n + 3)
                        for k in range(2):
                            nc.vector.tensor_tensor_reduce(prod[s][k], zrow[s], wsd[:, k * D:(k + 1) * D], 1.0, 0.0, ALU.mult,
                                                           ALU.add, dots[s][:, k:k + 1]).then_inc(dotted[s], 1)
                        dve.wait_ge(dotted[s], 3 * n + 5)
                        nc.vector.tensor_copy(terms[:, :].rearrange("p (k t) -> p k t", k=2)[:, :, bass.ds(t, 1)],
                                              dots[s][:, :].unsqueeze(2)).then_inc(dotted[s], 1)

                tiles_in_ring(dve, pipeline)
                for s in range(SLOTS):
                    dve.wait_ge(dotted[s], 3 * ((NT - 1) // SLOTS + (s == 0)) + 3)
                nc.vector.tensor_scalar(ad_tab, ad_tab, battn[:, 0:1], None, ALU.add).then_inc(b4, 1)
                dve.wait_ge(ad_raw, 1)
                nc.vector.tensor_copy(adT[:, :], bank[0][0:NT, 0:P]).then_inc(ad_made, 1)

            @block.sync
            def _(sp):
                def pipeline(a, b):
                    if b:
                        t, s, n = b
                        sp.wait_ge(guard[s], 4 * n + 4)
                        sp.dma_start(dram_tile(z_tab, t), zrow[s]).then_inc(z_stored[s], 16)

                for s in range(SLOTS):
                    sp.sem_inc(z_stored[s], 16)
                tiles_in_ring(sp, pipeline)
                sp.wait_ge(ad_made, 1)
                sp.dma_start(ad_row.rearrange("a (t p) -> (a t) p", p=P), adT[:, :]).then_inc(ad_stored, 16)
                sp.wait_ge(ad_stored, 16)
                for s in range(SLOTS):
                    sp.wait_ge(z_stored[s], 16 * ((NT - 1) // SLOTS + (s == 0) + 1))

        end_phase()

        lo_all = [sums[:, s * GROUP // 2:(s + 1) * GROUP // 2].bitcast(BF16) for s in range(2)]
        lo_hot = [side[:, s * GROUP:(s + 1) * GROUP] for s in range(2)]
        hi_hot = [whot[s][:, 0:TILES * NT] for s in range(2)]
        hi_pick = [hot[s][:, 0:TILES * NT] for s in range(2)]
        lo_in, lo_made, hi_made, picked, chosen, scored = (slot_sems(n) for n in (
            "lo_in", "lo_made", "hi_made", "picked", "chosen", "scored"))
        filled, issued5 = sem("filled"), sem("issued5")
        staged5, put_by = slot_sems("staged5"), slot_sems("put_by")

        score, gate, back = scanC
        fwd = edgeC[0]
        both = edgeC[1]
        edge_cols = st[:, 0:8]
        line = sums[0:1, 2 * GROUP:2 * GROUP + 12 * P]
        back_in = sem("back_in")
        to_chunk, v6, a6, to_line, to_col, to_tile = (sem(n) for n in (
            "to_chunk", "v6", "a6", "to_line", "to_col", "to_tile"))

        with nc.Block() as block:
            @block.sync
            def _(sp):
                def load(g, s):
                    sp.dma_start(lo_all[s], lo_row[:, bass.ds(g * GROUP, GROUP)].broadcast_to([P, GROUP])
                                 ).then_inc(lo_in[s], 16)

                sp.dma_start(dstC[:, :], dst_tab).then_inc(back_in, 16)
                sp.dma_start(sigT[:, :], sig_tab).then_inc(back_in, 16)
                for s in range(2):
                    load(s, s)
                with sp.Fori(0, PAIRS) as i:
                    for s in range(2):
                        sp.wait_ge(lo_made[s], i + 1)
                        load(2 * i + (2 + s), s)
                for s in range(2):
                    sp.wait_ge(lo_in[s], 16 * (PAIRS + 1))
                sp.wait_ge(back_in, 32)

            @block.gpsimd
            def _(pool):
                with pool.Fori(0, EARLY // 2) as i:
                    for s in range(2):
                        pool.wait_ge(staged5[s], i + 1)
                        pool.sem_inc(issued5)
                        for d in gather(z_tab, s):
                            d.then_inc(landed[s], 16)

            @block.scalar
            def _(act):
                def stage(g, s):
                    nc.scalar.copy(idx[s][:, :], columns(srcT, g)).then_inc(staged5[s], 1)

                for s in range(2):
                    stage(s, s)
                with act.Fori(0, EARLY // 2) as i:
                    for s in range(2):
                        act.wait_ge(landed[s], (i + (TURNS + 2)) * (16 * TILES))
                        act.dma_start(early[bass.ds((2 * i + s) * P, P), :], rows[s][:, :]).then_inc(put_by[s], 16)
                        act.wait_ge(put_by[s], (i + 1) * 16)
                        stage(2 * i + (2 + s), s)

            @block.tensor
            def _(pe):
                with pe.Fori(0, PAIRS) as i:
                    for s in range(2):
                        pe.wait_ge(lo_made[s], i + 1)
                        pe.wait_ge(chosen[s], i + 1)
                        for j in range(TILES):
                            mm = nc.tensor.matmul(bank[s][:, j * NT:(j + 1) * NT], lo_hot[s][:, j * P:(j + 1) * P],
                                                  as_tab, start=True, stop=True)
                        mm.then_inc(picked[s], 1)
                for s in range(2):
                    pe.wait_ge(scored[s], PAIRS)
                scores = logits[:, 0:ECOLS].rearrange("j (p b) -> j b p", b=BLOCKS)
                for b in range(BLOCKS):
                    mm = nc.tensor.transpose(bank[b // 4][:, (b % 4) * P:(b % 4 + 1) * P], scores[:, b, :], ident[:, :])
                    if b % 4 == 3 or b == BLOCKS - 1:
                        mm.then_inc(to_chunk, 1)
                pe.wait_ge(a6, 1)
                for k in range(4):
                    mm = nc.tensor.transpose(bank[5][0:1, k * P:(k + 1) * P], edge_cols[:, k:k + 1], ident[:, :])
                mm.then_inc(to_line, 1)
                pe.wait_ge(a6, 2)
                for k in range(2):
                    mm = nc.tensor.transpose(bank[6][:, k:k + 1], line[0:1, (8 + k) * P:(9 + k) * P], ident[0:1, 0:1])
                mm.then_inc(to_col, 1)
                pe.wait_ge(a6, 3)
                for b in range(BLOCKS):
                    mm = nc.tensor.transpose(bank[b // 4][:, (b % 4) * P:(b % 4 + 1) * P], both[:, b * P:(b + 1) * P], ident[:, :])
                    if b % 4 == 3 or b == BLOCKS - 1:
                        mm.then_inc(to_tile, 1)

            @block.vector
            def _(dve):
                def make(g, s, n):
                    dve.wait_ge(lo_in[s], (n + 1) * 16)
                    nc.vector.tensor_scalar(lo_hot[s], lo_all[s], pidx[:, 0:1], None, ALU.is_equal).then_inc(lo_made[s], 1)
                    onehot(hi_hot[s], columns(hiT, g)).then_inc(hi_made[s], 1)

                nc.vector.tensor_scalar(lo_i, srcT[:, :].bitcast(I32), 7, None, ALU.logical_shift_right).then_inc(filled, 1)
                dve.wait_ge(filled, 1)
                nc.vector.tensor_copy(hiT[:, :], lo_i).then_inc(filled, 1)
                dve.wait_ge(filled, 2)
                nc.vector.memset(logits[:, :], 0.0).then_inc(filled, 1)
                for s in range(2):
                    nc.vector.memset(hi_hot[s], 0.0).then_inc(chosen[s], 1)
                    dve.wait_ge(chosen[s], 1)
                dve.wait_ge(filled, 3)
                for s in range(2):
                    make(s, s, 0)
                with dve.Fori(0, PAIRS) as i:
                    for s in range(2):
                        dve.wait_ge(picked[s], i + 1)
                        dve.wait_ge(hi_made[s], i + 1)
                        nc.vector.tensor_tensor(hi_pick[s], bank[s][:, 0:TILES * NT], hi_hot[s], ALU.mult).then_inc(chosen[s], 1)
                        dve.wait_ge(chosen[s], i + 2)
                        make(2 * i + (2 + s), s, i + 1)
                        nc.vector.tensor_reduce(columns(logits, 2 * i + s), hi_pick[s].rearrange("p (j k) -> p j k", j=TILES),
                                                AX.X, ALU.add).then_inc(scored[s], 1)
                for s in range(2):
                    dve.wait_ge(lo_made[s], PAIRS + 1)
                    dve.wait_ge(scored[s], PAIRS)
                n = [0]

                def step(ins):
                    n[0] += 1
                    ins.then_inc(v6, 1)
                    dve.wait_ge(v6, n[0])

                def gates_from(same):
                    step(nc.vector.tensor_scalar(same, same, 2.0, -1.0, ALU.mult, ALU.add))
                    step(nc.vector.tensor_scalar(same, same, F32_MAX, None, ALU.mult))

                def scan(to, by, data, start, backward):
                    r = slice(None, None, -1) if backward else slice(None)
                    step(nc.vector.tensor_tensor_scan(to[:, r], by[:, r], data[:, r], start, ALU.min, ALU.max))

                for k in range(PER):
                    m = min(4, BLOCKS - 4 * k) * P
                    dve.wait_ge(to_chunk, k + 1)
                    step(nc.vector.tensor_copy(score[:, 4 * k * P:4 * k * P + m], bank[k][:, 0:m]))
                dve.wait_ge(back_in, 32)
                step(nc.vector.memset(gate, 1.0))
                step(nc.vector.tensor_tensor(gate[:, 1:CHUNK], dstC[:, 1:CHUNK], dstC[:, 0:CHUNK - 1], ALU.is_equal))
                gates_from(gate)
                step(nc.vector.memset(back, F32_MAX))
                step(nc.vector.tensor_copy(back[:, 0:CHUNK - 1], gate[:, 1:CHUNK]))
                scan(fwd, gate, score, -F32_MAX, False)
                scan(both, back, score, -F32_MAX, True)
                step(nc.vector.tensor_copy(edge_cols[:, 0:1], dstC[:, 0:1]))
                step(nc.vector.tensor_copy(edge_cols[:, 1:2], dstC[:, CHUNK - 1:CHUNK]))
                step(nc.vector.tensor_copy(edge_cols[:, 2:3], fwd[:, CHUNK - 1:CHUNK]))
                step(nc.vector.tensor_copy(edge_cols[:, 3:4], both[:, 0:1]))
                nc.vector.memset(line, 0.0).then_inc(a6, 1)
                dve.wait_ge(a6, 1)
                dve.wait_ge(to_line, 1)
                first, last, f_state, b_state, conn, through, through_b, fs, f_carry, b_carry, tmp, _ = (
                    line[:, k * P:(k + 1) * P] for k in range(12))
                step(nc.vector.tensor_copy(line[:, 0:4 * P], bank[5][0:1, 0:4 * P]))
                step(nc.vector.tensor_tensor(conn[:, 1:P], first[:, 1:P], last[:, 0:P - 1], ALU.is_equal))
                step(nc.vector.tensor_tensor(tmp, first, last, ALU.is_equal))
                step(nc.vector.tensor_tensor(through, tmp, conn, ALU.mult))
                step(nc.vector.tensor_tensor(through_b[:, 0:P - 1], tmp[:, 0:P - 1], conn[:, 1:P], ALU.mult))
                gates_from(through)
                gates_from(through_b)
                gates_from(conn)
                scan(fs, through, f_state, -F32_MAX, False)
                step(nc.vector.memset(f_carry, -F32_MAX))
                step(nc.vector.tensor_tensor(f_carry[:, 1:P], fs[:, 0:P - 1], conn[:, 1:P], ALU.min))
                scan(tmp, through_b, b_state, -F32_MAX, True)
                step(nc.vector.memset(b_carry, -F32_MAX))
                step(nc.vector.tensor_tensor(b_carry[:, 0:P - 1], tmp[:, 1:P], conn[:, 1:P], ALU.min))
                nc.vector.memset(line[:, 11 * P:12 * P], 0.0).then_inc(a6, 1)
                dve.wait_ge(to_col, 1)
                step(nc.vector.tensor_copy(edge_cols[:, 4:6], bank[6][:, 0:2]))
                scan(fwd, gate, score, edge_cols[:, 4:5], False)
                scan(both, back, score, edge_cols[:, 5:6], True)
                nc.vector.tensor_tensor(both, both, fwd, ALU.max).then_inc(a6, 1)
                for k in range(PER):
                    m = min(4, BLOCKS - 4 * k)
                    dve.wait_ge(to_tile, k + 1)
                    view = logits[:, ECOLS:2 * ECOLS].rearrange("j (p b) -> j b p", b=BLOCKS)[:, 4 * k:4 * k + m, :]
                    step(nc.vector.tensor_copy(view, bank[k][:, 0:m * P].rearrange("j (b p) -> j b p", b=m)))

        end_phase()

        ORDER = (0, 3, 1, 4, 2)
        ADDED0 = 2 * len(ORDER)

        def group_of(s, i):
            return EARLY + 3 * i + s if s < 3 else 2 * i + (s - 3)

        staged7, summed7, logit7, prob7, weigh7, small7, loaded7 = ([sem(f"{n}{s}") for s in range(5)] for n in (
            "staged7", "summed7", "logit7", "prob7", "weigh7", "small7", "loaded7"))
        turn_made = sem("turn_made")
        added7, terms_in, zero7, paused7, issued7 = (sem(n) for n in ("added7", "terms_in", "zero7", "paused7", "issued7"))
        small = [WihT[:, s * 9 * TILES:(s + 1) * 9 * TILES] for s in range(5)]
        pair = [t[:, 0:2 * TILES] for t in small]
        lg = [t[:, 2 * TILES:4 * TILES] for t in small]
        lgmask = [t[:, 4 * TILES:6 * TILES].bitcast(I32) for t in small]
        dterm, diff7, ew = ([t[:, k * TILES:(k + 1) * TILES] for t in small] for k in (6, 7, 8))
        SMALL = 9

        def probabilities(g, s):
            pw = pair[s].rearrange("p (j k) -> p k j", k=2)
            nc.scalar.activation(pw[:, 0, :], diff7[s], ACT.Exp).then_inc(prob7[s], 1)
            nc.scalar.activation(pw[:, 1, :], columns(sigT, g), ACT.Copy).then_inc(prob7[s], 1)

        def tile_view(t):
            return t.rearrange("p (j w) -> p j w", j=TILES)

        def stage(g, s):
            nc.vector.tensor_copy(idx[s][:, :], columns(srcT, g)).then_inc(staged7[s], 1)

        def build(g, s, n, at, rel=None, ids=iota):
            k = n * SMALL
            onehot(hot[s][:, :], columns(relT, g) if rel is None else rel, ids).then_inc(small7[s], 1)
            nc.vector.wait_ge(small7[s], k + 1)
            h, w = tile_view(hot[s][:, :]), tile_view(whot[s][:, :])
            nc.vector.tensor_tensor(w, h, dst_terms[:, bass.ds(at, WINDOW)].unsqueeze(1).broadcast_to(
                [P, TILES, WINDOW]), ALU.mult).then_inc(small7[s], 1)
            nc.vector.wait_ge(small7[s], k + 2)
            nc.vector.tensor_reduce(dterm[s], w, AX.X, ALU.add).then_inc(small7[s], 1)
            nc.vector.wait_ge(small7[s], k + 3)
            l3 = lg[s].rearrange("p (a j) -> p a j", a=2)
            nc.vector.tensor_tensor(l3, logits3[:, :, bass.ds(g * TILES, TILES)],
                                    dterm[s].unsqueeze(1).broadcast_to([P, 2, TILES]),
                                    ALU.add).then_inc(small7[s], 1)
            nc.vector.wait_ge(small7[s], k + 4)
            guard_inf(nc.vector, lg[s], lgmask[s], big[:, 0:2 * TILES], small7[s], k + 4, paused7).then_inc(small7[s], 1)
            nc.vector.wait_ge(small7[s], k + 7)
            nc.vector.scalar_tensor_tensor(lg[s], lg[s], 0.01, lg[s], ALU.mult,
                                           ALU.max).then_inc(small7[s], 1)
            nc.vector.wait_ge(small7[s], k + 8)
            nc.vector.tensor_tensor(diff7[s], lg[s][:, 0:TILES], lg[s][:, TILES:2 * TILES],
                                    ALU.subtract).then_inc(logit7[s], 1)
            nc.vector.wait_ge(prob7[s], 2 * n + 2)
            pw = pair[s].rearrange("p (j k) -> p k j", k=2)
            nc.vector.tensor_tensor(ew[s], pw[:, 0, :], pw[:, 1, :], ALU.mult).then_inc(small7[s], 1)
            nc.vector.wait_ge(small7[s], k + 9)
            nc.vector.tensor_tensor(w, h, ew[s].unsqueeze(2).broadcast_to([P, TILES, WINDOW]),
                                    ALU.mult).then_inc(weigh7[s], 1)

        with nc.Block() as block:
            @block.sync
            def _(sp):
                def load(s, i):
                    sp.dma_start(rows[s], early[bass.ds(group_of(s, i) * P, P), :]).then_inc(loaded7[s], 16)

                sp.dma_start(dst_terms[:, 0:ROWS], ad_row.broadcast_to([P, ROWS])).then_inc(terms_in, 16)
                for s in (3, 4):
                    load(s, 0)
                with sp.Fori(0, TURNS) as i:
                    for s in (3, 4):
                        sp.wait_ge(summed7[s], i + 1)
                        load(s, i + 1)

            @block.gpsimd
            def _(pool):
                with pool.Fori(0, TURNS) as i:
                    for s in range(3):
                        pool.wait_ge(staged7[s], i + 1)
                        pool.sem_inc(issued7)
                        for d in gather(z_tab, s):
                            d.then_inc(landed[s], 16)

            @block.tensor
            def _(pe):
                def unit(k, s, i):
                    pe.wait_ge(weigh7[s], i + 1)
                    pe.wait_ge(added7, 2 * (5 * i + k) + (ADDED0 - 8))
                    if s < 3:
                        before = TURNS + 1 + EARLY // 2 if s < 2 else TURNS
                        pe.wait_ge(landed[s], (i + (before + 1)) * (16 * TILES))
                    else:
                        pe.wait_ge(loaded7[s], (i + 1) * 16)
                    sum_tiles(s, whot[s], pair[s], 2, hot[s]).then_inc(summed7[s], 1)

                with pe.Fori(0, TURNS) as i:
                    for k, s in enumerate(ORDER):
                        unit(k, s, i)
                for k, s in enumerate((3, 4)):
                    unit(k, s, TURNS)

            @block.scalar
            def _(act):
                with act.Fori(0, TURNS + 1) as i:
                    for s in ORDER:
                        act.wait_ge(logit7[s], i + 1)
                        probabilities(group_of(s, i), s)

            @block.vector
            def _(dve):
                turns3 = base_turn[:, :].rearrange("p (i u) -> p u i", u=5)
                for k, s in enumerate(ORDER):
                    g0, step = (EARLY + s, 3) if s < 3 else (s - 3, 2)
                    nc.vector.tensor_copy(turns3[:, k, :], base_i[:, g0:g0 + step * TURNS + 1:step]).then_inc(turn_made, 1)
                for s in range(3):
                    stage(group_of(s, 0), s)
                nc.vector.memset(sums[:, :], 0.0).then_inc(added7, ADDED0 // 2)
                nc.vector.memset(side[:, :], 0.0).then_inc(added7, ADDED0 // 2)
                nc.vector.memset(dst_terms[:, ROWS:ACCN], 0.0).then_inc(zero7, 1)
                dve.wait_ge(zero7, 1)
                dve.wait_ge(terms_in, 16)
                dve.wait_ge(turn_made, 5)
                regs = [dve.alloc_register(f"base{k}") for k in range(10)]
                at = bases(dve, regs[0:5], 0)
                for k, s in enumerate(ORDER):
                    build(group_of(s, 0), s, 0, at[k])

                def finish(k, s, i, at):
                    dve.wait_ge(added7, 2 * (5 * i + k) + ADDED0)
                    for a in add_window(s, 2, at):
                        a.then_inc(added7, 1)

                with dve.Fori(0, TURNS) as i:
                    at = bases(dve, regs, i)
                    for k, s in enumerate(ORDER):
                        dve.wait_ge(summed7[s], i + 1)
                        if s < 3:
                            stage(group_of(s, i + 1), s)
                        finish(k, s, i, at[k])
                        build(group_of(s, i + 1), s, i + 1, at[k + 5])
                at = bases(dve, regs[0:5], TURNS)
                for k, s in enumerate((3, 4)):
                    dve.wait_ge(summed7[s], TURNS + 1)
                    finish(k, s, TURNS, at[ORDER.index(s)])

        far7 = sem("far7")
        with nc.Block() as block:
            @block.gpsimd
            def _(pool):
                def step(g, w, q):
                    pool.wait_ge(staged7[0], q + (TURNS + 2))
                    pool.sem_inc(issued7)
                    for d in gather(z_tab, 0):
                        d.then_inc(far_landed7, 16)

                far_steps(pool, step)

            @block.tensor
            def _(pe):
                def step(g, w, q):
                    pe.wait_ge(weigh7[0], q + (TURNS + 2))
                    pe.wait_ge(far_landed7, (q + 1) * (16 * TILES))
                    sum_tiles(0, whot[0], pair[0], 2, hot[0]).then_inc(summed7[0], 1)

                far_steps(pe, step)

            @block.scalar
            def _(act):
                def step(g, w, q):
                    act.wait_ge(logit7[0], q + (TURNS + 2))
                    probabilities(g, 0)

                far_steps(act, step)

            @block.vector
            def _(dve):
                def step(g, w, q):
                    stage(g, 0)
                    ids = far_destinations(dve, g, w, q, far7)
                    build(g, 0, q + (TURNS + 1), w * WINDOW, ids, win_ids)
                    dve.wait_ge(summed7[0], q + (TURNS + 1))
                    dve.wait_ge(added7, 2 * q + ADDED0 + 2 * GROUPS)
                    for a in add_window(0, 2, w * WINDOW):
                        a.then_inc(added7, 1)

                far_steps(dve, step)

        end_phase()

        den, bsm, scaled, paused8 = (sem(n) for n in ("den", "bsm", "scaled", "paused8"))
        v8, var8, std8 = sem("v8"), sem("var8"), sem("std8")
        quot = [rows[0][:, s * CH:(s + 1) * CH] for s in range(2)]
        bns = WhhT[:, 0:6 * (NCH + 1)]
        mv = sb("mv", 2)
        col = sb("col", 4)
        maskc = rows[1][:, 0:CH].bitcast(I32)
        bigc = whot[0]
        inv = dst_terms
        pos = [hot[s][:, 0:CH] for s in range(2)]
        ex = [whot[s][:, 0:CH] for s in range(2)]
        el = [rows[0][:, s * CH:(s + 1) * CH] for s in range(2)]
        res = [rows[1][:, s * CH:(s + 1) * CH] for s in range(2)]
        neg_ready, exp_ready, elu_ready, turned, res_ready, out_done = (slot_sems(n) for n in (
            "neg_ready", "exp_ready", "elu_ready", "turned", "res_ready", "out_done"))

        with nc.Block() as block:
            @block.tensor
            def _(pe):
                for c in range(NCH + 1):
                    m = CH if c < NCH else CTAIL
                    if c >= 2:
                        pe.wait_ge(v8, 5 * (c - 2) + 3)
                    for k in range(2):
                        nc.tensor.matmul(bank[2 * (c % 2) + k][:, 0:m], ident[0:2, k:k + 1].broadcast_to([2, P]),
                                         side[0:2, c * CH:c * CH + m], start=True, stop=True).then_inc(den, 1)

            @block.vector
            def _(dve):
                nc.vector.memset(bigc[:, :], BIG).then_inc(bsm, 1)
                dve.wait_ge(bsm, 1)
                for c in range(NCH + 1):
                    m = CH if c < NCH else CTAIL
                    part = sums[:, c * CH:c * CH + m]
                    q = quot[c % 2][:, 0:m]
                    r = inv[:, c * CH:c * CH + m]
                    n = 5 * c
                    dve.wait_ge(den, 2 * c + 2)
                    nc.vector.tensor_scalar(q, bank[2 * (c % 2)][:, 0:m], 0.5, None, ALU.max).then_inc(v8, 1)
                    dve.wait_ge(v8, n + 1)
                    nc.vector.scalar_tensor_tensor(r, bank[2 * (c % 2) + 1][:, 0:m], BETA_EPS, q, ALU.add,
                                                   ALU.mult).then_inc(v8, 1)
                    dve.wait_ge(v8, n + 2)
                    nc.vector.reciprocal(r, r).then_inc(v8, 1)
                    dve.wait_ge(v8, n + 3)
                    nc.vector.tensor_tensor(part, part, r, ALU.mult).then_inc(v8, 1)
                    dve.wait_ge(v8, n + 4)
                    guard_inf(dve, part, maskc[:, 0:m], bigc[:, 0:m], scaled, 3 * c, paused8).then_inc(scaled, 1)
                    dve.wait_ge(scaled, 3 * c + 3)
                    nc.vector.bn_stats(bns[:, 6 * c:6 * c + 6], part).then_inc(v8, 1)
                n = 5 * (NCH + 1)
                dve.wait_ge(v8, n)
                nc.vector.bn_aggr(mv[:, :], bns).then_inc(var8, 1)
                dve.wait_ge(std8, 1)
                nc.vector.reciprocal(col[:, 1:2], col[:, 0:1]).then_inc(v8, 1)
                dve.wait_ge(v8, n + 1)
                nc.vector.tensor_tensor(col[:, 2:3], col[:, 1:2], gamma[:, :], ALU.mult).then_inc(v8, 1)
                dve.wait_ge(v8, n + 2)

            @block.scalar
            def _(act):
                act.wait_ge(var8, 1)
                nc.scalar.activation(col[:, 0:1], mv[:, 1:2], ACT.Sqrt, bias=eps[:, 0:1]).then_inc(std8, 1)

        with nc.Block() as block:
            def chunk(c):
                return sums[:, bass.ds(c * CH, CH)]

            @block.vector
            def _(dve):
                def first(c, s, m, n):
                    part = sums[:, bass.ds(c * CH, m)]
                    y = el[s][:, 0:m]
                    nc.vector.tensor_scalar(part, part, mv[:, 0:1], col[:, 2:3], ALU.subtract, ALU.mult).then_inc(neg_ready[s], 1)
                    dve.wait_ge(neg_ready[s], 4 * n + 1)
                    nc.vector.tensor_scalar(part, part, beta[:, 0:1], None, ALU.add).then_inc(neg_ready[s], 1)
                    dve.wait_ge(neg_ready[s], 4 * n + 2)
                    nc.vector.tensor_scalar(ex[s][:, 0:m], part, 0.0, None, ALU.min).then_inc(neg_ready[s], 1)
                    nc.vector.tensor_scalar(pos[s][:, 0:m], part, 0.0, None, ALU.max).then_inc(neg_ready[s], 1)
                    dve.wait_ge(exp_ready[s], n + 1)
                    dve.wait_ge(neg_ready[s], 4 * n + 4)
                    nc.vector.scalar_tensor_tensor(y, ex[s][:, 0:m], -1.0, pos[s][:, 0:m], ALU.add, ALU.add).then_inc(elu_ready[s], 1)

                def second(c, s, m, n):
                    dve.wait_ge(turned[s], n + 1)
                    for k in range(-(-m // P)):
                        w = min(P, m - k * P)
                        ins = nc.vector.tensor_tensor(res[s][0:w, k * D:(k + 1) * D], bank[s][0:w, k * D:(k + 1) * D],
                                                      nodes[0:w, bass.ds(c * CH + k * P, D)], ALU.add)
                    ins.then_inc(res_ready[s], 1)

                with dve.Fori(0, NCH // 2) as i:
                    for s in range(2):
                        first(2 * i + s, s, CH, i)
                        dve.wait_ge(out_done[s], (i + 1) * 16)
                        second(2 * i + s, s, CH, i)
                first(NCH, 0, CTAIL, NCH // 2)
                dve.wait_ge(out_done[0], (NCH // 2 + 1) * 16)
                second(NCH, 0, CTAIL, NCH // 2)

            @block.scalar
            def _(act):
                def one(s, m, n):
                    act.wait_ge(neg_ready[s], 4 * n + 3)
                    nc.scalar.activation(ex[s][:, 0:m], ex[s][:, 0:m], ACT.Exp).then_inc(exp_ready[s], 1)

                with act.Fori(0, NCH // 2) as i:
                    for s in range(2):
                        one(s, CH, i)
                one(0, CTAIL, NCH // 2)

            @block.tensor
            def _(pe):
                def one(s, m, n):
                    pe.wait_ge(elu_ready[s], n + 1)
                    for k in range(-(-m // P)):
                        w = min(P, m - k * P)
                        mm = nc.tensor.transpose(bank[s][0:w, k * P:(k + 1) * P], el[s][:, k * P:k * P + w], ident[:, :])
                    mm.then_inc(turned[s], 1)

                with pe.Fori(0, NCH // 2) as i:
                    for s in range(2):
                        one(s, CH, i)
                one(0, CTAIL, NCH // 2)

            @block.sync
            def _(sp):
                for s in range(2):
                    sp.sem_inc(out_done[s], 16)
                with sp.Fori(0, NCH // 2) as i:
                    for s in range(2):
                        sp.wait_ge(res_ready[s], i + 1)
                        sp.dma_start(out[bass.ds((2 * i + s) * CH, CH), :].rearrange("(k p) d -> p k d", p=P),
                                     res[s].rearrange("p (k d) -> p k d", d=D)).then_inc(out_done[s], 16)
                sp.wait_ge(res_ready[0], NCH // 2 + 1)
                for k in range(-(-CTAIL // P)):
                    w = min(P, CTAIL - k * P)
                    sp.dma_start(out[NCH * CH + k * P:NCH * CH + k * P + w, :], res[0][0:w, k * D:(k + 1) * D]
                                 ).then_inc(out_done[0], 16)
                sp.wait_ge(out_done[0], 16 * (NCH // 2 + 1 + -(-CTAIL // P)))
                sp.wait_ge(out_done[1], 16 * (NCH // 2 + 1))

        phase.close()


_INS = ["x", "src", "dst", "edge_type_9", "edge_weight", "L0_gnn_W_msg", "L0_gnn_b_msg", "L0_gnn_edge_embed",
        "L0_gnn_W_ih", "L0_gnn_W_hh", "L0_gnn_b_ih", "L0_gnn_b_hh", "L1_gnn_fc_w", "L1_gnn_fc_b",
        "L1_gnn_attn_w", "L1_gnn_attn_b", "L1_gnn_bn_gamma", "L1_gnn_bn_beta"]


def kernel(**inputs):
    import numpy as _np
    import concourse.bacc as _bacc
    from concourse import mybir as _mybir
    from concourse.bass_utils import run_bass_kernel_spmd as _run

    nc = _bacc.Bacc("TRN2", target_bir_lowering=False, num_devices=1)
    arrays, args = {}, []
    for name in _INS:
        a = _np.ascontiguousarray(inputs[name])
        arrays[f"in_{name}"] = a
        args.append(nc.dram_tensor(f"in_{name}", a.shape, _mybir.dt.from_np(a.dtype), kind="ExternalInput").ap())
    shape = inputs["x"].shape
    args.append(nc.dram_tensor("out_dram", shape, _mybir.dt.float32, kind="ExternalOutput").ap())
    gnn(nc, *args)
    r = _run(nc, [arrays], core_ids=[0])
    return r.results[0]["out_dram"]
```

```python
from contextlib import ExitStack

import numpy as np

import concourse.bass as bass
from concourse import mybir

F32 = mybir.dt.float32
BF16 = mybir.dt.bfloat16
I32 = mybir.dt.int32
U32 = mybir.dt.uint32
ALU = mybir.AluOpType
ACT = mybir.ActivationFunctionType
AX = mybir.AxisListType

P = 128
TILES = 8
GROUP = TILES * P
WINDOW = 64
SPAN = 8
PAD_DST = -20000.0
LN_EPS = 1e-5
BETA_EPS = 1e-6
BIG = 1e9
F32_MAX = float(np.finfo(np.float32).max)
TYPES = 9


def gnn(nc, x, src, dst, edge_type, edge_weight, W_msg, b_msg, edge_embed, W_ih, W_hh, b_ih, b_hh,
        fc_w, fc_b, attn_w, attn_b, bn_gamma, bn_beta, out):
    N, D = x.shape
    (E,) = src.shape
    NT = -(-N // P)
    NTAIL = N - (NT - 1) * P
    ROWS = NT * P
    BLOCKS = -(-E // (P * P))
    CHUNK = BLOCKS * P
    FULL, REST = E // CHUNK, E % CHUNK
    GROUPS = -(-E // GROUP)
    PAIRS = GROUPS // 2
    ECOLS = BLOCKS * P
    assert D == P and GROUPS == 2 * PAIRS and ECOLS >= (GROUPS + 2) * TILES and NT % 4 == 1
    TURNS7 = (GROUPS - 1) // 3
    EARLY = TURNS7 + 1
    EARLY5 = EARLY - 8
    assert GROUPS == EARLY + 2 * TURNS7 and PAIRS % 2 == 1 and EARLY5 % 3 == 0 and (EARLY - EARLY5) % 2 == 0
    TURNS = (GROUPS - 2) // 5
    assert GROUPS == 5 * TURNS + 2
    DENSE = 2 * TURNS
    KEYS = NT * SPAN
    UTILES = 2 * TILES
    assert DENSE * GROUP <= E and KEYS <= 512 and UTILES * SPAN == P
    WINS = -(-N // WINDOW)
    ACCN = -(-(N + WINDOW) // P) * P
    CH = 4 * P
    NCH = N // CH
    CTAIL = N - NCH * CH

    h_tab = nc.dram_tensor("h_tab", [ROWS, D], F32, kind="Internal").ap()
    z_tab = nc.dram_tensor("z_tab", [ROWS, D], F32, kind="Internal").ap()
    early = nc.dram_tensor("early", [EARLY * P, TILES * D], F32, kind="Internal").ap()
    lo_row = nc.dram_tensor("lo_row", [1, P * CHUNK], BF16, kind="Internal").ap()
    dst_tab = nc.dram_tensor("dst_tab", [P, CHUNK], F32, kind="Internal").ap()
    sig_tab = nc.dram_tensor("sig_tab", [P, ECOLS], F32, kind="Internal").ap()
    rel_row = nc.dram_tensor("rel_row", [1, P * CHUNK], BF16, kind="Internal").ap()
    ad_row = nc.dram_tensor("ad_row", [1, ROWS], F32, kind="Internal").ap()
    ad_parts = nc.dram_tensor("ad_parts", [2, ROWS + WINDOW, 2], BF16, kind="Internal").ap()

    with ExitStack() as ctx:
        def sb(name, cols, dt=F32, rows=P):
            return ctx.enter_context(nc.sbuf_tensor(name, [rows, cols], dt))

        phase = ExitStack()
        held = []

        def sem(name):
            held.append(phase.enter_context(nc.semaphore(name)))
            return held[-1]

        landed = [ctx.enter_context(nc.semaphore(f"landed{s}")) for s in range(3)]
        far_landed1 = ctx.enter_context(nc.semaphore("far_landed1"))
        far_landed7 = ctx.enter_context(nc.semaphore("far_landed7"))

        def end_phase():
            with nc.Block() as block:
                @block.sync
                def _(sp):
                    for s in held:
                        sp.sem_clear(s)
            phase.close()
            held.clear()

        bank = [ctx.enter_context(nc.psum_tensor(f"bank{i}", [P, 512], F32)) for i in range(8)]

        nodes = sb("nodes", NT * D)
        sums = sb("sums", ACCN)
        side = sb("side", ACCN)
        wide = sb("wide", ACCN)
        srcT = sb("srcT", ECOLS, U32)
        hiT = sb("hiT", ECOLS)
        relT = sb("relT", ECOLS)
        typeT = sb("typeT", ECOLS)
        sigT = sb("sigT", ECOLS)
        logits = sb("logits", 2 * ECOLS)
        pairs = logits[:, :].rearrange("p (t k) -> p k t", k=2)
        dstC = sb("dstC", CHUNK)
        weightT = wide[:, 0:ECOLS]
        edgeC = [wide[:, k * CHUNK:(k + 1) * CHUNK] for k in range(3)]
        scanC = [side[:, k * CHUNK:(k + 1) * CHUNK] for k in range(3)]

        rows = [sb(f"rows{s}", TILES * D) for s in range(3)]
        HW = TILES * WINDOW
        hots = sb("hots", 10 * HW)
        hot = [hots[:, s * HW:(s + 1) * HW] for s in range(5)]
        whot = [hots[:, (5 + s) * HW:(6 + s) * HW] for s in range(5)]
        idx = [sb(f"idx{s}", TILES, U32) for s in range(3)]
        base_i = sb("base_i", GROUPS + 4, I32, 1)
        base_turn = sb("base_turn", 5 * (TURNS + 1), I32, 1)
        base_b = sb("base_b", GROUPS)

        ident = sb("ident", P)
        ones = sb("ones", P)
        iota = sb("iota", P)
        pidx_i = sb("pidx_i", 1, I32)
        pidx = sb("pidx", 1)
        eps = sb("eps", 1)
        big = sb("big", P)
        iota_key = sb("iota_key", KEYS)
        expand = sb("expand", P, F32, UTILES)
        unit_col = sb("unit_col", TURNS)
        col_base = sb("col_base", 2)
        far_group = sb("far_group", GROUPS, I32, 1)
        far_rank = sb("far_rank", GROUPS, I32, 1)
        far_any = sb("far_any", 1, I32, 1)
        far_ids = [sb(f"far_ids{k}", TILES) for k in range(2)]
        win_ids = sb("win_ids", WINDOW)
        win_base = sb("win_base", WINS)

        wraw = [rows[2][:, i * D:(i + 1) * D] for i in range(7)]
        WmT = sb("WmT", D)
        WihT = sb("WihT", 3 * D)
        WhhT = sb("WhhT", 3 * D)
        emb = sb("emb", D, F32, TYPES)
        bmsg = sb("bmsg", D, F32, TYPES)
        bias_ih, bias_hh = hot[2][0:3, 0:3 * D], hot[3][0:3, 0:3 * D]
        bias = sb("bias", 4 * D, F32, 3)
        fcw = sb("fcw", D)
        fcb = sb("fcb", D)
        wsd = sb("wsd", 2 * D)
        battn = sb("battn", 1)
        gamma = sb("gamma", 1)
        beta = sb("beta", 1)

        stats = sb("stats", NT * 6)
        st = sb("st", 8 * NT)
        rstd = sb("rstd", NT)
        shift = sb("shift", NT)
        terms = sb("terms", 2 * NT)
        as_tab, ad_tab = terms[:, 0:NT], terms[:, NT:2 * NT]
        adT = sb("adT", P, F32, NT)

        consts, ld_x, ld_e, ld_w, zeroed, padded, blank = (sem(n) for n in (
            "consts", "ld_x", "ld_e", "ld_w", "zeroed", "padded", "blank"))
        v1, a1, p1, put_by1, units_in = (sem(n) for n in ("v1", "a1", "p1", "put_by1", "units_in"))
        h_head, h_split, rel_made, normed1 = (sem(n) for n in ("h_head", "h_split", "rel_made", "normed1"))
        row_banks = (0, 7, 3, 4)
        rel_b = side[:, 0:BLOCKS * P // 2].bitcast(BF16)
        assert BLOCKS <= 16
        h_made, lo_stored = sem("h_made"), sem("lo_stored")
        h_stored = [sem(f"h_stored{i}") for i in range(2)]
        src_i = edgeC[0].bitcast(I32)
        raw_i = [edgeC[1].bitcast(I32), edgeC[2].bitcast(I32)]
        srcC, typeC, sigC = scanC
        lo_i = logits[:, 0:CHUNK].bitcast(I32)
        PER = -(-BLOCKS // 4)
        DCOLS = DENSE * TILES
        key = hiT[:, 0:DCOLS]
        key_i = sums[:, 0:KEYS].bitcast(I32)
        in_tile, in_span, near, pair_key = (sums[:, 512 + k * DCOLS:512 + (k + 1) * DCOLS] for k in range(4))
        far_edge = sums[:, 512 + 4 * DCOLS:512 + 4 * DCOLS + GROUPS * TILES]
        far_in = sums[:, ACCN - GROUPS:ACCN]
        ones_row = sums[0:1, ACCN - 2 * GROUPS:ACCN - GROUPS]
        base_f = sums[0:1, ACCN - 3 * GROUPS:ACCN - 2 * GROUPS]
        far_count = sums[0:1, ACCN - 4 * GROUPS:ACCN - 3 * GROUPS]
        iota_i = sums[:, ACCN - 4 * GROUPS - P:ACCN - 4 * GROUPS].bitcast(I32)
        units = sums[0:UTILES, ACCN - 4 * GROUPS - P - 4 * TURNS:ACCN - 4 * GROUPS - P]
        tile_base_i = units[:, 0:2 * TURNS].bitcast(I32)
        tile_base = units[:, 2 * TURNS:4 * TURNS]
        assert 512 + 4 * DCOLS + (TILES + 4) * GROUPS + P + 4 * TURNS <= ACCN
        HEADS = 32
        parts_at = [(wide[:, :].bitcast(BF16), 0), (logits[:, :].bitcast(BF16), HEADS)]

        def parts(t, m):
            mem, first = parts_at[t >= HEADS]
            return mem[:, (t - first) * 3 * D:(t - first + m) * 3 * D]

        def part_view(t, m, k):
            return parts(t, m).rearrange("p (t k d) -> p k t d", k=3, d=D)[:, k]

        rest = [sums[:, k * TILES * D:(k + 1) * TILES * D] for k in range(2)]
        lo_b = logits[:, CHUNK:2 * CHUNK].bitcast(BF16)[:, 0:CHUNK]
        hbuf = [rows[0], rows[1]]
        var1, std1, scale1 = sem("var1"), sem("std1"), sem("scale1")
        chunk_loads = [(src, src_i), (dst, raw_i[0]), (edge_type, raw_i[1]), (edge_weight, sigC)]

        def norm_scalars(eng, chain, n, var_ready, std_ready, scale_ready):
            s = stats[:, :].rearrange("p (t k) -> p k t", k=6)
            mean2, diff, m2, diff2, part, var, std = (st[:, k * NT:(k + 1) * NT] for k in range(7))
            nc.vector.tensor_tensor(mean2, s[:, 1, :], s[:, 4, :], ALU.add).then_inc(chain, 1)
            nc.vector.tensor_tensor(diff, s[:, 1, :], s[:, 4, :], ALU.subtract).then_inc(chain, 1)
            nc.vector.tensor_tensor(m2, s[:, 2, :], s[:, 5, :], ALU.add).then_inc(chain, 1)
            eng.wait_ge(chain, n + 3)
            nc.vector.tensor_tensor(diff2, diff, diff, ALU.mult).then_inc(chain, 1)
            nc.vector.tensor_scalar(part, m2, 1.0 / D, LN_EPS, ALU.mult, ALU.add).then_inc(chain, 1)
            eng.wait_ge(chain, n + 5)
            nc.vector.scalar_tensor_tensor(var, diff2, 0.25, part, ALU.mult, ALU.add).then_inc(var_ready, 1)
            eng.wait_ge(std_ready, 1)
            nc.vector.reciprocal(rstd[:, :], std).then_inc(chain, 1)
            eng.wait_ge(chain, n + 6)
            nc.vector.scalar_tensor_tensor(shift[:, :], mean2, -0.5, rstd[:, :], ALU.mult,
                                           ALU.mult).then_inc(scale_ready, 1)

        with nc.Block() as block:
            @block.sync
            def _(sp):
                sp.wait_ge(padded, 5)
                for a, to in chunk_loads:
                    a2 = a[0:FULL * CHUNK].rearrange("(p k) -> p k", k=CHUNK)
                    sp.dma_start(to[0:FULL, :], a2).then_inc(ld_e, 16)
                    sp.dma_start(to[FULL:FULL + 1, 0:REST],
                                 a[FULL * CHUNK:E].rearrange("(p k) -> p k", p=1)).then_inc(ld_e, 16)
                sp.dma_start(base_i[0:1, 0:GROUPS],
                             dst[0:E].rearrange("(p k) -> p k", p=1)[:, 0:(GROUPS - 1) * GROUP + 1:GROUP],
                             allow_slow_non_contiguous=True).then_inc(ld_e, 16)
                in_units = dst[0:DENSE * GROUP]
                sp.dma_start(tile_base_i[:, 0:TURNS], in_units.rearrange("(u k e) -> k u e", k=UTILES, e=P)[:, :, 0],
                             allow_slow_non_contiguous=True).then_inc(units_in, 16)
                for k in range(2):
                    sp.dma_start(tile_base_i[k * TILES:(k + 1) * TILES, TURNS:2 * TURNS],
                                 in_units.rearrange("(u k e) -> k u e", k=2, e=GROUP)[k:k + 1, :, 0].broadcast_to([TILES, TURNS]),
                                 allow_slow_non_contiguous=True).then_inc(units_in, 16)
                sp.dma_start(wraw[0], W_msg).then_inc(ld_w, 16)
                for k in range(3):
                    sp.dma_start(wraw[1 + k], W_ih[k * D:(k + 1) * D, :]).then_inc(ld_w, 16)
                    sp.dma_start(wraw[4 + k], W_hh[k * D:(k + 1) * D, :]).then_inc(ld_w, 16)
                sp.dma_start(emb[:, :], edge_embed).then_inc(ld_w, 16)
                sp.dma_start(bmsg[:, :], b_msg.rearrange("(a d) -> a d", a=1).broadcast_to([TYPES, D])).then_inc(ld_w, 16)
                sp.dma_start(bias_ih, b_ih.rearrange("(a d) -> a d", a=1).broadcast_to([3, 3 * D])).then_inc(ld_w, 16)
                sp.dma_start(bias_hh, b_hh.rearrange("(a d) -> a d", a=1).broadcast_to([3, 3 * D])).then_inc(ld_w, 16)
                sp.dma_start(fcw[:, :], fc_w).then_inc(ld_w, 16)
                sp.dma_start(fcb[:, :], fc_b.rearrange("(a d) -> a d", a=1).broadcast_to([P, D])).then_inc(ld_w, 16)
                sp.dma_start(wsd[:, :], attn_w.rearrange("k a -> a k").broadcast_to([P, 2 * D])).then_inc(ld_w, 16)
                sp.dma_start(battn[:, :], attn_b.rearrange("(a d) -> a d", a=1).broadcast_to([P, 1])).then_inc(ld_w, 16)
                sp.dma_start(gamma[:, :], bn_gamma.rearrange("(d a) -> d a", a=1)).then_inc(ld_w, 16)
                sp.dma_start(beta[:, :], bn_beta.rearrange("(d a) -> d a", a=1)).then_inc(ld_w, 16)
                sp.wait_ge(v1, 2)
                sp.dma_start(lo_row.rearrange("a (p k) -> (a p) k", p=P), lo_b).then_inc(lo_stored, 16)
                sp.wait_ge(v1, 4 + 4 * PER)
                sp.dma_start(dst_tab, dstC[:, :]).then_inc(put_by1, 16)
                sp.dma_start(sig_tab, sigT[:, :]).then_inc(put_by1, 16)
                sp.wait_ge(rel_made, PER)
                sp.dma_start(rel_row.rearrange("a (b r e) -> r (a b) e", r=P, e=P),
                             rel_b.rearrange("r (b e) -> r b e", e=P)).then_inc(put_by1, 16)
                for b in range(NT // 8):
                    sp.wait_ge(h_made, 8 * (b + 1))
                    sp.dma_start(h_tab[b * 8 * P:(b + 1) * 8 * P, :].rearrange("(t p) d -> p t d", p=P),
                                 hbuf[b % 2][:, :].rearrange("p (t d) -> p t d", d=D)).then_inc(h_stored[b % 2], 16)
                sp.wait_ge(h_made, NT)
                sp.dma_start(h_tab[(NT - 1) * P:NT * P, :], hbuf[0][:, 0:D]).then_inc(h_stored[0], 16)
                sp.wait_ge(h_stored[0], 16 * (NT // 16 + 1))
                sp.wait_ge(h_stored[1], 16 * (NT // 16))
                sp.wait_ge(lo_stored, 16)
                sp.wait_ge(put_by1, 48)
                sp.wait_ge(ld_w, 16 * 17)
                sp.wait_ge(ld_e, 16 * 9)

            @block.gpsimd
            def _(pool):
                nc.gpsimd.memset(src_i, 0).then_inc(padded, 1)
                nc.gpsimd.memset(raw_i[0], int(PAD_DST)).then_inc(padded, 1)
                nc.gpsimd.memset(raw_i[1], 0).then_inc(padded, 1)
                nc.gpsimd.memset(sigC, 0.0).then_inc(padded, 1)
                nc.gpsimd.memset(ident[:, :], 0.0).then_inc(blank, 1)
                nc.gpsimd.memset(ones[:, :], 1.0).then_inc(consts, 1)
                nc.gpsimd.memset(eps[:, :], LN_EPS).then_inc(consts, 1)
                nc.gpsimd.memset(big[:, :], BIG).then_inc(consts, 1)
                nc.gpsimd.iota(iota_i[:, :], [[1, P]], base=0, channel_multiplier=0).then_inc(consts, 1)
                nc.gpsimd.iota(pidx_i[:, :], [[0, 1]], base=0, channel_multiplier=1).then_inc(consts, 1)
                pool.wait_ge(blank, 1)
                nc.gpsimd.affine_select(out=ident[:, :], in_=ident[:, :], compare_op=ALU.not_equal, fill=1.0,
                                        base=0, pattern=[[-1, P]], channel_multiplier=1).then_inc(consts, 1)
                pool.wait_ge(consts, 6)
                nc.gpsimd.tensor_copy(iota[:, :], iota_i[:, :]).then_inc(consts, 1)
                nc.gpsimd.tensor_scalar(win_base[:, :], iota_i[:, 0:WINS], float(WINDOW), 1.0, ALU.mult, ALU.add).then_inc(consts, 1)
                nc.gpsimd.tensor_copy(pidx[:, :], pidx_i[:, :]).then_inc(consts, 1)
                nc.gpsimd.memset(expand[:, :], 1.0).then_inc(blank, 1)
                pool.wait_ge(blank, 2)
                nc.gpsimd.affine_select(out=expand[:, :], in_=expand[:, :], compare_op=ALU.is_ge, fill=0.0,
                                        base=0, pattern=[[1, P]], channel_multiplier=-SPAN).then_inc(blank, 1)
                pool.wait_ge(blank, 3)
                nc.gpsimd.affine_select(out=expand[:, :], in_=expand[:, :], compare_op=ALU.is_ge, fill=0.0,
                                        base=SPAN - 1, pattern=[[-1, P]], channel_multiplier=SPAN).then_inc(consts, 1)
                nc.gpsimd.iota(key_i, [[1, KEYS]], base=1, channel_multiplier=0).then_inc(blank, 1)
                pool.wait_ge(blank, 4)
                nc.gpsimd.tensor_copy(iota_key[:, :], key_i).then_inc(consts, 1)

            @block.scalar
            def _(act):
                act.wait_ge(zeroed, 1)
                act.dma_start(nodes[:, 0:(NT - 1) * D].rearrange("p (t d) -> p t d", d=D),
                              x[0:(NT - 1) * P, :].rearrange("(t p) d -> p t d", p=P)).then_inc(ld_x, 16)
                act.dma_start(nodes[0:NTAIL, (NT - 1) * D:NT * D], x[(NT - 1) * P:N, :]).then_inc(ld_x, 16)
                act.wait_ge(ld_e, 16 * 9)
                nc.scalar.activation(typeC, raw_i[1], ACT.Copy).then_inc(a1, 1)
                act.wait_ge(var1, 1)
                nc.scalar.activation(st[:, 6 * NT:7 * NT], st[:, 5 * NT:6 * NT], ACT.Sqrt).then_inc(std1, 1)
                act.wait_ge(scale1, 1)
                for b in range(NT // 8 + 1):
                    if b >= 2:
                        act.wait_ge(h_stored[b % 2], 16 * (b // 2))
                        act.wait_ge(h_split, 3 * (b - 1))
                    m = 8 if b < NT // 8 else 1
                    for k in range(m):
                        t = 8 * b + k
                        nc.scalar.activation(hbuf[b % 2][:, k * D:(k + 1) * D], nodes[:, t * D:(t + 1) * D],
                                             ACT.Relu, bias=shift[:, t:t + 1],
                                             scale=rstd[:, t:t + 1]).then_inc(h_made, 1)
                    act.wait_ge(h_made, 8 * b + m)
                    if b == 0:
                        act.wait_ge(a1, 1)
                        act.wait_ge(v1, 4)
                    if b == 2:
                        act.wait_ge(v1, 10 + 4 * PER)
                    nc.scalar.activation(part_view(8 * b, m, 0), hbuf[b % 2][:, 0:m * D].rearrange("p (t d) -> p t d", d=D),
                                         ACT.Copy).then_inc(h_head, 1)

            @block.tensor
            def _(pe):
                pe.wait_ge(consts, 11)
                k = 0
                for n, c in enumerate((srcC, dstC[:, :], typeC, sigC)):
                    if n == 0:
                        pe.wait_ge(v1, 4)
                    if n == 2:
                        pe.wait_ge(a1, 1)
                    for b in range(0, BLOCKS, 4):
                        if k >= 8:
                            pe.wait_ge(v1, 4 + k - 7)
                        for q in range(b, min(b + 4, BLOCKS)):
                            mm = nc.tensor.transpose(bank[k % 8][:, (q - b) * P:(q - b + 1) * P],
                                                     c[:, q * P:(q + 1) * P], ident[:, :])
                        mm.then_inc(p1, 1)
                        k += 1
                pe.wait_ge(v1, 5 + k)
                nc.tensor.matmul(bank[0][:, 0:GROUPS], ones[0:1, :], base_f[:, :], start=True, stop=True).then_inc(p1, 1)
                pe.wait_ge(v1, 5 + k + 2)
                for b in range(0, DCOLS, 512):
                    m = min(512, DCOLS - b)
                    mm = nc.tensor.matmul(bank[3 + b // 512][:, 0:m], ones[0:1, :], relT[0:1, b:b + m], start=True, stop=True)
                mm.then_inc(p1, 1)
                pe.wait_ge(v1, 5 + k + 6)
                nc.tensor.matmul(bank[5][:, 0:TURNS], expand[:, :], tile_base[:, 0:TURNS], start=True, stop=True).then_inc(p1, 1)
                pe.wait_ge(v1, 5 + k + 17)
                nc.tensor.matmul(bank[6][0:1, 0:GROUPS], ones[:, 0:1], far_in, start=True, stop=True).then_inc(p1, 1)
                pe.wait_ge(ld_w, 16 * 17)
                for i in range(7):
                    mm = nc.tensor.transpose(bank[1 + i // 4][:, (i % 4) * P:(i % 4 + 1) * P], wraw[i], ident[:, :])
                mm.then_inc(p1, 1)
                for q in range(BLOCKS):
                    mm = nc.tensor.transpose(bank[row_banks[q // 4]][:, (q % 4) * P:(q % 4 + 1) * P],
                                             relT[:, q * P:(q + 1) * P], ident[:, :])
                mm.then_inc(p1, 1)

            @block.vector
            def _(dve):
                nc.vector.memset(nodes[:, (NT - 1) * D:NT * D], 0.0).then_inc(zeroed, 1)
                nc.vector.memset(base_i[:, :], 0).then_inc(padded, 1)
                dve.wait_ge(ld_x, 32)
                STEP = 7
                assert NT % STEP == 0
                with dve.Fori(0, NT // STEP) as i:
                    for k in range(STEP):
                        t = i * STEP + k
                        nc.vector.bn_stats(stats[:, bass.ds(t * 6, 6)], nodes[:, bass.ds(t * D, D)]).then_inc(normed1, 1)
                dve.wait_ge(normed1, NT)
                norm_scalars(dve, normed1, NT, var1, std1, scale1)
                dve.wait_ge(ld_e, 16 * 9)
                nc.vector.tensor_scalar(lo_i, src_i, P - 1, None, ALU.bitwise_and).then_inc(v1, 1)
                dve.wait_ge(v1, 1)
                nc.vector.tensor_copy(lo_b, lo_i).then_inc(v1, 1)
                nc.vector.tensor_copy(srcC, src_i).then_inc(v1, 1)
                nc.vector.tensor_copy(dstC[:, :], raw_i[0]).then_inc(v1, 1)
                for k in range(4 * PER):
                    to = (srcT, relT, typeT, sigT)[k // PER]
                    b = 4 * (k % PER)
                    m = min(4, BLOCKS - b)
                    dve.wait_ge(p1, k + 1)
                    view = to[:, :].rearrange("j (p b) -> j b p", b=BLOCKS)[:, b:b + m, :]
                    nc.vector.tensor_copy(view, bank[k % 8][:, 0:m * P].rearrange("j (b p) -> j b p", b=m)).then_inc(v1, 1)
                n = 4 + 4 * PER
                nc.vector.tensor_copy(base_f[:, :], base_i[:, 0:GROUPS]).then_inc(v1, 1)
                n += 1
                dve.wait_ge(p1, 4 * PER + 1)
                nc.vector.tensor_copy(base_b[:, :], bank[0][:, 0:GROUPS]).then_inc(v1, 1)
                dve.wait_ge(v1, n + 1)
                rel3 = relT[:, 0:GROUPS * TILES].rearrange("p (g j) -> p g j", j=TILES)
                nc.vector.tensor_tensor(rel3, rel3, base_b[:, :].unsqueeze(2).broadcast_to([P, GROUPS, TILES]),
                                        ALU.subtract).then_inc(v1, 1)
                nc.vector.tensor_scalar(typeT[:, :], typeT[:, :], 0.0, float(TYPES - 1), ALU.max, ALU.min).then_inc(v1, 1)
                nc.vector.tensor_scalar(lo_i, srcT[:, :].bitcast(I32), 7, None, ALU.logical_shift_right).then_inc(v1, 1)
                dve.wait_ge(lo_stored, 16)
                dve.wait_ge(v1, n + 4)
                nc.vector.tensor_copy(hiT[:, :], lo_i).then_inc(v1, 1)
                dve.wait_ge(units_in, 48)
                nc.vector.tensor_tensor(tile_base[:, 0:TURNS], tile_base_i[:, 0:TURNS], tile_base_i[:, TURNS:2 * TURNS],
                                        ALU.subtract).then_inc(v1, 1)
                nc.vector.tensor_scalar(col_base[:, 0:1].bitcast(I32), pidx_i[:, :], (SPAN - 1) | WINDOW, None,
                                        ALU.bitwise_and).then_inc(v1, 1)
                dve.wait_ge(v1, n + 7)
                nc.vector.tensor_copy(col_base[:, 1:2], col_base[:, 0:1].bitcast(I32)).then_inc(v1, 1)
                dve.wait_ge(p1, 4 * PER + 2)
                for b in range(0, DCOLS, 512):
                    m = min(512, DCOLS - b)
                    nc.vector.tensor_tensor(in_tile[:, b:b + m], relT[:, b:b + m], bank[3 + b // 512][:, 0:m],
                                            ALU.subtract).then_inc(v1, 1)
                assert DCOLS > 512 and DCOLS <= 1024
                dve.wait_ge(v1, n + 10)
                nc.vector.tensor_scalar(in_span, in_tile, float(SPAN), None, ALU.is_lt).then_inc(v1, 1)
                nc.vector.scalar_tensor_tensor(pair_key, hiT[:, 0:DCOLS], float(SPAN), in_tile, ALU.mult, ALU.add).then_inc(v1, 1)
                dve.wait_ge(v1, n + 12)
                nc.vector.scalar_tensor_tensor(near, relT[:, 0:DCOLS], float(WINDOW), in_span, ALU.is_lt, ALU.mult).then_inc(v1, 1)
                dve.wait_ge(v1, n + 13)
                nc.vector.scalar_tensor_tensor(key, pair_key, 1.0, near, ALU.add, ALU.mult).then_inc(v1, 1)
                nc.vector.tensor_scalar(far_edge[:, DCOLS:], relT[:, DCOLS:GROUPS * TILES], float(WINDOW), None,
                                        ALU.is_ge).then_inc(v1, 1)
                dve.wait_ge(v1, n + 15)
                nc.vector.tensor_scalar(far_edge[:, 0:DCOLS], key, 0.0, None, ALU.is_equal).then_inc(v1, 1)
                dve.wait_ge(v1, n + 16)
                nc.vector.tensor_reduce(far_in, far_edge.rearrange("p (g j) -> p g j", j=TILES), AX.X, ALU.max).then_inc(v1, 1)
                n += 17
                dve.wait_ge(p1, 4 * PER + 3)
                nc.vector.tensor_scalar(unit_col[:, :], bank[5][:, 0:TURNS], col_base[:, 1:2], None, ALU.add).then_inc(v1, 1)
                nc.vector.memset(ones_row, 1.0).then_inc(v1, 1)
                dve.wait_ge(p1, 4 * PER + 4)
                nc.vector.tensor_scalar(far_group[:, :], bank[6][0:1, 0:GROUPS], 1.0, None, ALU.min).then_inc(v1, 1)
                dve.wait_ge(v1, n + 3)
                nc.vector.tensor_reduce(far_any[:, :], far_group[:, :], AX.X, ALU.max).then_inc(v1, 1)
                nc.vector.tensor_tensor_scan(far_count[:, :], ones_row, far_group[:, :], 0.0, ALU.mult, ALU.add).then_inc(v1, 1)
                dve.wait_ge(v1, n + 5)
                nc.vector.tensor_tensor(far_rank[:, :], far_count[:, :], far_group[:, :], ALU.subtract).then_inc(v1, 1)
                n += 6
                dve.wait_ge(p1, 4 * PER + 5)
                nc.vector.tensor_copy(WmT[:, :], bank[1][:, 0:D]).then_inc(v1, 1)
                nc.vector.tensor_copy(WihT[:, :], bank[1][:, D:4 * D]).then_inc(v1, 1)
                nc.vector.tensor_copy(WhhT[:, :], bank[2][:, 0:3 * D]).then_inc(v1, 1)
                nc.vector.tensor_tensor(emb[:, :], emb[:, :], bmsg[:, :], ALU.add).then_inc(v1, 1)
                nc.vector.tensor_tensor(bias[:, 0:2 * D], bias_ih[:, 0:2 * D], bias_hh[:, 0:2 * D], ALU.add).then_inc(v1, 1)
                nc.vector.tensor_copy(bias[:, 2 * D:3 * D], bias_ih[:, 2 * D:3 * D]).then_inc(v1, 1)
                nc.vector.tensor_copy(bias[:, 3 * D:4 * D], bias_hh[:, 2 * D:3 * D]).then_inc(v1, 1)
                n += 7
                dve.wait_ge(p1, 4 * PER + 6)
                for k in range(PER):
                    m = min(4, BLOCKS - 4 * k) * P
                    nc.vector.tensor_copy(rel_b[:, 4 * k * P:4 * k * P + m], bank[row_banks[k]][:, 0:m]).then_inc(rel_made, 1)
                for b in range(NT // 8 + 1):
                    m = 8 if b < NT // 8 else 1
                    left = rest[b % 2][:, 0:m * D].rearrange("p (t d) -> p t d", d=D)
                    dve.wait_ge(h_head, b + 1)
                    nc.vector.tensor_tensor(left, hbuf[b % 2][:, 0:m * D].rearrange("p (t d) -> p t d", d=D),
                                            part_view(8 * b, m, 0), ALU.subtract).then_inc(h_split, 1)
                    dve.wait_ge(h_split, 3 * b + 1)
                    nc.vector.tensor_copy(part_view(8 * b, m, 1), left).then_inc(h_split, 1)
                    dve.wait_ge(h_split, 3 * b + 2)
                    nc.vector.tensor_tensor(part_view(8 * b, m, 2), left, part_view(8 * b, m, 1), ALU.subtract).then_inc(h_split, 1)

        end_phase()

        def slot_sems(name):
            return [sem(f"{name}{s}") for s in range(2)]

        def onehot(to, rel, ids=iota):
            k = to.shape[1] // TILES
            return nc.vector.tensor_tensor(to.rearrange("p (j w) -> p j w", j=TILES),
                                           rel.unsqueeze(2).broadcast_to([P, TILES, k]),
                                           ids[:, 0:k].unsqueeze(1).broadcast_to([P, TILES, k]), ALU.is_equal)

        def columns(t, g):
            return t[:, bass.ds(g * TILES, TILES)]

        def gather(table, s):
            for j in range(TILES):
                yield nc.gpsimd.indirect_dma_start(rows[s][:, j * D:(j + 1) * D], None, table,
                                                   bass.IndirectOffsetOnAxis(ap=idx[s][:, j:j + 1], axis=0))

        def sum_tiles(s, weighted, extra, m, plain):
            for lhs, k, by, c in ((rows[s], D, weighted, 0), (extra, m, plain, WINDOW)):
                for j in range(TILES):
                    mm = nc.tensor.matmul(bank[s][0:k, c:c + WINDOW], lhs[:, j * k:(j + 1) * k],
                                          by[:, j * WINDOW:(j + 1) * WINDOW], start=j == 0, stop=j == TILES - 1)
            return mm

        def add_window(s, m, at, main=0, other=WINDOW):
            to, to2 = sums[:, bass.ds(at, WINDOW)], side[0:m, bass.ds(at, WINDOW)]
            yield nc.vector.tensor_tensor(to, to, bank[s][:, main:main + WINDOW], ALU.add)
            yield nc.vector.tensor_tensor(to2, to2, bank[s][0:m, other:other + WINDOW], ALU.add)

        def far_steps(eng, step, first=0, end=GROUPS):
            with eng.If(eng.value_load(far_any[0:1, 0:1], min_val=0, max_val=1) > 0):
                with eng.Fori(first, end) as g:
                    with eng.If(eng.value_load(far_group[0:1, bass.ds(g, 1)], min_val=0, max_val=1) > 0):
                        rank = eng.value_load(far_rank[0:1, bass.ds(g, 1)], min_val=0, max_val=GROUPS)
                        with eng.Fori(0, WINS) as w:
                            step(g, w, rank * WINS + w)
                    eng.nop()
                eng.nop()
            eng.nop()

        def far_destinations(dve, g, w, q, done, dense=False):
            n = 4 * q
            rel = columns(relT, g)
            if dense:
                nc.vector.tensor_scalar(far_ids[0][:, :], columns(key, g), 0.0, None, ALU.is_equal).then_inc(done, 1)
            else:
                nc.vector.tensor_scalar(far_ids[0][:, :], rel, float(WINDOW), None, ALU.is_ge).then_inc(done, 1)
            nc.vector.tensor_scalar(far_ids[1][:, :], rel, base_b[:, bass.ds(g, 1)], 1.0, ALU.add, ALU.add).then_inc(done, 1)
            dve.wait_ge(done, n + 2)
            nc.vector.tensor_tensor(far_ids[1][:, :], far_ids[1][:, :], far_ids[0][:, :], ALU.mult).then_inc(done, 1)
            nc.vector.tensor_scalar(win_ids[:, :], iota[:, 0:WINDOW], win_base[:, bass.ds(w, 1)], None, ALU.add).then_inc(done, 1)
            dve.wait_ge(done, n + 4)
            return far_ids[1][:, :]

        CROWD = 3
        KEYBUF = 4
        AHEAD = DCOLS + KEYBUF
        lo_of = dstC[:, 0:AHEAD]
        key_hot = [dstC[:, AHEAD + k * KEYS // 2:AHEAD + (k + 1) * KEYS // 2].bitcast(BF16) for k in range(KEYBUF)]
        to_window = dstC[:, AHEAD + KEYBUF * KEYS // 2:AHEAD + KEYBUF * KEYS // 2 + P]
        narrow = [sigT[:, s * HW // 2:(s + 1) * HW // 2].bitcast(BF16) for s in range(3)]
        unit_hot = sigT[:, 3 * HW // 2:5 * HW // 2].bitcast(BF16)
        unit_sums = sigT[:, 5 * HW // 2:5 * HW // 2 + 3 * D]
        spare = hots[:, 3 * HW:10 * HW]
        counts = spare[:, 0:NT * P // 2].bitcast(BF16)
        lo_hot1 = [spare[:, (NT + k) * P // 2:(NT + k + 1) * P // 2].bitcast(BF16) for k in range(KEYBUF)]
        small_at = (NT + KEYBUF) * P // 2
        thot = [spare[:, small_at + s * TILES * TYPES // 2:small_at + (s + 1) * TILES * TYPES // 2].bitcast(BF16) for s in range(3)]
        unit_types = spare[:, small_at + 3 * TILES * TYPES // 2:small_at + 5 * TILES * TYPES // 2].bitcast(BF16)
        assert small_at + 5 * TILES * TYPES // 2 <= 7 * HW
        low_i = counts.bitcast(I32)[:, 0:AHEAD]
        count_bank, unit_bank, window_bank = bank[3:3 + CROWD], bank[6], bank[7]

        staged1, hot1, narrow1, summed1 = ([sem(f"{n}{s}") for s in range(3)] for n in ("staged1", "hot1", "narrow1", "summed1"))
        issued1 = sem("issued1")
        added1 = sem("added1")
        low1 = sem("low1")
        table1, tile_hot, counted, kept, unit_made, unit_raw, unit_kept, unit_done = (sem(n) for n in (
            "table1", "tile_hot", "counted", "kept", "unit_made", "unit_raw", "unit_kept", "unit_done"))

        def bases(dve, regs, i):
            dve.reg_load(regs, base_turn[0:1, bass.ds(i * len(regs), len(regs))])
            return [dve.snap(r, min_val=0, max_val=N - 1) for r in regs]

        def gathered(s, i):
            return DENSE + 3 * i + s

        with nc.Block() as block:
            @block.gpsimd
            def _(pool):
                def group(s, i):
                    pool.wait_ge(staged1[s], i + 1)
                    pool.sem_inc(issued1)
                    for d in gather(h_tab, s):
                        d.then_inc(landed[s], 16)

                with pool.Fori(0, TURNS) as i:
                    for s in range(3):
                        group(s, i)
                for s in range(2):
                    group(s, TURNS)

            @block.tensor
            def _(pe):
                def group(s, i):
                    pe.wait_ge(hot1[s], 2 * i + 2)
                    pe.wait_ge(narrow1[s], i + 1)
                    pe.wait_ge(landed[s], (i + 1) * (16 * TILES))
                    sum_tiles(s, hot[s], thot[s], TYPES, narrow[s]).then_inc(summed1[s], 1)

                def count(i, j):
                    pe.wait_ge(tile_hot, (i * UTILES + (j + 1)) * 2)
                    pe.wait_ge(kept, i * UTILES + (j + 1 if j >= CROWD else CROWD))
                    nc.tensor.matmul(count_bank[j % CROWD][:, 0:KEYS], lo_hot1[j % KEYBUF], key_hot[j % KEYBUF],
                                     start=True, stop=True).then_inc(counted, 1)

                def unit(i):
                    pe.wait_ge(kept, i * UTILES + (UTILES + CROWD))
                    for t in range(NT):
                        mm = nc.tensor.matmul(unit_bank[:, 0:3 * D], counts[:, t * P:(t + 1) * P], parts(t, 1),
                                              start=t == 0, stop=t == NT - 1)
                    mm.then_inc(unit_raw, 1)
                    pe.wait_ge(unit_made, (i + 1) * 3)
                    for g in range(2):
                        for j in range(g * TILES, (g + 1) * TILES):
                            nc.tensor.matmul(window_bank[0:TYPES, P + g * WINDOW:P + (g + 1) * WINDOW],
                                             unit_types[:, j * TYPES:(j + 1) * TYPES], unit_hot[:, j * WINDOW:(j + 1) * WINDOW],
                                             start=j == g * TILES, stop=j == (g + 1) * TILES - 1)
                    pe.wait_ge(unit_kept, i + 1)
                    for k in range(3):
                        mm = nc.tensor.matmul(window_bank[:, 0:P], unit_sums[:, k * D:(k + 1) * D], to_window,
                                              start=k == 0, stop=k == 2)
                    mm.then_inc(unit_done, 1)

                pe.sem_inc(counted, KEYBUF)
                with pe.Fori(0, TURNS) as i:
                    for s in range(3):
                        group(s, i)
                        if s < 2:
                            for j in range(s * TILES, (s + 1) * TILES):
                                count(i, j)
                    unit(i)
                for s in range(2):
                    group(s, TURNS)

            @block.scalar
            def _(act):
                def narrow_copy(s, i):
                    act.wait_ge(hot1[s], 2 * i + 1)
                    nc.scalar.activation(narrow[s], hot[s], ACT.Copy).then_inc(narrow1[s], 1)

                by_tile = counts.rearrange("p (t c) -> p t c", c=P)
                for s in range(3):
                    narrow_copy(s, 0)
                act.sem_inc(kept, CROWD)
                act.sem_inc(unit_raw)
                with act.Fori(0, TURNS) as i:
                    for j in range(UTILES):
                        act.wait_ge(counted, i * UTILES + (j + 1 + KEYBUF))
                        if j == 0:
                            act.wait_ge(unit_raw, i + 1)
                        nc.scalar.activation(by_tile[:, :, j * SPAN:(j + 1) * SPAN],
                                             count_bank[j % CROWD][:, 0:KEYS].rearrange("p (t w) -> p t w", w=SPAN),
                                             ACT.Copy).then_inc(kept, 1)
                        if j == TILES - 1:
                            narrow_copy(0, i + 1)
                    narrow_copy(1, i + 1)
                    act.wait_ge(unit_raw, i + 2)
                    nc.scalar.activation(unit_sums, unit_bank[:, 0:3 * D], ACT.Copy).then_inc(unit_kept, 1)
                    narrow_copy(2, i + 1)

            @block.vector
            def _(dve):
                def stage(g, s):
                    nc.vector.tensor_copy(idx[s][:, :], columns(srcT, g)).then_inc(staged1[s], 1)

                def build(g, s):
                    onehot(hot[s], columns(relT, g)).then_inc(hot1[s], 1)
                    onehot(thot[s], columns(typeT, g)).then_inc(hot1[s], 1)

                def tile_onehots(i, j):
                    dve.wait_ge(counted, i * UTILES + (j + 1))
                    col = bass.ds(i * UTILES + j, 1)
                    nc.vector.tensor_scalar(key_hot[j % KEYBUF], iota_key[:, :], hiT[:, col], None, ALU.is_equal).then_inc(tile_hot, 1)
                    nc.vector.tensor_scalar(lo_hot1[j % KEYBUF], iota[:, :], dstC[:, col], None, ALU.is_equal).then_inc(tile_hot, 1)

                def unit_onehots(i):
                    cols = bass.ds(i * UTILES, UTILES)
                    for to, ids, m in ((unit_hot, relT, WINDOW), (unit_types, typeT, TYPES)):
                        nc.vector.tensor_tensor(to.rearrange("p (j w) -> p j w", w=m), ids[:, cols].unsqueeze(2).broadcast_to([P, UTILES, m]),
                                                iota[:, 0:m].unsqueeze(1).broadcast_to([P, UTILES, m]), ALU.is_equal).then_inc(unit_made, 1)
                    nc.vector.tensor_scalar(to_window, iota[:, :], unit_col[:, bass.ds(i, 1)], None, ALU.is_equal).then_inc(unit_made, 1)

                def add_group(s, at, n):
                    dve.wait_ge(added1, n)
                    for a in add_window(s, TYPES, at):
                        a.then_inc(added1, 1)

                def add_unit(at, n):
                    for g in range(2):
                        dve.wait_ge(added1, n + 2 * g)
                        for a in add_window(7, TYPES, at[g], g * WINDOW, P + g * WINDOW):
                            a.then_inc(added1, 1)

                turns3 = base_turn[:, :].rearrange("p (i u) -> p u i", u=5)
                for s in range(3):
                    stage(gathered(s, 0), s)
                    nc.vector.tensor_copy(turns3[:, s, :], base_i[:, DENSE + s:DENSE + s + 3 * TURNS + 1:3]).then_inc(table1, 1)
                for s in range(3):
                    build(gathered(s, 0), s)
                for g in range(2):
                    nc.vector.memset(turns3[:, 3 + g, 0:1], 0).then_inc(table1, 1)
                    nc.vector.tensor_copy(turns3[:, 3 + g, 1:TURNS + 1], base_i[:, g:g + 2 * TURNS - 1:2]).then_inc(table1, 1)
                nc.vector.tensor_scalar(low_i, srcT[:, 0:AHEAD].bitcast(I32), P - 1, None, ALU.bitwise_and).then_inc(low1, 1)
                dve.wait_ge(low1, 1)
                nc.vector.tensor_copy(lo_of, low_i).then_inc(low1, 1)
                dve.wait_ge(low1, 2)
                nc.vector.memset(sums[:, :], 0.0).then_inc(added1, 5)
                nc.vector.memset(side[:, :], 0.0).then_inc(added1, 5)
                nc.vector.memset(window_bank[:, 0:2 * P], 0.0).then_inc(unit_done, 1)
                for j in range(KEYBUF):
                    tile_onehots(0, j)
                dve.wait_ge(table1, 7)
                regs = [dve.alloc_register(f"first{k}") for k in range(5)]
                with dve.Fori(0, TURNS) as i:
                    at = bases(dve, regs, i)
                    for s in range(3):
                        n = i * 10 + 10 + (2 * s if s < 2 else 8)
                        dve.wait_ge(summed1[s], i + 1)
                        stage(gathered(s, i + 1), s)
                        if s < 2:
                            for j in range(s * TILES + KEYBUF, (s + 1) * TILES + KEYBUF):
                                tile_onehots(i + j // UTILES, j % UTILES)
                        add_group(s, at[s], n)
                        build(gathered(s, i + 1), s)
                        if s == 1:
                            dve.wait_ge(unit_done, i + 1)
                            add_unit(at[3:5], n + 2)
                            unit_onehots(i)
                at = bases(dve, regs, TURNS)
                for s in range(2):
                    dve.wait_ge(summed1[s], TURNS + 1)
                    add_group(s, at[s], 10 * (TURNS + 1) + 2 * s)
                dve.wait_ge(unit_done, TURNS + 1)
                add_unit(at[3:5], 10 * (TURNS + 1) + 4)

        far1 = sem("far1")
        LAST_ADD = 10 * (TURNS + 1) + 8
        with nc.Block() as block:
            @block.gpsimd
            def _(pool):
                def step(g, w, q):
                    pool.wait_ge(staged1[0], q + (TURNS + 2))
                    pool.sem_inc(issued1)
                    for d in gather(h_tab, 0):
                        d.then_inc(far_landed1, 16)

                far_steps(pool, step)

            @block.tensor
            def _(pe):
                def step(g, w, q):
                    pe.wait_ge(hot1[0], 2 * q + (2 * TURNS + 4))
                    pe.wait_ge(narrow1[0], q + (TURNS + 2))
                    pe.wait_ge(far_landed1, (q + 1) * (16 * TILES))
                    sum_tiles(0, hot[0], thot[0], TYPES, narrow[0]).then_inc(summed1[0], 1)

                far_steps(pe, step)

            @block.scalar
            def _(act):
                def step(g, w, q):
                    act.wait_ge(hot1[0], 2 * q + (2 * TURNS + 3))
                    nc.scalar.activation(narrow[0], hot[0], ACT.Copy).then_inc(narrow1[0], 1)

                far_steps(act, step)

            @block.vector
            def _(dve):
                def step(g, w, q, dense):
                    nc.vector.tensor_copy(idx[0][:, :], columns(srcT, g)).then_inc(staged1[0], 1)
                    ids = far_destinations(dve, g, w, q, far1, dense)
                    onehot(hot[0], ids, win_ids).then_inc(hot1[0], 1)
                    onehot(thot[0], columns(typeT, g)).then_inc(hot1[0], 1)
                    dve.wait_ge(summed1[0], q + (TURNS + 2))
                    dve.wait_ge(added1, 2 * q + LAST_ADD)
                    for a in add_window(0, TYPES, w * WINDOW):
                        a.then_inc(added1, 1)

                far_steps(dve, lambda g, w, q: step(g, w, q, True), 0, DENSE)
                far_steps(dve, lambda g, w, q: step(g, w, q, False), DENSE, GROUPS)

        end_phase()

        SLOTS = 8
        BANKS = 4
        assert (NT - 1) % SLOTS == 0
        wide_slots = 5
        slot_at = [wide[:, (10 + 7 * s) * D:(17 + 7 * s) * D] for s in range(wide_slots)] + [
            logits[:, 7 * s * D:7 * (s + 1) * D] for s in range(SLOTS - wide_slots)]
        hcur, hT, msgT, new, cand = ([t[:, k * D:(k + 1) * D] for t in slot_at] for k in range(5))
        turned = [t[:, D:3 * D] for t in slot_at]
        gates = [t[:, 5 * D:7 * D] for t in slot_at]

        def ring(name):
            return [sem(f"{name}{s}") for s in range(SLOTS)]

        def tiles_in_ring(eng, *stages):
            def short_steps(steps):
                for t in steps:
                    for lag, stage in enumerate(stages):
                        if 0 <= t - lag < NT:
                            stage(t - lag, (t - lag) % SLOTS, (t - lag) // SLOTS)

            short_steps(range(SLOTS + 1))
            with eng.Fori(1, (NT - 1) // SLOTS) as i:
                for k in range(1, SLOTS + 1):
                    for lag, stage in enumerate(stages):
                        stage(i * SLOTS + (k - lag), (k - lag) % SLOTS, i + (k - lag) // SLOTS)
            short_steps(range(NT, NT + len(stages) - 1))

        (h_in, msg_raw, msg_ready, gate_raw, gate_ready, pre_ready, cand_ready,
         tile_free) = (ring(n) for n in ("h_in", "msg_raw", "msg_ready", "gate_raw",
                                         "gate_ready", "pre_ready", "cand_ready", "tile_free"))
        v3, var3, std3, scale3, bias_split = (sem(n) for n in ("v3", "var3", "std3", "scale3", "bias_split"))
        bias3, ones3, bias_part = (wide[0:3, k * 2 * D:(k + 1) * 2 * D].bitcast(BF16) for k in range(3))
        bias_sum = wide[0:3, 6 * D:10 * D]

        with nc.Block() as block:
            @block.tensor
            def _(pe):
                def message(t, s, n):
                    pe.wait_ge(h_in[s], n + 1)
                    nc.tensor.transpose(bank[s % BANKS][:, 0:D], hcur[s], ident[:, :])
                    nodes_t = bass.ds(t * P, P)
                    nc.tensor.matmul(bank[s % BANKS][:, D:2 * D], WmT[:, :], sums[:, nodes_t], start=True, stop=False)
                    nc.tensor.matmul(bank[s % BANKS][:, D:2 * D], emb[:, :], side[0:TYPES, nodes_t], start=False,
                                     stop=True).then_inc(msg_raw[s], 1)

                def gate(t, s, n):
                    pe.wait_ge(pre_ready[(s + BANKS) % SLOTS], 2 * n + (4 if s >= BANKS else 2))
                    g = bank[BANKS + s % BANKS]
                    nc.tensor.matmul(g[:, 0:4 * D], ones3[:, 0:P], bias3, start=True, stop=False)
                    pe.wait_ge(msg_ready[s], n + 1)
                    nc.tensor.matmul(g[:, 0:2 * D], hT[s], WhhT[:, 0:2 * D], start=False, stop=False)
                    nc.tensor.matmul(g[:, 3 * D:4 * D], hT[s], WhhT[:, 2 * D:3 * D], start=False, stop=False)
                    nc.tensor.matmul(g[:, 0:3 * D], msgT[s], WihT[:, :], start=False, stop=True).then_inc(gate_raw[s], 1)

                pe.wait_ge(bias_split, 12)
                tiles_in_ring(pe, message, gate)

            @block.scalar
            def _(act):
                def norm(t, s, n):
                    act.wait_ge(tile_free[s], n + 1)
                    nc.scalar.activation(hcur[s], nodes[:, bass.ds(t * D, D)], ACT.Relu, bias=shift[:, bass.ds(t, 1)],
                                         scale=rstd[:, bass.ds(t, 1)]).then_inc(h_in[s], 1)

                def messages_in(t, s, n):
                    act.wait_ge(msg_raw[s], n + 1)
                    nc.scalar.activation(turned[s], bank[s % BANKS][:, 0:2 * D], ACT.Copy).then_inc(msg_ready[s], 1)

                def gates_in(t, s, n):
                    act.wait_ge(gate_raw[s], n + 1)
                    nc.scalar.activation(gates[s], bank[BANKS + s % BANKS][:, 0:2 * D], ACT.Sigmoid).then_inc(gate_ready[s], 1)

                def candidate(t, s, n):
                    act.wait_ge(pre_ready[s], 2 * n + 4)
                    nc.scalar.activation(new[s], cand[s], ACT.Tanh).then_inc(cand_ready[s], 1)

                tiles_in_ring(act, norm, messages_in, gates_in, candidate)
                act.wait_ge(var3, 1)
                nc.scalar.activation(st[:, 6 * NT:7 * NT], st[:, 5 * NT:6 * NT], ACT.Sqrt).then_inc(std3, 1)

            @block.vector
            def _(dve):
                def hidden_part(t, s, n):
                    dve.wait_ge(gate_ready[s], n + 1)
                    nc.vector.tensor_tensor(cand[s], gates[s][:, 0:D], bank[BANKS + s % BANKS][:, 3 * D:4 * D], ALU.mult).then_inc(pre_ready[s], 1)
                    dve.wait_ge(pre_ready[s], 2 * n + 3)
                    nc.vector.tensor_tensor(cand[s], cand[s], bank[BANKS + s % BANKS][:, 2 * D:3 * D], ALU.add).then_inc(pre_ready[s], 1)

                def update(t, s, n):
                    dve.wait_ge(cand_ready[s], n + 1)
                    x_t = nodes[:, bass.ds(t * D, D)]
                    nc.vector.tensor_tensor(cand[s], hcur[s], new[s], ALU.subtract).then_inc(v3, 1)
                    nc.vector.tensor_tensor(x_t, x_t, new[s], ALU.add).then_inc(v3, 1)
                    dve.wait_ge(v3, 4 * t + 1)
                    nc.vector.tensor_tensor(cand[s], cand[s], gates[s][:, D:2 * D], ALU.mult).then_inc(v3, 1)
                    dve.wait_ge(v3, 4 * t + 3)
                    nc.vector.tensor_tensor(x_t, x_t, cand[s], ALU.add).then_inc(v3, 1)
                    dve.wait_ge(v3, 4 * t + 4)
                    nc.vector.bn_stats(stats[:, bass.ds(t * 6, 6)], x_t).then_inc(tile_free[s], 1)

                for s in range(SLOTS):
                    dve.sem_inc(tile_free[s])
                    dve.sem_inc(pre_ready[s], 2)
                nc.vector.memset(ones3[:, :], 1.0).then_inc(bias_split, 1)
                nc.vector.memset(bias_sum, 0.0).then_inc(bias_split, 1)
                n = 2
                for k in range(3):
                    dve.wait_ge(bias_split, n)
                    nc.vector.tensor_copy(bias_part, bias[:, :]).then_inc(bias_split, 1)
                    dve.wait_ge(bias_split, n + 1)
                    nc.vector.scalar_tensor_tensor(bias_sum, bias_part, ident[0:3, k:k + 1], bias_sum, ALU.mult, ALU.add).then_inc(bias_split, 1)
                    nc.vector.tensor_tensor(bias[:, :], bias[:, :], bias_part, ALU.subtract).then_inc(bias_split, 1)
                    n += 3
                dve.wait_ge(bias_split, n)
                nc.vector.tensor_copy(bias3, bias_sum).then_inc(bias_split, 1)
                tiles_in_ring(dve, hidden_part, update)
                for s in range(SLOTS):
                    dve.wait_ge(tile_free[s], (NT - 1) // SLOTS + (s == 0) + 1)
                norm_scalars(dve, v3, 4 * NT, var3, std3, scale3)

        end_phase()

        QUAD = 4
        UNITS = NT // QUAD
        assert NT == QUAD * UNITS + 1 and UNITS % 2 == 0
        h2 = [rows[s][:, 0:QUAD * D] for s in range(2)]
        h2T = [rows[s][:, QUAD * D:2 * QUAD * D] for s in range(2)]
        zrow = [rows[2][:, s * QUAD * D:(s + 1) * QUAD * D] for s in range(2)]
        zmask = [hot[s].bitcast(I32) for s in range(2)]
        prod = [[whot[2 * s + k] for k in range(2)] for s in range(2)]
        h2_ready, h2T_raw, h2T_ready, z_raw, z_stored, guard, dotted = (slot_sems(n) for n in (
            "h2_ready", "h2T_raw", "h2T_ready", "z_raw", "z_stored", "guard", "dotted"))
        filler = whot[4]
        b4, ad_raw, ad_made, ad_stored, paused4 = (sem(n) for n in ("b4", "ad_raw", "ad_made", "ad_stored", "paused4"))
        as_parts = WmT[:, 0:(3 * NT + 1) // 2].bitcast(BF16)[:, 0:3 * NT]
        adT_parts = WhhT[0:NT, 0:2 * P].bitcast(BF16)
        as_left, adT_left = WihT[:, 0:NT], WihT[0:NT, P:2 * P]
        past_end = WihT[0:WINDOW, 2 * P:2 * P + 1].bitcast(BF16)

        def units(eng, pipeline):
            pipeline((0, 0, 0, QUAD), None)
            with eng.Fori(0, UNITS // 2 - 1) as i:
                pipeline((2 * i + 1, 1, i, QUAD), (2 * i, 0, i, QUAD))
                pipeline((2 * i + 2, 0, i + 1, QUAD), (2 * i + 1, 1, i, QUAD))
            i = UNITS // 2 - 1
            pipeline((2 * i + 1, 1, i, QUAD), (2 * i, 0, i, QUAD))
            pipeline((UNITS, 0, i + 1, 1), (2 * i + 1, 1, i, QUAD))
            pipeline(None, (UNITS, 0, i + 1, 1))

        def guard_inf(eng, value, mask, filler, done, n, carrier):
            nc.vector.tensor_scalar(mask, value, -F32_MAX, None, ALU.is_lt).then_inc(done, 1)
            eng.wait_ge(done, n + 1)
            nc.vector.scalar_tensor_tensor(mask, value, F32_MAX, mask, ALU.is_gt, ALU.max).then_inc(done, 1)
            eng.wait_ge(done, n + 2)
            eng.sem_inc(carrier)
            return nc.vector.copy_predicated(value, mask, filler)

        with nc.Block() as block:
            @block.scalar
            def _(act):
                def pipeline(a, b):
                    if a:
                        u, s, n, m = a
                        for k in range(m):
                            t = u * QUAD + k
                            one = nc.scalar.activation(h2[s][:, k * D:(k + 1) * D], nodes[:, bass.ds(t * D, D)], ACT.Relu,
                                                       bias=shift[:, bass.ds(t, 1)], scale=rstd[:, bass.ds(t, 1)])
                        one.then_inc(h2_ready[s], 1)
                    if b:
                        u, s, n, m = b
                        act.wait_ge(h2T_raw[s], n + 1)
                        act.wait_ge(z_raw[s], n + 1)
                        nc.scalar.activation(h2T[s][:, 0:m * D], bank[s][:, 0:m * D], ACT.Copy).then_inc(h2T_ready[s], 1)

                units(act, pipeline)

            @block.tensor
            def _(pe):
                for s in range(2):
                    pe.sem_inc(z_raw[s])

                def pipeline(a, b):
                    if a:
                        u, s, n, m = a
                        pe.wait_ge(h2_ready[s], n + 1)
                        for k in range(m):
                            mm = nc.tensor.transpose(bank[s][:, k * D:(k + 1) * D], h2[s][:, k * D:(k + 1) * D], ident[:, :])
                        mm.then_inc(h2T_raw[s], 1)
                    if b:
                        u, s, n, m = b
                        pe.wait_ge(h2T_ready[s], n + 1)
                        pe.wait_ge(guard[s], 4 * n + 1)
                        for k in range(m):
                            mm = nc.tensor.matmul(bank[4 + s][:, k * D:(k + 1) * D], h2T[s][:, k * D:(k + 1) * D], fcw[:, :],
                                                  start=True, stop=True)
                        mm.then_inc(z_raw[s], 1)

                units(pe, pipeline)
                pe.wait_ge(b4, 2)
                nc.tensor.transpose(bank[0][0:NT, 0:P], ad_tab, ident[:, :]).then_inc(ad_raw, 1)

            @block.vector
            def _(dve):
                for s in range(2):
                    dve.sem_inc(guard[s], 4)

                def pipeline(a, b):
                    if b:
                        u, s, n, m = b
                        z = zrow[s][:, 0:m * D]
                        tiles = z.rearrange("p (k d) -> p k d", d=D)
                        dve.wait_ge(z_raw[s], n + 2)
                        dve.wait_ge(z_stored[s], (n + 1) * 16)
                        nc.vector.tensor_tensor(tiles, bank[4 + s][:, 0:m * D].rearrange("p (k d) -> p k d", d=D),
                                                fcb[:, :].unsqueeze(1).broadcast_to([P, m, D]), ALU.add).then_inc(guard[s], 1)
                        dve.wait_ge(guard[s], 4 * n + 5)
                        guard_inf(dve, z, zmask[s][:, 0:m * D], filler[:, 0:m * D], guard[s], 4 * n + 5, paused4).then_inc(guard[s], 1)
                        dve.wait_ge(guard[s], 4 * n + 8)
                        for k in range(2):
                            nc.vector.tensor_tensor(prod[s][k][:, 0:m * D].rearrange("p (k d) -> p k d", d=D), tiles,
                                                    wsd[:, k * D:(k + 1) * D].unsqueeze(1).broadcast_to([P, m, D]),
                                                    ALU.mult).then_inc(dotted[s], 1)
                        for k in range(2):
                            dve.wait_ge(dotted[s], 4 * n + 2)
                            nc.vector.tensor_reduce(terms[:, bass.ds(k * NT + u * QUAD, m)],
                                                    prod[s][k][:, 0:m * D].rearrange("p (k d) -> p k d", d=D),
                                                    AX.X, ALU.add).then_inc(dotted[s], 1)

                nc.vector.memset(filler, BIG).then_inc(b4, 1)
                dve.wait_ge(b4, 1)
                units(dve, pipeline)
                dve.wait_ge(dotted[0], 4 * (UNITS // 2 + 1))
                dve.wait_ge(dotted[1], 4 * (UNITS // 2))
                nc.vector.tensor_scalar(ad_tab, ad_tab, battn[:, 0:1], None, ALU.add).then_inc(b4, 1)
                nc.vector.memset(past_end, 0.0).then_inc(ad_made, 1)
                nc.vector.memset(adT_parts, 0.0).then_inc(ad_made, 1)
                dve.wait_ge(ad_raw, 1)
                nc.vector.tensor_copy(adT[:, :], bank[0][0:NT, 0:P]).then_inc(ad_made, 1)
                as3 = as_parts.rearrange("p (k t) -> p k t", k=3)
                ad4 = adT_parts.rearrange("t (j p c) -> t j c p", j=2, c=2)
                ad3 = {0: ad4[:, 0, 0], 1: ad4[:, 1, 0], 2: ad4[:, 0, 1]}
                dve.wait_ge(ad_made, 3)
                n = 3
                for value, part, left in ((as_tab, {k: as3[:, k] for k in range(3)}, as_left), (adT[:, :], ad3, adT_left)):
                    nc.vector.tensor_copy(part[0], value).then_inc(ad_made, 1)
                    dve.wait_ge(ad_made, n + 1)
                    nc.vector.tensor_tensor(left, value, part[0], ALU.subtract).then_inc(ad_made, 1)
                    dve.wait_ge(ad_made, n + 2)
                    nc.vector.tensor_copy(part[1], left).then_inc(ad_made, 1)
                    dve.wait_ge(ad_made, n + 3)
                    nc.vector.tensor_tensor(part[2], left, part[1], ALU.subtract).then_inc(ad_made, 1)
                    n += 4

            @block.sync
            def _(sp):
                def store(u, s, n, m):
                    sp.wait_ge(guard[s], 4 * n + 8)
                    sp.dma_start(z_tab[bass.ds(u * QUAD * P, m * P), :].rearrange("(k p) d -> p k d", p=P),
                                 zrow[s][:, 0:m * D].rearrange("p (k d) -> p k d", d=D)).then_inc(z_stored[s], 16)

                for s in range(2):
                    sp.sem_inc(z_stored[s], 16)
                with sp.Fori(0, UNITS // 2) as i:
                    for s in range(2):
                        store(2 * i + s, s, i, QUAD)
                store(UNITS, 0, UNITS // 2, 1)
                sp.wait_ge(ad_made, 3)
                sp.dma_start(ad_row.rearrange("a (t p) -> (a t) p", p=P), adT[:, :]).then_inc(ad_stored, 16)
                for k in range(2):
                    sp.dma_start(ad_parts[k, ROWS:ROWS + WINDOW, :], past_end).then_inc(ad_stored, 16)
                sp.wait_ge(ad_made, 11)
                for k in range(2):
                    sp.dma_start(ad_parts[k, 0:ROWS, :].rearrange("(t p) c -> t (p c)", p=P), adT_parts[:, k * 2 * P:(k + 1) * 2 * P]
                                 ).then_inc(ad_stored, 16)
                sp.wait_ge(ad_stored, 80)
                sp.wait_ge(z_stored[0], 16 * (UNITS // 2 + 2))
                sp.wait_ge(z_stored[1], 16 * (UNITS // 2 + 1))

        end_phase()

        half = GROUP // 2
        lo_all = [sums[:, b * GROUP:(b + 1) * GROUP].bitcast(BF16) for b in range(2)]
        rel_all = [sums[:, (2 + b) * GROUP:(3 + b) * GROUP].bitcast(BF16) for b in range(2)]
        term_win = [[sums[:, 4 * GROUP + 2 * b + s:4 * GROUP + 2 * b + s + 1].bitcast(BF16) for s in range(2)] for b in range(2)]
        lo_hot = [side[:, s * half:(s + 1) * half].bitcast(BF16) for s in range(2)]
        rel_hot = [side[:, (2 + s) * half:(3 + s) * half].bitcast(BF16) for s in range(2)]
        pidx_win = col_base[:, 1:2]
        hi_hot = [whot[s][:, 0:TILES * NT] for s in range(2)]
        hi_pick = [hot[s][:, 0:TILES * NT] for s in range(2)]
        row_in, term_in, row_hot, hi_made, picked, chosen, scored = (slot_sems(n) for n in (
            "row_in", "term_in", "row_hot", "hi_made", "picked", "chosen", "scored"))
        staged5, put_by = ([sem(f"{n}{s}") for s in range(3)] for n in ("staged5", "put_by"))
        filled, issued5, back_in = sem("filled"), sem("issued5"), sem("back_in")

        TURNS5, TURNS6 = EARLY5 // 3, (EARLY - EARLY5) // 2

        def early_groups(eng, one):
            with eng.Fori(0, TURNS5) as i:
                for s in range(3):
                    one(i, s, TURNS + (s < 2), 3 * i + s, 3 * i + (3 + s))

        def later_groups(eng, one):
            with eng.Fori(0, TURNS6) as i:
                for s in range(2):
                    one(i + TURNS5, s, TURNS + 1, 2 * i + (EARLY5 + s), 2 * i + (EARLY5 + 2 + s))

        def gather_early(i, s, before, g, after):
            nc.gpsimd.wait_ge(staged5[s], i + 1)
            nc.gpsimd.sem_inc(issued5)
            for d in gather(z_tab, s):
                d.then_inc(landed[s], 16)

        def put_early_by(i, s, before, g, after):
            nc.scalar.wait_ge(landed[s], (i + (before + 1)) * (16 * TILES))
            nc.scalar.dma_start(early[bass.ds(g * P, P), :], rows[s][:, :]).then_inc(put_by[s], 16)
            nc.scalar.wait_ge(put_by[s], (i + 1) * 16)
            nc.scalar.copy(idx[s][:, :], columns(srcT, after)).then_inc(staged5[s], 1)

        with nc.Block() as block:
            @block.sync
            def _(sp):
                def load_rows(i, b):
                    for to, table in ((lo_all[b], lo_row), (rel_all[b], rel_row)):
                        sp.dma_start(to, table[:, bass.ds(i * 2 * GROUP, 2 * GROUP)].broadcast_to([P, 2 * GROUP])
                                     ).then_inc(row_in[b], 16)

                def load_terms(i, b):
                    sp.reg_load(regs, base_i[0:1, bass.ds(2 * i, 2)])
                    for r, to in zip(regs, term_win[b]):
                        at = sp.snap(r, min_val=0, max_val=N - 1)
                        sp.dma_start(to, ad_parts[:, bass.ds(at, WINDOW), :]).then_inc(term_in[b], 16)

                regs = [sp.alloc_register(f"term_base{s}") for s in range(2)]

                sp.dma_start(dstC[:, :], dst_tab).then_inc(back_in, 16)
                sp.dma_start(sigT[:, :], sig_tab).then_inc(back_in, 16)
                for b in range(2):
                    load_rows(b, b)
                    load_terms(b, b)

                def pair(i, b, m):
                    sp.wait_ge(row_hot[b], 4 * m + 4)
                    load_rows(i + 2, b)
                    sp.wait_ge(picked[1], i + 1)
                    load_terms(i + 2, b)

                with sp.Fori(0, (PAIRS - 1) // 2) as m:
                    for b in range(2):
                        pair(2 * m + b, b, m)
                for s in range(2):
                    sp.wait_ge(row_in[s], 32 * ((PAIRS - 1) // 2 + 1))
                    sp.wait_ge(term_in[s], 32 * ((PAIRS - 1) // 2 + 1))
                sp.wait_ge(back_in, 32)

            @block.gpsimd
            def _(pool):
                early_groups(pool, gather_early)

            @block.scalar
            def _(act):
                for s in range(3):
                    nc.scalar.copy(idx[s][:, :], columns(srcT, s)).then_inc(staged5[s], 1)
                early_groups(act, put_early_by)

            @block.tensor
            def _(pe):
                def group(i, b, m, s):
                    pe.wait_ge(row_hot[b], 4 * m + 2 * s + 2)
                    pe.wait_ge(term_in[b], (m + 1) * 32)
                    pe.wait_ge(chosen[s], i + 1)
                    for j in range(TILES):
                        to, e = bank[s][:, j * NT:(j + 1) * NT], slice(j * P, (j + 1) * P)
                        for k in range(3):
                            nc.tensor.matmul(to, lo_hot[s][:, e], as_parts[:, k * NT:(k + 1) * NT], start=k == 0, stop=False)
                        for k, n in enumerate((2 * WINDOW, WINDOW)):
                            mm = nc.tensor.matmul(to, rel_hot[s][0:n, e], term_win[b][s][0:n, k:k + 1].broadcast_to([n, NT]),
                                                  start=False, stop=k == 1)
                    mm.then_inc(picked[s], 1)

                with pe.Fori(0, (PAIRS - 1) // 2) as m:
                    for b in range(2):
                        for s in range(2):
                            group(2 * m + b, b, m, s)
                for s in range(2):
                    group(PAIRS - 1, 0, (PAIRS - 1) // 2, s)

            @block.vector
            def _(dve):
                def make(i, b, m, s):
                    dve.wait_ge(row_in[b], (m + 1) * 32)
                    part = slice(s * GROUP, (s + 1) * GROUP)
                    nc.vector.tensor_scalar(lo_hot[s], lo_all[b][:, part], pidx[:, 0:1], None, ALU.is_equal).then_inc(row_hot[b], 1)
                    nc.vector.tensor_scalar(rel_hot[s], rel_all[b][:, part], pidx_win[:, 0:1], None, ALU.is_equal).then_inc(row_hot[b], 1)
                    onehot(hi_hot[s], columns(hiT, 2 * i + s)).then_inc(hi_made[s], 1)

                def choose(i, s):
                    dve.wait_ge(picked[s], i + 1)
                    dve.wait_ge(hi_made[s], i + 1)
                    nc.vector.tensor_tensor(hi_pick[s], bank[s][:, 0:TILES * NT], hi_hot[s], ALU.mult).then_inc(chosen[s], 1)
                    dve.wait_ge(chosen[s], i + 2)

                def sum_up(i, s):
                    nc.vector.tensor_reduce(columns(logits, 2 * i + s), hi_pick[s].rearrange("p (j k) -> p j k", j=TILES),
                                            AX.X, ALU.add).then_inc(scored[s], 1)

                nc.vector.tensor_scalar(lo_i, srcT[:, :].bitcast(I32), 7, None, ALU.logical_shift_right).then_inc(filled, 1)
                dve.wait_ge(filled, 1)
                nc.vector.tensor_copy(hiT[:, :], lo_i).then_inc(filled, 1)
                dve.wait_ge(filled, 2)
                nc.vector.memset(logits[:, :], 0.0).then_inc(filled, 1)
                nc.vector.tensor_scalar(col_base[:, 0:1].bitcast(I32), pidx_i[:, :], WINDOW - 1, None, ALU.bitwise_and).then_inc(filled, 1)
                dve.wait_ge(filled, 4)
                nc.vector.tensor_copy(pidx_win, col_base[:, 0:1].bitcast(I32)).then_inc(filled, 1)
                for s in range(2):
                    nc.vector.memset(hi_hot[s], 0.0).then_inc(chosen[s], 1)
                    dve.wait_ge(chosen[s], 1)
                dve.wait_ge(filled, 5)
                for s in range(2):
                    make(0, 0, 0, s)
                with dve.Fori(0, (PAIRS - 1) // 2) as m:
                    for b in range(2):
                        for s in range(2):
                            choose(2 * m + b, s)
                            make(2 * m + b + 1, 1 - b, m + b, s)
                            sum_up(2 * m + b, s)
                for s in range(2):
                    choose(PAIRS - 1, s)
                    sum_up(PAIRS - 1, s)
                for s in range(2):
                    dve.wait_ge(scored[s], PAIRS)
                dve.wait_ge(row_in[1], 32 * ((PAIRS - 1) // 2 + 1))

        win_in, win_used, far5, termed = (sem(n) for n in ("win_in", "win_used", "far5", "termed"))
        term_row = hot[1][:, 0:WINDOW]
        far_term = hot[1][:, WINDOW:WINDOW + TILES]
        with nc.Block() as block:
            @block.sync
            def _(sp):
                def step(g, w, q):
                    sp.wait_ge(win_used, q + 1)
                    sp.dma_start(term_row, ad_row[:, bass.ds(w * WINDOW, WINDOW)].broadcast_to([P, WINDOW])
                                 ).then_inc(win_in, 16)

                sp.sem_inc(win_used)
                far_steps(sp, step)

            @block.vector
            def _(dve):
                def step(g, w, q):
                    n = 3 * q
                    ids = far_destinations(dve, g, w, q, far5)
                    onehot(hot[0], ids, win_ids).then_inc(termed, 1)
                    dve.wait_ge(win_in, (q + 1) * 16)
                    dve.wait_ge(termed, n + 1)
                    nc.vector.tensor_tensor(whot[0].rearrange("p (j w) -> p j w", j=TILES), hot[0].rearrange("p (j w) -> p j w", j=TILES),
                                            term_row.unsqueeze(1).broadcast_to([P, TILES, WINDOW]), ALU.mult).then_inc(win_used, 1)
                    dve.wait_ge(win_used, q + 2)
                    nc.vector.tensor_reduce(far_term, whot[0].rearrange("p (j w) -> p j w", j=TILES), AX.X, ALU.add).then_inc(termed, 1)
                    dve.wait_ge(termed, n + 2)
                    at = columns(logits, g)
                    nc.vector.tensor_tensor(at, at, far_term, ALU.add).then_inc(termed, 1)
                    dve.wait_ge(termed, n + 3)

                far_steps(dve, step)

        score, gate, back = scanC
        fwd = edgeC[0]
        both = edgeC[1]
        edge_cols = st[:, 0:8]
        line = sums[0:1, 0:12 * P]
        to_chunk, v6, a6, to_line, to_col, to_tile, exp6, guard6, paused6 = (sem(n) for n in (
            "to_chunk", "v6", "a6", "to_line", "to_col", "to_tile", "exp6", "guard6", "paused6"))
        with nc.Block() as block:
            @block.gpsimd
            def _(pool):
                later_groups(pool, gather_early)

            @block.scalar
            def _(act):
                later_groups(act, put_early_by)
                act.wait_ge(a6, 3)
                nc.scalar.activation(both, both, ACT.Exp).then_inc(exp6, 1)

            @block.tensor
            def _(pe):
                scores = logits[:, 0:ECOLS].rearrange("j (p b) -> j b p", b=BLOCKS)
                for b in range(BLOCKS):
                    mm = nc.tensor.transpose(bank[b // 4][:, (b % 4) * P:(b % 4 + 1) * P], scores[:, b, :], ident[:, :])
                    if b % 4 == 3 or b == BLOCKS - 1:
                        mm.then_inc(to_chunk, 1)
                pe.wait_ge(a6, 1)
                for k in range(4):
                    mm = nc.tensor.transpose(bank[5][0:1, k * P:(k + 1) * P], edge_cols[:, k:k + 1], ident[:, :])
                mm.then_inc(to_line, 1)
                pe.wait_ge(a6, 2)
                for k in range(2):
                    mm = nc.tensor.transpose(bank[6][:, k:k + 1], line[0:1, (8 + k) * P:(9 + k) * P], ident[0:1, 0:1])
                mm.then_inc(to_col, 1)
                pe.wait_ge(exp6, 1)
                for b in range(BLOCKS):
                    mm = nc.tensor.transpose(bank[b // 4][:, (b % 4) * P:(b % 4 + 1) * P], both[:, b * P:(b + 1) * P], ident[:, :])
                    if b % 4 == 3 or b == BLOCKS - 1:
                        mm.then_inc(to_tile, 1)

            @block.vector
            def _(dve):
                n = [0]

                def step(ins):
                    n[0] += 1
                    ins.then_inc(v6, 1)
                    dve.wait_ge(v6, n[0])

                def gates_from(same):
                    step(nc.vector.tensor_scalar(same, same, 2.0, -1.0, ALU.mult, ALU.add))
                    step(nc.vector.tensor_scalar(same, same, F32_MAX, None, ALU.mult))

                def scan(to, by, data, start, backward):
                    r = slice(None, None, -1) if backward else slice(None)
                    step(nc.vector.tensor_tensor_scan(to[:, r], by[:, r], data[:, r], start, ALU.min, ALU.max))

                for k in range(PER):
                    m = min(4, BLOCKS - 4 * k) * P
                    dve.wait_ge(to_chunk, k + 1)
                    step(nc.vector.tensor_copy(score[:, 4 * k * P:4 * k * P + m], bank[k][:, 0:m]))
                step(nc.vector.memset(edgeC[2], BIG))
                step(guard_inf(dve, score, edgeC[0].bitcast(I32), edgeC[2], guard6, 0, paused6))
                step(nc.vector.scalar_tensor_tensor(score, score, 0.01, score, ALU.mult, ALU.max))
                step(nc.vector.memset(gate, 1.0))
                step(nc.vector.tensor_tensor(gate[:, 1:CHUNK], dstC[:, 1:CHUNK], dstC[:, 0:CHUNK - 1], ALU.is_equal))
                gates_from(gate)
                step(nc.vector.memset(back, F32_MAX))
                step(nc.vector.tensor_copy(back[:, 0:CHUNK - 1], gate[:, 1:CHUNK]))
                scan(fwd, gate, score, -F32_MAX, False)
                scan(both, back, score, -F32_MAX, True)
                step(nc.vector.tensor_copy(edge_cols[:, 0:1], dstC[:, 0:1]))
                step(nc.vector.tensor_copy(edge_cols[:, 1:2], dstC[:, CHUNK - 1:CHUNK]))
                step(nc.vector.tensor_copy(edge_cols[:, 2:3], fwd[:, CHUNK - 1:CHUNK]))
                step(nc.vector.tensor_copy(edge_cols[:, 3:4], both[:, 0:1]))
                nc.vector.memset(line, 0.0).then_inc(a6, 1)
                dve.wait_ge(a6, 1)
                dve.wait_ge(to_line, 1)
                first, last, f_state, b_state, conn, through, through_b, fs, f_carry, b_carry, tmp, _ = (
                    line[:, k * P:(k + 1) * P] for k in range(12))
                step(nc.vector.tensor_copy(line[:, 0:4 * P], bank[5][0:1, 0:4 * P]))
                step(nc.vector.tensor_tensor(conn[:, 1:P], first[:, 1:P], last[:, 0:P - 1], ALU.is_equal))
                step(nc.vector.tensor_tensor(tmp, first, last, ALU.is_equal))
                step(nc.vector.tensor_tensor(through, tmp, conn, ALU.mult))
                step(nc.vector.tensor_tensor(through_b[:, 0:P - 1], tmp[:, 0:P - 1], conn[:, 1:P], ALU.mult))
                gates_from(through)
                gates_from(through_b)
                gates_from(conn)
                scan(fs, through, f_state, -F32_MAX, False)
                step(nc.vector.memset(f_carry, -F32_MAX))
                step(nc.vector.tensor_tensor(f_carry[:, 1:P], fs[:, 0:P - 1], conn[:, 1:P], ALU.min))
                scan(tmp, through_b, b_state, -F32_MAX, True)
                step(nc.vector.memset(b_carry, -F32_MAX))
                step(nc.vector.tensor_tensor(b_carry[:, 0:P - 1], tmp[:, 1:P], conn[:, 1:P], ALU.min))
                nc.vector.memset(line[:, 11 * P:12 * P], 0.0).then_inc(a6, 1)
                dve.wait_ge(to_col, 1)
                step(nc.vector.tensor_copy(edge_cols[:, 4:6], bank[6][:, 0:2]))
                scan(fwd, gate, score, edge_cols[:, 4:5], False)
                scan(both, back, score, edge_cols[:, 5:6], True)
                step(nc.vector.tensor_tensor(both, both, fwd, ALU.max))
                nc.vector.tensor_tensor(both, score, both, ALU.subtract).then_inc(a6, 1)
                for k in range(PER):
                    m = min(4, BLOCKS - 4 * k)
                    dve.wait_ge(to_tile, k + 1)
                    view = pairs[:, 0, :].rearrange("j (p b) -> j b p", b=BLOCKS)[:, 4 * k:4 * k + m, :]
                    step(nc.vector.tensor_copy(view, bank[k][:, 0:m * P].rearrange("j (b p) -> j b p", b=m)))
                step(nc.vector.tensor_copy(pairs[:, 1, :], sigT[:, :]))
                step(nc.vector.tensor_tensor(weightT, pairs[:, 0, :], sigT[:, :], ALU.mult))

        end_phase()

        ORDER = (0, 2, 1)
        ADDED0 = 2 * len(ORDER)

        def group_of(s, i):
            return EARLY + 2 * i + s if s < 2 else i

        staged7, summed7, pair7, plain7, weigh7, loaded7 = ([sem(f"{n}{s}") for s in range(3)] for n in (
            "staged7", "summed7", "pair7", "plain7", "weigh7", "loaded7"))
        added7, turn_made, issued7 = (sem(n) for n in ("added7", "turn_made", "issued7"))
        pair = [WihT[:, s * 2 * TILES:(s + 1) * 2 * TILES] for s in range(3)]

        def copy_pair(g, s):
            nc.scalar.activation(pair[s], logits[:, bass.ds(g * 2 * TILES, 2 * TILES)], ACT.Copy).then_inc(pair7[s], 1)

        def stage(g, s):
            nc.vector.tensor_copy(idx[s][:, :], columns(srcT, g)).then_inc(staged7[s], 1)

        def build(g, s, n, rel=None, ids=iota):
            onehot(hot[s], columns(relT, g) if rel is None else rel, ids).then_inc(plain7[s], 1)
            nc.vector.wait_ge(plain7[s], n + 1)
            h, w = (t.rearrange("p (j w) -> p j w", j=TILES) for t in (hot[s], whot[s]))
            ew = columns(weightT, g)
            nc.vector.tensor_tensor(w, h, ew.unsqueeze(2).broadcast_to([P, TILES, WINDOW]), ALU.mult).then_inc(weigh7[s], 1)

        with nc.Block() as block:
            @block.sync
            def _(sp):
                def load(i):
                    sp.dma_start(rows[2][:, :], early[bass.ds(group_of(2, i) * P, P), :]).then_inc(loaded7[2], 16)

                load(0)
                with sp.Fori(0, TURNS7) as i:
                    sp.wait_ge(summed7[2], i + 1)
                    load(i + 1)

            @block.gpsimd
            def _(pool):
                with pool.Fori(0, TURNS7) as i:
                    for s in range(2):
                        pool.wait_ge(staged7[s], i + 1)
                        pool.sem_inc(issued7)
                        for d in gather(z_tab, s):
                            d.then_inc(landed[s], 16)

            @block.tensor
            def _(pe):
                def unit(k, s, i):
                    pe.wait_ge(weigh7[s], i + 1)
                    pe.wait_ge(pair7[s], i + 1)
                    pe.wait_ge(added7, 2 * (3 * i + k) + (ADDED0 - 4))
                    if s < 2:
                        pe.wait_ge(landed[s], (i + (TURNS + 1 + TURNS5 + TURNS6 + 1)) * (16 * TILES))
                    else:
                        pe.wait_ge(loaded7[s], (i + 1) * 16)
                    sum_tiles(s, whot[s], pair[s], 2, hot[s]).then_inc(summed7[s], 1)

                with pe.Fori(0, TURNS7) as i:
                    for k, s in enumerate(ORDER):
                        unit(k, s, i)
                unit(0, 2, TURNS7)

            @block.scalar
            def _(act):
                for s in ORDER:
                    copy_pair(group_of(s, 0), s)
                with act.Fori(0, TURNS7) as i:
                    for s in ORDER:
                        act.wait_ge(summed7[s], i + 1)
                        copy_pair(group_of(s, i + 1), s)

            @block.vector
            def _(dve):
                turns3 = base_turn[:, 0:3 * (TURNS7 + 1)].rearrange("p (i u) -> p u i", u=3)
                for k, s in enumerate(ORDER):
                    g0, step = (EARLY + s, 2) if s < 2 else (0, 1)
                    nc.vector.tensor_copy(turns3[:, k, :], base_i[:, g0:g0 + step * TURNS7 + 1:step]).then_inc(turn_made, 1)
                for s in range(2):
                    stage(group_of(s, 0), s)
                for s in ORDER:
                    build(group_of(s, 0), s, 0)
                nc.vector.memset(sums[:, :], 0.0).then_inc(added7, ADDED0 // 2)
                nc.vector.memset(side[:, :], 0.0).then_inc(added7, ADDED0 // 2)
                dve.wait_ge(turn_made, 3)
                regs = [dve.alloc_register(f"base{k}") for k in range(3)]

                def finish(k, s, i, at):
                    dve.wait_ge(added7, 2 * (3 * i + k) + ADDED0)
                    for a in add_window(s, 2, at):
                        a.then_inc(added7, 1)

                with dve.Fori(0, TURNS7) as i:
                    at = bases(dve, regs, i)
                    for k, s in enumerate(ORDER):
                        dve.wait_ge(summed7[s], i + 1)
                        if s < 2:
                            stage(group_of(s, i + 1), s)
                        finish(k, s, i, at[k])
                        build(group_of(s, i + 1), s, i + 1)
                at = bases(dve, regs, TURNS7)
                dve.wait_ge(summed7[2], TURNS7 + 1)
                finish(0, 2, TURNS7, at[1])

        far7 = sem("far7")
        with nc.Block() as block:
            @block.gpsimd
            def _(pool):
                def step(g, w, q):
                    pool.wait_ge(staged7[0], q + (TURNS7 + 2))
                    pool.sem_inc(issued7)
                    for d in gather(z_tab, 0):
                        d.then_inc(far_landed7, 16)

                far_steps(pool, step)

            @block.tensor
            def _(pe):
                def step(g, w, q):
                    pe.wait_ge(weigh7[0], q + (TURNS7 + 2))
                    pe.wait_ge(pair7[0], q + (TURNS7 + 2))
                    pe.wait_ge(far_landed7, (q + 1) * (16 * TILES))
                    sum_tiles(0, whot[0], pair[0], 2, hot[0]).then_inc(summed7[0], 1)

                far_steps(pe, step)

            @block.scalar
            def _(act):
                def step(g, w, q):
                    act.wait_ge(summed7[0], q + TURNS7)
                    copy_pair(g, 0)

                far_steps(act, step)

            @block.vector
            def _(dve):
                def step(g, w, q):
                    stage(g, 0)
                    ids = far_destinations(dve, g, w, q, far7)
                    build(g, 0, q + (TURNS7 + 1), ids, win_ids)
                    dve.wait_ge(summed7[0], q + (TURNS7 + 1))
                    dve.wait_ge(added7, 2 * q + ADDED0 + 2 * GROUPS)
                    for a in add_window(0, 2, w * WINDOW):
                        a.then_inc(added7, 1)

                far_steps(dve, step)

        end_phase()

        turned8, inv_ready, inv_turned, inv_in, spread8, paused8 = (sem(n) for n in (
            "turned8", "inv_ready", "inv_turned", "inv_in", "spread8", "paused8"))
        v8, scaled, var8, std8 = sem("v8"), sem("scaled"), sem("var8"), sem("std8")
        bns = WhhT[:, 0:6 * (NCH + 1)]
        mv = sb("mv", 2)
        col = sb("col", 6)
        maskc = rows[1][:, 0:CH].bitcast(I32)
        bigc = whot[0]
        inverse = [st[:, k * NT:(k + 1) * NT] for k in range(2)]
        sums2 = bank[7][:, 0:2 * NT].rearrange("p (t k) -> p k t", k=2)
        pos = [hot[s][:, 0:CH] for s in range(2)]
        neg = [hot[2 + s][:, 0:CH] for s in range(2)]
        ex = [whot[s][:, 0:CH] for s in range(2)]
        el = [rows[0][:, s * CH:(s + 1) * CH] for s in range(2)]
        res = [rows[1][:, s * CH:(s + 1) * CH] for s in range(2)]
        neg_ready, exp_ready, elu_ready, turned, res_ready, out_done = (slot_sems(n) for n in (
            "neg_ready", "exp_ready", "elu_ready", "turned", "res_ready", "out_done"))

        with nc.Block() as block:
            @block.tensor
            def _(pe):
                for t in range(NT):
                    mm = nc.tensor.transpose(bank[7][:, 2 * t:2 * t + 2], side[0:2, t * P:(t + 1) * P], ident[0:2, 0:2])
                mm.then_inc(turned8, 1)
                pe.wait_ge(inv_ready, 1)
                nc.tensor.transpose(bank[6][0:NT, 0:P], inverse[1], ident[:, :]).then_inc(inv_turned, 1)
                pe.wait_ge(inv_in, 1)
                for c in range(NCH + 1):
                    m = CH if c < NCH else CTAIL
                    if c >= 4:
                        pe.wait_ge(v8, 2 * (c - 4) + 5)
                    for k in range(-(-m // P)):
                        mm = nc.tensor.matmul(bank[c % 4][:, k * P:(k + 1) * P],
                                              ident[0:NT, 4 * c + k:4 * c + k + 1].broadcast_to([NT, P]),
                                              adT[:, :], start=True, stop=True)
                    mm.then_inc(spread8, 1)

            @block.vector
            def _(dve):
                nc.vector.memset(bigc, BIG).then_inc(v8, 1)
                dve.wait_ge(turned8, 1)
                nc.vector.tensor_scalar(inverse[0], sums2[:, 0, :], 0.5, None, ALU.max).then_inc(v8, 1)
                dve.wait_ge(v8, 2)
                nc.vector.scalar_tensor_tensor(inverse[1], sums2[:, 1, :], BETA_EPS, inverse[0], ALU.add, ALU.mult).then_inc(v8, 1)
                dve.wait_ge(v8, 3)
                nc.vector.reciprocal(inverse[1], inverse[1]).then_inc(inv_ready, 1)
                dve.wait_ge(inv_turned, 1)
                nc.vector.tensor_copy(adT[:, :], bank[6][0:NT, 0:P]).then_inc(inv_in, 1)
                n = 3
                for c in range(NCH + 1):
                    m = CH if c < NCH else CTAIL
                    part = sums[:, c * CH:c * CH + m]
                    dve.wait_ge(spread8, c + 1)
                    nc.vector.tensor_tensor(part, part, bank[c % 4][:, 0:m], ALU.mult).then_inc(v8, 1)
                    dve.wait_ge(v8, n + 1)
                    guard_inf(dve, part, maskc[:, 0:m], bigc[:, 0:m], scaled, 3 * c, paused8).then_inc(scaled, 1)
                    dve.wait_ge(scaled, 3 * c + 3)
                    nc.vector.bn_stats(bns[:, 6 * c:6 * c + 6], part).then_inc(v8, 1)
                    n += 2
                dve.wait_ge(v8, n)
                nc.vector.bn_aggr(mv[:, :], bns).then_inc(var8, 1)
                dve.wait_ge(std8, 1)
                nc.vector.reciprocal(col[:, 1:2], col[:, 0:1]).then_inc(v8, 1)
                dve.wait_ge(v8, n + 1)
                nc.vector.tensor_tensor(col[:, 2:3], col[:, 1:2], gamma[:, :], ALU.mult).then_inc(v8, 1)
                dve.wait_ge(v8, n + 2)
                nc.vector.tensor_tensor(col[:, 4:5], mv[:, 0:1], col[:, 2:3], ALU.mult).then_inc(v8, 1)
                dve.wait_ge(v8, n + 3)
                nc.vector.tensor_tensor(col[:, 3:4], beta[:, :], col[:, 4:5], ALU.subtract).then_inc(v8, 1)
                dve.wait_ge(v8, n + 4)
                nc.vector.tensor_scalar(col[:, 4:6], col[:, 2:4], -1.0, None, ALU.mult).then_inc(v8, 1)
                dve.wait_ge(v8, n + 5)

            @block.scalar
            def _(act):
                act.wait_ge(var8, 1)
                nc.scalar.activation(col[:, 0:1], mv[:, 1:2], ACT.Sqrt, bias=eps[:, 0:1]).then_inc(std8, 1)

        with nc.Block() as block:
            @block.scalar
            def _(act):
                def one(c, s, m, n):
                    act.wait_ge(elu_ready[s], n + 1)
                    part = sums[:, bass.ds(c * CH, m)]
                    nc.scalar.activation(neg[s][:, 0:m], part, ACT.Relu, bias=col[:, 5:6], scale=col[:, 4:5]).then_inc(neg_ready[s], 1)
                    nc.scalar.activation(pos[s][:, 0:m], part, ACT.Relu, bias=col[:, 3:4], scale=col[:, 2:3]).then_inc(exp_ready[s], 1)
                    act.wait_ge(neg_ready[s], n + 1)
                    nc.scalar.activation(ex[s][:, 0:m], neg[s][:, 0:m], ACT.Exp, scale=-1.0).then_inc(exp_ready[s], 1)

                with act.Fori(0, NCH // 2) as i:
                    for s in range(2):
                        one(2 * i + s, s, CH, i)
                one(NCH, 0, CTAIL, NCH // 2)

            @block.vector
            def _(dve):
                def join(s, m, n):
                    dve.wait_ge(exp_ready[s], 2 * n + 2)
                    nc.vector.scalar_tensor_tensor(el[s][:, 0:m], ex[s][:, 0:m], -1.0, pos[s][:, 0:m], ALU.add,
                                                   ALU.add).then_inc(elu_ready[s], 1)

                def residual(c, s, m, n):
                    dve.wait_ge(turned[s], n + 1)
                    dve.wait_ge(out_done[s], (n + 1) * 16)
                    if m == CH:
                        nc.vector.tensor_tensor(res[s], bank[s][:, 0:CH], nodes[:, bass.ds(c * CH, CH)], ALU.add).then_inc(res_ready[s], 1)
                    else:
                        assert m <= P
                        nc.vector.tensor_tensor(res[s][0:m, 0:D], bank[s][0:m, 0:D], nodes[0:m, c * CH:c * CH + D],
                                                ALU.add).then_inc(res_ready[s], 1)

                for s in range(2):
                    dve.sem_inc(elu_ready[s])
                    dve.sem_inc(res_ready[s])
                join(0, CH, 0)
                with dve.Fori(0, NCH // 2 - 1) as i:
                    join(1, CH, i)
                    residual(2 * i, 0, CH, i)
                    join(0, CH, i + 1)
                    residual(2 * i + 1, 1, CH, i)
                LAST = NCH // 2 - 1
                join(1, CH, LAST)
                residual(2 * LAST, 0, CH, LAST)
                join(0, CTAIL, LAST + 1)
                residual(2 * LAST + 1, 1, CH, LAST)
                residual(NCH, 0, CTAIL, LAST + 1)

            @block.tensor
            def _(pe):
                def one(s, m, n):
                    pe.wait_ge(elu_ready[s], n + 2)
                    pe.wait_ge(res_ready[s], n + 1)
                    for k in range(-(-m // P)):
                        w = min(P, m - k * P)
                        mm = nc.tensor.transpose(bank[s][0:w, k * P:(k + 1) * P], el[s][:, k * P:k * P + w], ident[:, :])
                    mm.then_inc(turned[s], 1)

                with pe.Fori(0, NCH // 2) as i:
                    for s in range(2):
                        one(s, CH, i)
                one(0, CTAIL, NCH // 2)

            @block.sync
            def _(sp):
                for s in range(2):
                    sp.sem_inc(out_done[s], 16)
                with sp.Fori(0, NCH // 2) as i:
                    for s in range(2):
                        sp.wait_ge(res_ready[s], i + 2)
                        sp.dma_start(out[bass.ds((2 * i + s) * CH, CH), :].rearrange("(k p) d -> p k d", p=P),
                                     res[s].rearrange("p (k d) -> p k d", d=D)).then_inc(out_done[s], 16)
                sp.wait_ge(res_ready[0], NCH // 2 + 2)
                sp.dma_start(out[NCH * CH:N, :], res[0][0:CTAIL, 0:D]).then_inc(out_done[0], 16)
                sp.wait_ge(out_done[0], 16 * (NCH // 2 + 2))
                sp.wait_ge(out_done[1], 16 * (NCH // 2 + 1))

        phase.close()


_INS = ["x", "src", "dst", "edge_type_9", "edge_weight", "L0_gnn_W_msg", "L0_gnn_b_msg", "L0_gnn_edge_embed",
        "L0_gnn_W_ih", "L0_gnn_W_hh", "L0_gnn_b_ih", "L0_gnn_b_hh", "L1_gnn_fc_w", "L1_gnn_fc_b",
        "L1_gnn_attn_w", "L1_gnn_attn_b", "L1_gnn_bn_gamma", "L1_gnn_bn_beta"]


def kernel(**inputs):
    import numpy as _np
    import concourse.bacc as _bacc
    from concourse import mybir as _mybir
    from concourse.bass_utils import run_bass_kernel_spmd as _run

    nc = _bacc.Bacc("TRN2", target_bir_lowering=False, num_devices=1)
    arrays, args = {}, []
    for name in _INS:
        a = _np.ascontiguousarray(inputs[name])
        arrays[f"in_{name}"] = a
        args.append(nc.dram_tensor(f"in_{name}", a.shape, _mybir.dt.from_np(a.dtype), kind="ExternalInput").ap())
    shape = inputs["x"].shape
    args.append(nc.dram_tensor("out_dram", shape, _mybir.dt.float32, kind="ExternalOutput").ap())
    gnn(nc, *args)
    r = _run(nc, [arrays], core_ids=[0])
    return r.results[0]["out_dram"]
```
